# Optimizing a Trainium2 kernel written in Bass

```python
import numpy as np
import jax
import jax.numpy as jnp

def _softmax(x, axis=-1):
    return jax.nn.softmax(x, axis=axis)

def _gelu(x):
    return jax.nn.gelu(x, approximate=True)

def _silu(x):
    return jax.nn.silu(x)

def _sigmoid(x):
    return jax.nn.sigmoid(x)

def _layernorm(x, axis=-1, eps=1e-05):
    m = jnp.mean(x, axis=axis, keepdims=True)
    v = jnp.var(x, axis=axis, keepdims=True)
    return (x - m) / jnp.sqrt(v + eps)

def _scatter_add(tgt, idx, src, axis=0):
    return tgt.at[idx].add(src)

def _segment_sum(src, seg, n):
    return jax.ops.segment_sum(src, seg, n)
kernel_name = 'mk_seq_postln_d2_jaxref_r8_f1b0a7'

def setup_inputs(seed: int=0):
    np.random.seed(seed)
    _w = jnp.asarray

    def _L0_attn_setup():
        import jax, jax.numpy as jnp
        import numpy as np
        B, T, HM = (2, 256, 128)
        HEADS = 16
        DK = HM // 2 // HEADS
        DV = HM // HEADS
        LOW_RANK = 16
        GATE_NORM = 16.0
        EPS = 1e-05

        def _ln(x, w, b):
            m = x.mean(-1, keepdims=True)
            v = ((x - m) ** 2).mean(-1, keepdims=True)
            return (x - m) * jax.lax.rsqrt(v + EPS) * w + b

        def _rms(x, w):
            return x * jax.lax.rsqrt((x * x).mean(-1, keepdims=True) + EPS) * w

        def _gla(q, k, v, gk):

            def step(S, inp):
                qt, kt, vt, gt = inp
                S = jnp.exp(gt)[..., None] * S + kt[..., None] * vt[..., None, :]
                return (S, jnp.einsum('bhk,bhkv->bhv', qt, S))
            xs = tuple((jnp.moveaxis(a, 1, 0) for a in (q, k, v, gk)))
            S0 = jnp.zeros((q.shape[0], q.shape[2], q.shape[3], v.shape[3]), q.dtype)
            _, o = jax.lax.scan(step, S0, xs)
            return jnp.moveaxis(o, 0, 1)
        key = jax.random.key(seed)
        ks = jax.random.split(key, 12)

        def p(k, shape, s=0.02):
            return jax.random.normal(k, shape, jnp.float32) * s
        return dict(x=jax.random.normal(ks[0], (B, T, HM), jnp.float32), ln_w=jnp.ones((HM,), jnp.float32), ln_b=jnp.zeros((HM,), jnp.float32), Wq=p(ks[1], (HM, HEADS * DK)), Wk=p(ks[2], (HM, HEADS * DK)), Wv=p(ks[3], (HM, HEADS * DV)), gk_w1=p(ks[4], (HM, LOW_RANK)), gk_w2=p(ks[5], (LOW_RANK, HEADS * DK)), gk_b2=jnp.zeros((HEADS * DK,), jnp.float32), Wg=p(ks[6], (HM, HEADS * DV)), rms_w=jnp.ones((DV,), jnp.float32), Wo=p(ks[7], (HEADS * DV, HM)), W1=p(ks[8], (HM, 2 * HM)), b1=jnp.zeros((2 * HM,), jnp.float32), W2=p(ks[9], (2 * HM, HM)), b2=jnp.zeros((HM,), jnp.float32))
    _L0_attn_in = _L0_attn_setup()

    def _L0_ffn_setup():
        import jax, jax.numpy as jnp
        import numpy as np
        D, H, E, K, S = (128, 256, 8, 2, 1)
        B, L = (4, 256)
        key = jax.random.key(seed)
        ks = jax.random.split(key, 9)
        std = 0.02
        return {'x': jax.random.normal(ks[0], (B, L, D), dtype=jnp.float32), 'router_w': jax.random.normal(ks[1], (E, D), dtype=jnp.float32) * std, 'experts_bias': jnp.zeros((E,), dtype=jnp.float32), 'w1': jax.random.normal(ks[2], (E, D, H), dtype=jnp.float32) * std, 'w3': jax.random.normal(ks[3], (E, D, H), dtype=jnp.float32) * std, 'w2': jax.random.normal(ks[4], (E, H, D), dtype=jnp.float32) * std, 'sw1': jax.random.normal(ks[5], (S, D, H), dtype=jnp.float32) * std, 'sw3': jax.random.normal(ks[6], (S, D, H), dtype=jnp.float32) * std, 'sw2': jax.random.normal(ks[7], (S, H, D), dtype=jnp.float32) * std}
    _L0_ffn_in = _L0_ffn_setup()

    def _L1_attn_setup():
        import jax, jax.numpy as jnp
        import numpy as np
        DIM = 128
        B, S = (8, 256)
        LN_EPS = 1e-05
        key = jax.random.key(seed)
        k1, k2, k3 = jax.random.split(key, 3)
        x = jax.random.normal(k1, (B, S, DIM), dtype=jnp.float32)
        w_qkv = jax.random.normal(k2, (3 * DIM, DIM), dtype=jnp.float32) * np.sqrt(2.0 / (DIM + 3 * DIM))
        w_fc = jax.random.normal(k3, (DIM, DIM), dtype=jnp.float32) * np.sqrt(2.0 / (DIM + DIM))
        b_fc = jnp.zeros((DIM,), dtype=jnp.float32)
        gamma = jnp.ones((DIM,), dtype=jnp.float32)
        beta = jnp.zeros((DIM,), dtype=jnp.float32)
        return {'x': x, 'w_qkv': w_qkv, 'w_fc': w_fc, 'b_fc': b_fc, 'gamma': gamma, 'beta': beta}
    _L1_attn_in = _L1_attn_setup()

    def _L1_ffn_setup():
        import jax, jax.numpy as jnp
        import numpy as np
        N_EMBD = 128
        N_STATE = 512
        key = jax.random.key(seed)
        k_x, k_w1, k_b1, k_w2, k_b2 = jax.random.split(key, 5)
        x = jax.random.normal(k_x, (4, 256, N_EMBD), dtype=jnp.float32)
        w1 = jax.random.normal(k_w1, (N_EMBD, N_STATE), dtype=jnp.float32) * (1.0 / np.sqrt(N_EMBD))
        b1 = jax.random.normal(k_b1, (N_STATE,), dtype=jnp.float32) * 0.02
        w2 = jax.random.normal(k_w2, (N_STATE, N_EMBD), dtype=jnp.float32) * (1.0 / np.sqrt(N_STATE))
        b2 = jax.random.normal(k_b2, (N_EMBD,), dtype=jnp.float32) * 0.02
        return {'x': x, 'w1': w1, 'b1': b1, 'w2': w2, 'b2': b2}
    _L1_ffn_in = _L1_ffn_setup()
    _d = {'L0_attn_x': _L0_attn_in['x'], 'L0_attn_ln_w': _L0_attn_in['ln_w'], 'L0_attn_ln_b': _L0_attn_in['ln_b'], 'L0_attn_Wq': _L0_attn_in['Wq'], 'L0_attn_Wk': _L0_attn_in['Wk'], 'L0_attn_Wv': _L0_attn_in['Wv'], 'L0_attn_gk_w1': _L0_attn_in['gk_w1'], 'L0_attn_gk_w2': _L0_attn_in['gk_w2'], 'L0_attn_gk_b2': _L0_attn_in['gk_b2'], 'L0_attn_Wg': _L0_attn_in['Wg'], 'L0_attn_rms_w': _L0_attn_in['rms_w'], 'L0_attn_Wo': _L0_attn_in['Wo'], 'L0_attn_W1': _L0_attn_in['W1'], 'L0_attn_b1': _L0_attn_in['b1'], 'L0_attn_W2': _L0_attn_in['W2'], 'L0_attn_b2': _L0_attn_in['b2'], 'L0_ffn_router_w': _L0_ffn_in['router_w'], 'L0_ffn_experts_bias': _L0_ffn_in['experts_bias'], 'L0_ffn_w1': _L0_ffn_in['w1'], 'L0_ffn_w3': _L0_ffn_in['w3'], 'L0_ffn_w2': _L0_ffn_in['w2'], 'L0_ffn_sw1': _L0_ffn_in['sw1'], 'L0_ffn_sw3': _L0_ffn_in['sw3'], 'L0_ffn_sw2': _L0_ffn_in['sw2'], 'L1_attn_w_qkv': _L1_attn_in['w_qkv'], 'L1_attn_w_fc': _L1_attn_in['w_fc'], 'L1_attn_b_fc': _L1_attn_in['b_fc'], 'L1_attn_gamma': _L1_attn_in['gamma'], 'L1_attn_beta': _L1_attn_in['beta'], 'L1_ffn_w1': _L1_ffn_in['w1'], 'L1_ffn_b1': _L1_ffn_in['b1'], 'L1_ffn_w2': _L1_ffn_in['w2'], 'L1_ffn_b2': _L1_ffn_in['b2']}
    _x0 = _d['L0_attn_x']
    _d['L0_attn_x'] = jax.random.normal(jax.random.fold_in(jax.random.key(seed), 1), (8, 512, 128), dtype=_x0.dtype)
    del _x0
    return _d

def reference(L0_attn_x, L0_attn_ln_w, L0_attn_ln_b, L0_attn_Wq, L0_attn_Wk, L0_attn_Wv, L0_attn_gk_w1, L0_attn_gk_w2, L0_attn_gk_b2, L0_attn_Wg, L0_attn_rms_w, L0_attn_Wo, L0_attn_W1, L0_attn_b1, L0_attn_W2, L0_attn_b2, L0_ffn_router_w, L0_ffn_experts_bias, L0_ffn_w1, L0_ffn_w3, L0_ffn_w2, L0_ffn_sw1, L0_ffn_sw3, L0_ffn_sw2, L1_attn_w_qkv, L1_attn_w_fc, L1_attn_b_fc, L1_attn_gamma, L1_attn_beta, L1_ffn_w1, L1_ffn_b1, L1_ffn_w2, L1_ffn_b2):

    def _L0_attn_ref(x, ln_w, ln_b, Wq, Wk, Wv, gk_w1, gk_w2, gk_b2, Wg, rms_w, Wo, W1, b1, W2, b2):
        import jax, jax.numpy as jnp
        import numpy as np
        B, T, HM = (2, 256, 128)
        HEADS = 16
        DK = HM // 2 // HEADS
        DV = HM // HEADS
        LOW_RANK = 16
        GATE_NORM = 16.0
        EPS = 1e-05

        def _ln(x, w, b):
            m = x.mean(-1, keepdims=True)
            v = ((x - m) ** 2).mean(-1, keepdims=True)
            return (x - m) * jax.lax.rsqrt(v + EPS) * w + b

        def _rms(x, w):
            return x * jax.lax.rsqrt((x * x).mean(-1, keepdims=True) + EPS) * w

        def _gla(q, k, v, gk):

            def step(S, inp):
                qt, kt, vt, gt = inp
                S = jnp.exp(gt)[..., None] * S + kt[..., None] * vt[..., None, :]
                return (S, jnp.einsum('bhk,bhkv->bhv', qt, S))
            xs = tuple((jnp.moveaxis(a, 1, 0) for a in (q, k, v, gk)))
            S0 = jnp.zeros((q.shape[0], q.shape[2], q.shape[3], v.shape[3]), q.dtype)
            _, o = jax.lax.scan(step, S0, xs)
            return jnp.moveaxis(o, 0, 1)
        Bb, Tt, _ = x.shape
        h = _ln(x, ln_w, ln_b)
        q = (h @ Wq).reshape(Bb, Tt, HEADS, DK)
        k = (h @ Wk).reshape(Bb, Tt, HEADS, DK)
        v = (h @ Wv).reshape(Bb, Tt, HEADS, DV)
        gk = jax.nn.log_sigmoid(h @ gk_w1 @ gk_w2 + gk_b2) / GATE_NORM
        gk = gk.reshape(Bb, Tt, HEADS, DK)
        o = _gla(q * DK ** (-0.5), k, v, gk)
        g = (h @ Wg).reshape(Bb, Tt, HEADS, DV)
        o = _rms(o, rms_w) * (g * jax.nn.sigmoid(g))
        x = x + o.reshape(Bb, Tt, HEADS * DV) @ Wo
        h2 = _ln(x, ln_w, ln_b)
        return x + jax.nn.gelu(h2 @ W1 + b1, approximate=False) @ W2 + b2

    def _L0_ffn_ref(x, router_w, experts_bias, w1, w3, w2, sw1, sw3, sw2):
        import jax, jax.numpy as jnp
        import numpy as np
        D, H, E, K, S = (128, 256, 8, 2, 1)
        B, L = (4, 256)
        b, l, d = x.shape
        xf = x.reshape(-1, d)
        sg = jnp.einsum('td,sdh->tsh', xf, sw1)
        su = jnp.einsum('td,sdh->tsh', xf, sw3)
        shared_out = jnp.einsum('tsh,shd->td', jax.nn.silu(sg) * su, sw2)
        logits = xf @ router_w.T + experts_bias
        rw, sel = jax.lax.top_k(logits, K)
        rw = jax.nn.softmax(rw.astype(jnp.float32), axis=-1).astype(x.dtype)
        cw = (jax.nn.one_hot(sel, E, dtype=x.dtype) * rw[..., None]).sum(axis=1)
        g = jnp.einsum('td,edh->teh', xf, w1)
        u = jnp.einsum('td,edh->teh', xf, w3)
        eo = jax.nn.silu(g) * u
        moe_out = jnp.einsum('te,teh,ehd->td', cw, eo, w2)
        return (moe_out + shared_out).reshape(b, l, d)

    def _L1_attn_ref(x, w_qkv, w_fc, b_fc, gamma, beta):
        import jax, jax.numpy as jnp
        import numpy as np
        DIM = 128
        B, S = (8, 256)
        LN_EPS = 1e-05
        scaling = DIM ** (-0.5)
        qkv = jnp.einsum('bsd,ed->bse', x, w_qkv)
        q, k, v = jnp.split(qkv, 3, axis=-1)
        att = jax.nn.softmax(jnp.einsum('bqd,bkd->bqk', q, k) * scaling, axis=-1)
        y = jnp.einsum('bqk,bvd->bqd', att, v)
        y = jnp.einsum('bqd,ed->bqe', y, w_fc) + b_fc
        h = x + y
        mu = jnp.mean(h, axis=-1, keepdims=True)
        var = jnp.var(h, axis=-1, keepdims=True)
        return (h - mu) * jax.lax.rsqrt(var + LN_EPS) * gamma + beta

    def _L1_ffn_ref(x, w1, b1, w2, b2):
        import jax, jax.numpy as jnp
        import numpy as np
        N_EMBD = 128
        N_STATE = 512
        h = jax.nn.gelu(jnp.einsum('bse,eh->bsh', x, w1) + b1, approximate=False)
        return jnp.einsum('bsh,he->bse', h, w2) + b2
    x = L0_attn_x
    x = _layernorm(x + _L0_attn_ref(x, L0_attn_ln_w, L0_attn_ln_b, L0_attn_Wq, L0_attn_Wk, L0_attn_Wv, L0_attn_gk_w1, L0_attn_gk_w2, L0_attn_gk_b2, L0_attn_Wg, L0_attn_rms_w, L0_attn_Wo, L0_attn_W1, L0_attn_b1, L0_attn_W2, L0_attn_b2), axis=-1)
    x = _layernorm(x + _L0_ffn_ref(x, L0_ffn_router_w, L0_ffn_experts_bias, L0_ffn_w1, L0_ffn_w3, L0_ffn_w2, L0_ffn_sw1, L0_ffn_sw3, L0_ffn_sw2), axis=-1)
    x = _layernorm(x + _L1_attn_ref(x, L1_attn_w_qkv, L1_attn_w_fc, L1_attn_b_fc, L1_attn_gamma, L1_attn_beta), axis=-1)
    x = _layernorm(x + _L1_ffn_ref(x, L1_ffn_w1, L1_ffn_b1, L1_ffn_w2, L1_ffn_b2), axis=-1)
    return x

_drawn_inputs = setup_inputs


def setup_inputs(seed=0):
    import zlib

    import numpy as np

    out = dict(_drawn_inputs(seed))
    spreads = {'L0_attn_ln_w': (1.0, 0.6),
     'L0_attn_ln_b': (0.0, 0.431),
     'L0_attn_gk_b2': (0.0, 0.8),
     'L0_attn_rms_w': (1.0, 0.6),
     'L0_attn_b1': (0.0, 0.1),
     'L0_attn_b2': (0.0, 0.1),
     'L0_ffn_experts_bias': (0.0, 0.8),
     'L1_attn_b_fc': (0.0, 2.0),
     'L1_attn_gamma': (1.0, 0.2),
     'L1_attn_beta': (0.0, 0.1)}
    factors = {'L0_attn_Wq': 4.317,
     'L0_attn_Wk': 4.228,
     'L0_attn_Wv': 4.457,
     'L0_attn_gk_w1': 8.0,
     'L0_attn_gk_w2': 8.0,
     'L0_attn_Wg': 4.426,
     'L0_attn_Wo': 4.381,
     'L0_ffn_router_w': 8.0,
     'L0_ffn_w1': 8.0,
     'L0_ffn_w3': 8.0,
     'L0_ffn_w2': 8.0,
     'L0_ffn_sw1': 5.827,
     'L0_ffn_sw3': 5.456,
     'L0_ffn_sw2': 5.147,
     'L1_ffn_b1': 5.238,
     'L1_ffn_b2': 3.302}
    for name, (base, spread) in spreads.items():
        noise = np.random.default_rng([zlib.crc32(name.encode()), seed]).standard_normal(out[name].shape)
        drawn = base * np.exp(spread * noise) if base else spread * noise
        out[name] = jnp.asarray(drawn.astype(out[name].dtype))
    for name, factor in factors.items():
        out[name] = (out[name] * factor).astype(out[name].dtype)
    return out
```

```python
from contextlib import ExitStack

import concourse.bass as bass
from concourse import mybir

F32 = mybir.dt.float32
F32R = mybir.dt.float32r
I32 = mybir.dt.int32
U32 = mybir.dt.uint32
ALU = mybir.AluOpType
ACT = mybir.ActivationFunctionType
AX = mybir.AxisListType

P = 128
HEAD = 4
EPS = 1e-5
GATE_NORM = 16.0


def at(n):
    return HEAD + (max(n, 0) if isinstance(n, int) else n)


def build(nc, a, out):
    B, T, D = a["L0_attn_x"].shape
    assert D == P and B % 2 == 0
    TILES = T // P
    HK = a["L0_attn_Wq"].shape[1]
    DV = a["L0_attn_rms_w"].shape[0]
    H = D // DV
    DK = HK // H
    E, _, HID = a["L0_ffn_w1"].shape
    HALVES = HID // P
    UNITS = (E + 1) * HALVES
    MLP0 = a["L0_attn_W1"].shape[1] // P
    MLP1 = a["L1_ffn_w1"].shape[1] // P
    LOWR = a["L0_attn_gk_w1"].shape[1]
    SCALE = float(D) ** -0.5

    with ExitStack() as ctx:
        def sb(name, shape, dt=F32):
            return ctx.enter_context(nc.sbuf_tensor(name, shape, dt))

        starts = {"pe": [], "act": [], "dve": [], "pool": []}

        def sem(name, engine=None):
            s = ctx.enter_context(nc.semaphore(name))
            if engine:
                starts[engine].append(s)
            return s

        apart = ctx.enter_context(nc.semaphore("apart"))

        def wait_apart(eng, s, value):
            eng.wait_ge(s, value)
            eng.sem_inc(apart, 1)

        def open_semaphores(eng, name):
            for s in starts[name]:
                eng.sem_inc(s, HEAD)

        def pipelined(eng, step, lags):
            for s in range(lags):
                step(s, s % 2)
            turns = (B - lags) // 2
            with eng.Fori(0, turns) as i:
                s = 2 * i + lags
                step(s, lags % 2)
                step(s + 1, (lags + 1) % 2)
            for s in range(lags + 2 * turns, B + lags):
                step(s, s % 2)

        def there(b):
            return not isinstance(b, int) or 0 <= b < B

        bank = [ctx.enter_context(nc.psum_tensor(f"bank{i}", [P, 512], F32)) for i in range(8)]

        ident = sb("ident", [P, P])
        ones = sb("ones", [P, P])
        head_mean = sb("head_mean", [P, P])
        eps_row = sb("eps_row", [P, TILES])
        minus_half = sb("minus_half", [P, TILES])
        iota_i = sb("iota_i", [P, E], I32)
        iota_e = sb("iota_e", [P, E])
        spread_k = sb("spread_k", [HK, DK, P], F32R)
        pick_e = sb("pick_e", [E, E, P], F32R)

        ln_w = sb("ln_w", [P, 1])
        ln_b = sb("ln_b", [P, 1])
        rms_col = sb("rms_col", [P, 1])
        gk_b = sb("gk_b", [HK, 1])
        b1_col = sb("b1_col", [P, MLP0])
        b2_col = sb("b2_col", [P, 1])
        ebias = sb("ebias", [P, E])
        f_b1 = sb("f_b1", [P, MLP1])
        f_b2 = sb("f_b2", [P, 1])
        bfc = sb("bfc", [P, P])
        gamma = sb("gamma", [P, P])
        beta = sb("beta", [P, P])

        GK, V, G, K0 = 0, 1, 2, 3
        Q0 = K0 + DK
        UP0 = Q0 + DK
        NB0 = UP0 + MLP0
        w_hi = sb("w_hi", [P, NB0, P], F32R)
        w_lo = sb("w_lo", [P, NB0, P], F32R)
        w_bias = sb("w_bias", [P, NB0])
        wo_scaled = sb("wo_scaled", [P, P])
        wo_hi = sb("wo_hi", [P, P], F32R)
        wo_lo = sb("wo_lo", [P, P], F32R)
        r_raw = sb("r_raw", [E, P])
        r_hi = sb("r_hi", [P, E], F32R)
        r_lo = sb("r_lo", [P, E], F32R)

        qkv_raw = sb("qkv_raw", [P, 3, P])
        fc_raw = sb("fc_raw", [P, P])
        fc_t = sb("fc_t", [P, P])
        qk_hi = sb("qk_hi", [P, P], F32R)
        qk_lo = sb("qk_lo", [P, P], F32R)
        vfc = sb("vfc", [P, P])


        R = sb("R", [P, B, TILES, P])
        gate = sb("gate", [P, B, T])
        rms_o = R[:, :, :, :].rearrange("p b j d -> p b (j d)")
        work = sb("work", [P, 24, T])
        workr = sb("workr", [P, 16, T], F32R)

        def buf(i):
            return work[:, i, :]

        def tok(i):
            return work[:, i, :].rearrange("p (j d) -> p j d", d=P)

        def bufr(i):
            return workr[:, i, :]
        wq_raw, wk_raw, wo_raw = buf(8)[:, 0:HK], buf(8)[:, HK:2 * HK], buf(9)[:, 0:P]
        gkw1, gkw1_t, gkw2 = buf(10)[:, 0:LOWR], work[0:LOWR, 11, 0:P], work[0:LOWR, 11, P:P + HK]
        w_raw = work[:, 12:16, :].rearrange("p n t -> p (n t)")[:, 0:NB0 * P].rearrange("p (n c) -> p n c", c=P)
        w_fold = work[:, 16:20, :].rearrange("p n t -> p (n t)")[:, 0:NB0 * P].rearrange("p (n c) -> p n c", c=P)

        EXPERTS = (E + 1) * HID
        UP1, DN1 = 3 * EXPERTS, 3 * EXPERTS + MLP1 * P
        DN0 = DN1 + MLP1 * P
        assert DN0 + MLP0 * P == 2 * B * T
        w_late_hi = sb("w_late_hi", [P, 2 * B, T], F32R)
        w_late_lo = sb("w_late_lo", [P, 2 * B, T], F32R)
        late_hi_row = w_late_hi[:, :, :].rearrange("p n t -> p (n t)")
        late_lo_row = w_late_lo[:, :, :].rearrange("p n t -> p (n t)")

        def late_raw(start, n):
            assert start // (B * T) == (start + n - 1) // (B * T)
            half = gate[:, :, :].rearrange("p b t -> p (b t)") if start < B * T else rms_o.rearrange("p b t -> p (b t)")
            return half[:, start % (B * T):start % (B * T) + n]

        def late(start, n=P):
            return late_hi_row[:, start:start + n], late_lo_row[:, start:start + n]

        early = sem("early_weights")
        late_raw_in = sem("late_raw_in")
        small_in = sem("small_in")
        const_made = sem("const_made", "pool")
        pool_chain = sem("pool_chain", "pool")
        prep_pe = sem("prep_pe", "pe")
        prep_dve = sem("prep_dve", "dve")
        prep_act = sem("prep_act", "act")
        late_hi = sem("late_hi", "act")
        late_lo = sem("late_lo", "pool")

        EARLY = [
            (ln_w[:, :], a["L0_attn_ln_w"].unsqueeze(1)),
            (ln_b[:, :], a["L0_attn_ln_b"].unsqueeze(1)),
            (gkw1[:, :], a["L0_attn_gk_w1"]),
            (gkw2[:, :], a["L0_attn_gk_w2"]),
            (wq_raw[:, :], a["L0_attn_Wq"]),
            (wk_raw[:, :], a["L0_attn_Wk"]),
            (w_raw[:, V, :], a["L0_attn_Wv"]),
            (w_raw[:, G, :], a["L0_attn_Wg"]),
            (w_raw[:, UP0:NB0, :], a["L0_attn_W1"].rearrange("d (c h) -> d c h", c=MLP0)),
            (gk_b[:, :], a["L0_attn_gk_b2"].unsqueeze(1)),
            (b1_col[:, :], a["L0_attn_b1"].rearrange("(c p) -> p c", p=P)),
            (b2_col[:, :], a["L0_attn_b2"].unsqueeze(1)),
            (rms_col[:, :], a["L0_attn_rms_w"].unsqueeze(1).partition_broadcast(H)),
            (wo_raw[:, :], a["L0_attn_Wo"]),
        ]
        def experts(m, e, n):
            return late_raw(m * EXPERTS + e * HID, n * HID)
        split = B * T // HID - EXPERTS // HID
        LATE = [
            (experts(0, 0, 1), a["L0_ffn_sw1"][0]),
            (experts(0, 1, E).rearrange("d (e h) -> d e h", e=E), a["L0_ffn_w1"].rearrange("e d h -> d e h")),
            (experts(1, 0, 1), a["L0_ffn_sw3"][0]),
            (experts(1, 1, split - 1).rearrange("d (e h) -> d e h", h=HID),
             a["L0_ffn_w3"][0:split - 1].rearrange("e d h -> d e h")),
            (experts(1, split, E + 1 - split).rearrange("d (e h) -> d e h", h=HID),
             a["L0_ffn_w3"][split - 1:E].rearrange("e d h -> d e h")),
            (experts(2, 0, 1).rearrange("h (c d) -> h c d", c=HALVES),
             a["L0_ffn_sw2"][0].rearrange("(c h) d -> h c d", c=HALVES)),
            (experts(2, 1, E).rearrange("h (n d) -> h n d", d=P),
             a["L0_ffn_w2"].rearrange("e (c h) d -> h (e c) d", c=HALVES)),
            (late_raw(UP1, MLP1 * P), a["L1_ffn_w1"]),
            (late_raw(DN1, MLP1 * P).rearrange("h (c d) -> h c d", c=MLP1),
             a["L1_ffn_w2"].rearrange("(c h) d -> h c d", c=MLP1)),
            (late_raw(DN0, MLP0 * P).rearrange("h (c d) -> h c d", c=MLP0),
             a["L0_attn_W2"].rearrange("(c h) d -> h c d", c=MLP0)),
        ]
        SMALL = [
            (r_raw[:, :], a["L0_ffn_router_w"]),
            (ebias[:, :], a["L0_ffn_experts_bias"].partition_broadcast(P)),
            (qkv_raw[:, :, :], a["L1_attn_w_qkv"].rearrange("(c e) d -> e c d", c=3)),
            (fc_raw[:, :], a["L1_attn_w_fc"]),
            (bfc[:, :], a["L1_attn_b_fc"].partition_broadcast(P)),
            (gamma[:, :], a["L1_attn_gamma"].partition_broadcast(P)),
            (beta[:, :], a["L1_attn_beta"].partition_broadcast(P)),
            (f_b1[:, :], a["L1_ffn_b1"].rearrange("(c p) -> p c", p=P)),
            (f_b2[:, :], a["L1_ffn_b2"].unsqueeze(1)),
        ]

        def flat(t):
            return t[:, :, :].rearrange("p a b -> p (a b)")

        def project(pe, o, start_col, x_hi, x_lo, start=True, stop=True):
            hi, lo = late(start_col)
            return mm3(pe, o, hi, lo, x_hi, x_lo, start=start, stop=stop)

        def mm3(pe, o, weight_hi, weight_lo, x_hi, x_lo, start=True, stop=True):
            pe.matmul(o, weight_hi, x_hi, start=start, stop=False)
            pe.matmul(o, weight_hi, x_lo, start=False, stop=False)
            return pe.matmul(o, weight_lo, x_hi, start=False, stop=stop)

        def turn_tiles(pe, o, x):
            for j in range(TILES):
                m = pe.transpose(o[:, j * P:(j + 1) * P], x(j), ident[:, :])
            return m

        class Norm:
            def __init__(self, name):
                self.stats = sb(f"{name}_stats", [P, TILES, 6])
                self.moments = sb(f"{name}_moments", [P, TILES, 2])
                self.var_eps = sb(f"{name}_var_eps", [P, TILES])
                self.rstd = sb(f"{name}_rstd", [P, TILES])
                self.moments_ready = sem(f"{name}_moments_ready", "dve")
                self.rstd_ready = sem(f"{name}_rstd_ready", "pool")
                self.ready = sem(f"{name}_ready", "dve")

        def norm_moments(dve, n, b, x):
            for j in range(TILES):
                dve.bn_stats(n.stats[:, j, :], x[:, j, :]).then_inc(n.moments_ready, 1)
            wait_apart(dve, n.moments_ready, at((TILES + 1) * b + TILES))
            for j in range(TILES):
                i = dve.bn_aggr(n.moments[:, j, :], n.stats[:, j, :])
            i.then_inc(n.moments_ready, 1)

        def norm_rstd(pool, n, b):
            pool.wait_ge(n.moments_ready, at((TILES + 1) * (b + 1)))
            pool.tensor_tensor(n.var_eps[:, :], n.moments[:, :, 1], eps_row[:, :], ALU.add).then_inc(n.rstd_ready, 1)
            pool.wait_ge(n.rstd_ready, at(2 * b + 1))
            pool.tensor_tensor(n.rstd[:, :], n.var_eps[:, :], minus_half[:, :], ALU.pow).then_inc(n.rstd_ready, 1)

        def norm_apply(dve, n, b, o, x):
            dve.wait_ge(n.rstd_ready, at(2 * b + 2))
            for j in range(TILES):
                i = dve.tensor_scalar(o[:, j, :], x[:, j, :], n.moments[:, j, 0:1], n.rstd[:, j:j + 1],
                                      ALU.subtract, ALU.mult)
            i.then_inc(n.ready, 1)

        g_x = [tok(0), tok(1)]
        g_xhat = [tok(2), tok(3)]
        g_hhi, g_hlo = [bufr(0), bufr(1)], [bufr(2), bufr(3)]
        g_z, g_log, g_ls = [work[0:HK, i, :] for i in (4, 5, 6)]
        g_lshi, g_lslo = [workr[0:HK, i, :] for i in (4, 5)]
        g_v = buf(7)
        g_dec = [buf(8 + k) for k in range(DK)]
        g_kv = [buf(12 + k) for k in range(DK)]
        g_S = [buf(16 + k) for k in range(DK)]
        g_o = [buf(20), buf(21)]
        g_sq = buf(22)
        g_r = buf(23)

        g_loaded = [sem(f"g_loaded{i}") for i in range(2)]
        g_norm = Norm("g_norm")
        g_turned = sem("g_turned", "pe")
        g_hi_ready = sem("g_hi_ready", "act")
        g_lo_ready = sem("g_lo_ready", "dve")
        g_gk_done = sem("g_gk_done", "pe")
        g_v_done = sem("g_v_done", "pe")
        g_g_done = sem("g_g_done", "pe")
        g_k_done = sem("g_k_done", "pe")
        g_dec_done = sem("g_dec_done", "pe")
        g_q_done = sem("g_q_done", "pe")
        g_ms_done = sem("g_ms_done", "pe")
        g_z_ready = sem("g_z_ready", "act")
        g_abs_ready = sem("g_abs_ready", "act")
        g_exp_ready = sem("g_exp_ready", "act")
        g_log_ready = sem("g_log_ready", "act")
        g_v_ready = sem("g_v_ready", "act")
        g_gate_ready = sem("g_gate_ready", "act")
        g_dec_ready = sem("g_dec_ready", "act")
        g_sq_ready = sem("g_sq_ready", "act")
        g_ln_ready = sem("g_ln_ready", "act")
        g_r_ready = sem("g_r_ready", "act")
        g_ls_ready = sem("g_ls_ready", "dve")
        g_lshi_ready = sem("g_lshi_ready", "dve")
        g_lslo_ready = sem("g_lslo_ready", "pool")
        g_kv_ready = sem("g_kv_ready", "dve")
        g_S_ready = sem("g_S_ready", "dve")
        g_qS_ready = sem("g_qS_ready", "dve")
        g_sum_ready = sem("g_sum_ready", "pool")
        g_o_ready = sem("g_o_ready", "pool")
        g_rms_ready = sem("g_rms_ready", "pool")

        Q_BANK = [1, 2, 3, 1]

        def gla_sync(sp):
            def load(b, r):
                sp.dma_start(g_x[r][:, :, :], a["L0_attn_x"][b].rearrange("(j p) d -> p j d", p=P)).then_inc(g_loaded[r], 16)
            load(0, 0)
            load(1, 1)
            return load

        def gla_loads(sp, load):
            with sp.Fori(1, B // 2) as i:
                b = 2 * i
                for r in range(2):
                    sp.wait_ge(g_norm.ready, at(b + r - 1))
                    load(b + r, r)

        def gla_pe(pe):
            def step(s, r):
                b, q = s - 1, 1 - r
                if there(b):
                    hhi, hlo = g_hhi[q][:, :], g_hlo[q][:, :]

                    def apply(block, o):
                        return mm3(pe, o[:, :], w_hi[:, block, :], w_lo[:, block, :], hhi, hlo)
                    pe.wait_ge(g_lo_ready, at(b + 1))
                    pe.wait_ge(g_qS_ready, at(4 * b))
                    apply(GK, bank[1]).then_inc(g_gk_done, 1)
                    apply(V, bank[2]).then_inc(g_v_done, 1)
                if there(s - 2):
                    pe.wait_ge(g_sq_ready, at(s - 1))
                    pe.matmul(bank[0][:, :], head_mean[:, :], g_sq[:, :], start=True, stop=True).then_inc(g_ms_done, 1)
                if there(b):
                    apply(G, bank[3]).then_inc(g_g_done, 1)
                    for k in range(DK):
                        pe.wait_ge(g_dec_ready, at(DK * (b - 1) + k + 1))
                        apply(K0 + k, bank[4 + k]).then_inc(g_k_done, 1)
                if there(s):
                    pe.wait_ge(g_norm.ready, at(s + 1))
                    pe.wait_ge(g_ln_ready, at(s - 1))
                    turn_tiles(pe, bank[0], lambda j: g_xhat[r][:, j, :]).then_inc(g_turned, 1)
                if there(b):
                    pe.wait_ge(g_lslo_ready, at(b + 1))
                    for k in range(DK):
                        pe.wait_ge(g_kv_ready, at(DK * b + k + 1))
                        pe.matmul(bank[4 + k][:, :], spread_k[:, k, :], g_lshi[:, :], start=True, stop=False)
                        pe.matmul(bank[4 + k][:, :], spread_k[:, k, :], g_lslo[:, :], start=False, stop=True)\
                          .then_inc(g_dec_done, 1)
                        if k == 0:
                            pe.wait_ge(g_abs_ready, at(b + 1))
                        elif k == 1:
                            pe.wait_ge(g_v_ready, at(b + 1))
                        elif k == 2:
                            pe.wait_ge(g_gate_ready, at(b + 1))
                        else:
                            pe.wait_ge(g_qS_ready, at(DK * b + 1))
                        apply(Q0 + k, bank[Q_BANK[k]]).then_inc(g_q_done, 1)
            pipelined(pe, step, 2)

        def gla_act(act):
            def step(s, r):
                b = s - 1
                if there(b):
                    act.wait_ge(g_gk_done, at(b + 1))
                    act.wait_ge(g_ls_ready, at(b))
                    act.activation(g_z[:, :], bank[1][0:HK, :], ACT.Identity, bias=w_bias[0:HK, GK:GK + 1]).then_inc(g_z_ready, 1)
                    act.wait_ge(g_v_done, at(b + 1))
                    act.wait_ge(g_kv_ready, at(DK * b))
                    act.activation(g_v[:, :], bank[2][:, :], ACT.Identity, bias=w_bias[:, V:V + 1]).then_inc(g_v_ready, 1)
                    act.activation(g_log[:, :], bank[1][0:HK, :], ACT.Abs, bias=w_bias[0:HK, GK:GK + 1]).then_inc(g_abs_ready, 1)
                    act.wait_ge(g_abs_ready, at(b + 1))
                    act.activation(g_log[:, :], g_log[:, :], ACT.Exp, scale=-1.0).then_inc(g_exp_ready, 1)
                if there(s - 2):
                    act.wait_ge(g_ms_done, at(s - 1))
                    act.wait_ge(g_rms_ready, at(s - 2))
                    act.activation(g_r[:, :], bank[0][:, :], ACT.Ln, bias=eps_row[:, 0:1]).then_inc(g_ln_ready, 1)
                    act.wait_ge(g_ln_ready, at(s - 1))
                    act.activation(g_r[:, :], g_r[:, :], ACT.Exp, scale=-0.5).then_inc(g_r_ready, 1)
                if there(b):
                    act.wait_ge(g_g_done, at(b + 1))
                    wait_apart(act, late_lo, at(2 * b + 2))
                    act.activation(gate[:, b, :], bank[3][:, :], ACT.Identity, bias=w_bias[:, G:G + 1]).then_inc(g_gate_ready, 1)
                    act.wait_ge(g_exp_ready, at(b + 1))
                    act.activation(g_log[:, :], g_log[:, :], ACT.Ln, bias=1.0).then_inc(g_log_ready, 1)
                if there(s):
                    act.wait_ge(g_turned, at(s + 1))
                    act.wait_ge(g_q_done, at(DK * (s - 1)))
                    act.activation(g_hhi[r][:, :], bank[0][:, :], ACT.Copy).then_inc(g_hi_ready, 1)
                if there(b):
                    for k in range(DK):
                        act.wait_ge(g_dec_done, at(DK * b + k + 1))
                        act.wait_ge(g_S_ready, at(DK * (b - 1) + k + 1))
                        act.activation(g_dec[k][:, :], bank[4 + k][:, :], ACT.Exp, scale=1.0 / GATE_NORM)\
                           .then_inc(g_dec_ready, 1)
                    act.wait_ge(g_o_ready, at(b + 1))
                    act.wait_ge(g_ms_done, at(b))
                    act.activation(g_sq[:, :], g_o[1 - r][:, :], ACT.Square).then_inc(g_sq_ready, 1)
                if there(s):
                    act.wait_ge(late_raw_in, 16 * len(LATE))
                    for half, raw in enumerate((gate[:, s, :], rms_o[:, s, :])):
                        act.activation(w_late_hi[:, half * B + s, :], raw, ACT.Copy).then_inc(late_hi, 1)
            pipelined(act, step, 2)

        def gla_dve(dve):
            def step(s, r):
                b = s - 1
                if there(s):
                    dve.wait_ge(g_loaded[r], 8 * (s - r) + 16)
                    norm_moments(dve, g_norm, s, g_x[r])
                if there(b):
                    dve.wait_ge(g_v_ready, at(b + 1))
                    for k in range(DK):
                        dve.wait_ge(g_k_done, at(DK * b + k + 1))
                        dve.scalar_tensor_tensor(out=g_kv[k][:, :], in0=bank[4 + k][:, :], scalar=w_bias[:, K0 + k:K0 + k + 1],
                                                 in1=g_v[:, :], op0=ALU.add, op1=ALU.mult).then_inc(g_kv_ready, 1)
                if there(s):
                    dve.wait_ge(g_turned, at(s - 1))
                    norm_apply(dve, g_norm, s, g_xhat[r], g_x[r])
                if there(b):
                    dve.wait_ge(g_z_ready, at(b + 1))
                    dve.wait_ge(g_log_ready, at(b + 1))
                    dve.wait_ge(g_lslo_ready, at(b))
                    dve.scalar_tensor_tensor(out=g_ls[:, :], in0=g_z[:, :], scalar=0.0, in1=g_log[:, :],
                                             op0=ALU.min, op1=ALU.subtract).then_inc(g_ls_ready, 1)
                    dve.wait_ge(g_ls_ready, at(b + 1))
                    dve.wait_ge(g_dec_done, at(DK * b))
                    dve.tensor_copy(g_lshi[:, :], g_ls[:, :]).then_inc(g_lshi_ready, 1)
                if there(s):
                    dve.wait_ge(g_hi_ready, at(s + 1))
                    dve.wait_ge(g_q_done, at(DK * (s - 1)))
                    dve.tensor_tensor(g_hlo[r][:, :], bank[0][:, :], g_hhi[r][:, :].bitcast(F32), ALU.subtract)\
                       .then_inc(g_lo_ready, 1)
                if there(b):
                    for k in range(DK):
                        dve.wait_ge(g_dec_ready, at(DK * b + k + 1))
                        dve.wait_ge(g_kv_ready, at(DK * b + k + 1))
                        dve.wait_ge(g_o_ready, at(b))
                        dve.tensor_tensor_scan(g_S[k][:, :], g_dec[k][:, :], g_kv[k][:, :], 0.0, ALU.mult, ALU.add)\
                           .then_inc(g_S_ready, 1)
                        dve.wait_ge(g_S_ready, at(DK * b + k + 1))
                        dve.wait_ge(g_q_done, at(DK * b + k + 1))
                        dve.scalar_tensor_tensor(out=g_S[k][:, :], in0=bank[Q_BANK[k]][:, :],
                                                 scalar=w_bias[:, Q0 + k:Q0 + k + 1], in1=g_S[k][:, :],
                                                 op0=ALU.add, op1=ALU.mult).then_inc(g_qS_ready, 1)
            pipelined(dve, step, 2)

        def gla_pool(pool):
            def step(s, r):
                b = s - 1
                if there(s):
                    norm_rstd(pool, g_norm, s)
                if there(b):
                    pool.wait_ge(g_lshi_ready, at(b + 1))
                    pool.wait_ge(g_dec_done, at(DK * b))
                    pool.tensor_tensor(g_lslo[:, :], g_ls[:, :], g_lshi[:, :].bitcast(F32), ALU.subtract)\
                        .then_inc(g_lslo_ready, 1)
                if there(s - 2):
                    pool.wait_ge(g_r_ready, at(s - 1))
                    pool.tensor_tensor(rms_o[:, s - 2, :], g_o[r][:, :], g_r[:, :], ALU.mult).then_inc(g_rms_ready, 1)
                if there(b):
                    for h in range(DK // 2):
                        pool.wait_ge(g_qS_ready, at(DK * b + 2 * h + 2))
                        pool.tensor_tensor(g_S[2 * h][:, :], g_S[2 * h][:, :], g_S[2 * h + 1][:, :], ALU.add)\
                            .then_inc(g_sum_ready, 1)
                    pool.wait_ge(g_sum_ready, at(2 * b + 2))
                    pool.wait_ge(g_rms_ready, at(b - 1))
                    pool.tensor_tensor(g_o[1 - r][:, :], g_S[0][:, :], g_S[2][:, :], ALU.add).then_inc(g_o_ready, 1)
                if there(s):
                    for half, raw in enumerate((gate[:, s, :], rms_o[:, s, :])):
                        pool.wait_ge(late_hi, at(2 * s + half + 1))
                        pool.tensor_tensor(w_late_lo[:, half * B + s, :], raw, w_late_hi[:, half * B + s, :].bitcast(F32),
                                           ALU.subtract).then_inc(late_lo, 1)
            pipelined(pool, step, 2)

        h_x = [tok(0), tok(1)]
        h_tanh, h_gs, h_og = buf(2), buf(3), buf(4)
        h_oghi, h_oglo = [bufr(0), bufr(1)], [bufr(2), bufr(3)]
        h_y, h_y2 = buf(5), buf(6)
        h_x1, h_xhat, h_acc = tok(7), tok(8), tok(9)
        h_hi, h_lo = bufr(4), bufr(5)
        h_up = [buf(10 + c) for c in range(MLP0)]
        h_uphi = [[bufr(6 + 2 * c + i) for i in range(2)] for c in range(MLP0)]
        h_uplo = [[bufr(10 + 2 * c + i) for i in range(2)] for c in range(MLP0)]

        h_loaded = [sem(f"h_loaded{i}") for i in range(2)]
        h_tanh_ready = sem("h_tanh_ready", "act")
        h_gs_ready = sem("h_gs_ready", "dve")
        h_og_ready = sem("h_og_ready", "dve")
        h_oghi_ready = sem("h_oghi_ready", "act")
        h_oglo_ready = sem("h_oglo_ready", "pool")
        h_wo_done = sem("h_wo_done", "pe")
        h_y_ready = sem("h_y_ready", "act")
        h_y_turned = sem("h_y_turned", "pe")
        h_x1_ready = sem("h_x1_ready", "dve")
        h_xx_ready = sem("h_xx_ready", "pool")
        h_norm = Norm("h_norm")
        h_turned = sem("h_turned", "pe")
        h_hi_ready = sem("h_hi_ready", "act")
        h_lo_ready = sem("h_lo_ready", "dve")
        h_up_done = sem("h_up_done", "pe")
        h_gelu_ready = sem("h_gelu_ready", "act")
        h_uphi_ready = sem("h_uphi_ready", "dve")
        h_uplo_ready = sem("h_uplo_ready", "pool")
        h_down_done = sem("h_down_done", "pe")
        h_y2_ready = sem("h_y2_ready", "act")
        h_y2_turned = sem("h_y2_turned", "pe")
        h_acc_ready = sem("h_acc_ready", "dve")
        h_out = Norm("h_out")

        def mid_sync(sp):
            def load(b, r):
                sp.dma_start(h_x[r][:, :, :], a["L0_attn_x"][b].rearrange("(j p) d -> p j d", p=P)).then_inc(h_loaded[r], 16)
            for r in range(2):
                sp.wait_ge(g_norm.ready, at(B - 1 + r))
                load(r, r)
            with sp.Fori(1, B // 2) as i:
                b = 2 * i
                for r in range(2):
                    sp.wait_ge(h_xx_ready, at(b + r - 1))
                    load(b + r, r)

        def mid_pe(pe):
            def step(s, r):
                b = s - 1
                if there(b):
                    pe.wait_ge(h_oglo_ready, at(b + 1))
                    pe.wait_ge(h_oghi_ready, at(b + 1))
                    pe.wait_ge(h_y_ready, at(b))
                    mm3(pe, bank[0][:, :], wo_hi[:, :], wo_lo[:, :], h_oghi[1 - r][:, :], h_oglo[1 - r][:, :])\
                        .then_inc(h_wo_done, 1)
                b = s - 2
                if there(b):
                    pe.wait_ge(h_norm.ready, at(b + 1))
                    pe.wait_ge(h_lo_ready, at(b))
                    turn_tiles(pe, bank[2], lambda j: h_xhat[:, j, :]).then_inc(h_turned, 1)
                b = s - 3
                if there(b):
                    pe.wait_ge(h_uplo_ready, at(MLP0 * b + MLP0))
                    pe.wait_ge(h_y2_ready, at(b))
                    for c in range(MLP0):
                        m = project(pe, bank[5][:, :], DN0 + c * P, h_uphi[c][1 - r], h_uplo[c][1 - r],
                                    start=c == 0, stop=c == MLP0 - 1)
                    m.then_inc(h_down_done, 1)
                b = s - 1
                if there(b):
                    pe.wait_ge(h_y_ready, at(b + 1))
                    pe.wait_ge(h_x1_ready, at(b))
                    turn_tiles(pe, bank[1], lambda j: h_y[:, j * P:(j + 1) * P]).then_inc(h_y_turned, 1)
                b = s - 2
                if there(b):
                    pe.wait_ge(h_lo_ready, at(b + 1))
                    for c in range(MLP0):
                        pe.wait_ge(h_gelu_ready, at(MLP0 * (b - 1) + c + 1))
                        mm3(pe, bank[3 + c][:, :], w_hi[:, UP0 + c, :], w_lo[:, UP0 + c, :], h_hi[:, :], h_lo[:, :])\
                            .then_inc(h_up_done, 1)
                b = s - 3
                if there(b):
                    pe.wait_ge(h_y2_ready, at(b + 1))
                    pe.wait_ge(h_acc_ready, at(b))
                    turn_tiles(pe, bank[6], lambda j: h_y2[:, j * P:(j + 1) * P]).then_inc(h_y2_turned, 1)
            pipelined(pe, step, 3)

        def mid_act(act):
            def step(s, r):
                if there(s):
                    act.wait_ge(h_gs_ready, at(s))
                    act.activation(h_tanh[:, :], gate[:, s, :], ACT.Tanh, scale=0.5).then_inc(h_tanh_ready, 1)
                b = s - 1
                if there(b):
                    act.wait_ge(h_wo_done, at(b + 1))
                    act.wait_ge(h_y_turned, at(b))
                    act.activation(h_y[:, :], bank[0][:, :], ACT.Copy).then_inc(h_y_ready, 1)
                b = s - 2
                if there(b):
                    act.wait_ge(h_turned, at(b + 1))
                    act.wait_ge(h_up_done, at(MLP0 * b))
                    act.activation(h_hi[:, :], bank[2][:, :], ACT.Copy).then_inc(h_hi_ready, 1)
                b = s - 3
                if there(b):
                    act.wait_ge(h_down_done, at(b + 1))
                    act.wait_ge(h_y2_turned, at(b))
                    act.activation(h_y2[:, :], bank[5][:, :], ACT.Identity, bias=b2_col[:, :]).then_inc(h_y2_ready, 1)
                if there(s):
                    act.wait_ge(h_og_ready, at(s + 1))
                    act.wait_ge(h_wo_done, at(s - 1))
                    act.activation(h_oghi[r][:, :], h_og[:, :], ACT.Copy).then_inc(h_oghi_ready, 1)
                b = s - 2
                if there(b):
                    for c in range(MLP0):
                        act.wait_ge(h_up_done, at(MLP0 * b + c + 1))
                        act.wait_ge(h_uplo_ready, at(MLP0 * (b - 1) + c + 1))
                        act.activation(h_up[c][:, :], bank[3 + c][:, :], ACT.Gelu, bias=w_bias[:, UP0 + c:UP0 + c + 1])\
                           .then_inc(h_gelu_ready, 1)
            pipelined(act, step, 3)

        def mid_dve(dve):
            def step(s, r):
                b = s - 1
                if there(b):
                    dve.wait_ge(h_y_turned, at(b + 1))
                    dve.wait_ge(h_loaded[1 - r], 8 * (b - (1 - r)) + 16)
                    dve.wait_ge(h_xx_ready, at(b))
                    dve.tensor_tensor(flat(h_x1), bank[1][:, :], flat(h_x[1 - r]), ALU.add).then_inc(h_x1_ready, 1)
                    dve.wait_ge(h_x1_ready, at(b + 1))
                    norm_moments(dve, h_norm, b, h_x1)
                b = s - 2
                if there(b):
                    dve.wait_ge(h_hi_ready, at(b + 1))
                    dve.wait_ge(h_up_done, at(MLP0 * b))
                    dve.tensor_tensor(h_lo[:, :], bank[2][:, :], h_hi[:, :].bitcast(F32), ALU.subtract).then_inc(h_lo_ready, 1)
                if there(s):
                    dve.wait_ge(h_tanh_ready, at(s + 1))
                    dve.scalar_tensor_tensor(out=h_gs[:, :], in0=h_tanh[:, :], scalar=1.0, in1=gate[:, s, :],
                                             op0=ALU.add, op1=ALU.mult).then_inc(h_gs_ready, 1)
                    dve.wait_ge(h_gs_ready, at(s + 1))
                    dve.wait_ge(h_oglo_ready, at(s))
                    dve.wait_ge(g_rms_ready, at(s + 1))
                    dve.tensor_tensor(h_og[:, :], h_gs[:, :], rms_o[:, s, :], ALU.mult).then_inc(h_og_ready, 1)
                b = s - 1
                if there(b):
                    dve.wait_ge(h_turned, at(b))
                    norm_apply(dve, h_norm, b, h_xhat, h_x1)
                b = s - 3
                if there(b):
                    dve.wait_ge(h_y2_turned, at(b + 1))
                    dve.wait_ge(h_xx_ready, at(b + 1))
                    dve.wait_ge(h_out.ready, at(b))
                    dve.tensor_tensor(flat(h_acc), bank[6][:, :], R[:, b, :, :].rearrange("p a b -> p (a b)"),
                                      ALU.add).then_inc(h_acc_ready, 1)
                    dve.wait_ge(h_acc_ready, at(b + 1))
                    norm_moments(dve, h_out, b, h_acc)
                b = s - 2
                if there(b):
                    for c in range(MLP0):
                        dve.wait_ge(h_gelu_ready, at(MLP0 * b + c + 1))
                        dve.wait_ge(h_down_done, at(b - 1))
                        dve.tensor_copy(h_uphi[c][r][:, :], h_up[c][:, :]).then_inc(h_uphi_ready, 1)
                b = s - 3
                if there(b):
                    norm_apply(dve, h_out, b, R[:, b, :, :], h_acc)
            pipelined(dve, step, 3)

        def mid_pool(pool):
            def step(s, r):
                b = s - 1
                if there(b):
                    norm_rstd(pool, h_norm, b)
                    pool.wait_ge(h_x1_ready, at(b + 1))
                    pool.tensor_tensor(R[:, b, :, :].rearrange("p a b -> p (a b)"), flat(h_x[1 - r]), flat(h_x1), ALU.add)\
                        .then_inc(h_xx_ready, 1)
                if there(s):
                    pool.wait_ge(h_oghi_ready, at(s + 1))
                    pool.wait_ge(h_wo_done, at(s - 1))
                    pool.tensor_tensor(h_oglo[r][:, :], h_og[:, :], h_oghi[r][:, :].bitcast(F32), ALU.subtract)\
                        .then_inc(h_oglo_ready, 1)
                b = s - 3
                if there(b):
                    norm_rstd(pool, h_out, b)
                b = s - 2
                if there(b):
                    for c in range(MLP0):
                        pool.wait_ge(h_uphi_ready, at(MLP0 * b + c + 1))
                        pool.wait_ge(h_down_done, at(b - 1))
                        pool.tensor_tensor(h_uplo[c][r][:, :], h_up[c][:, :], h_uphi[c][r][:, :].bitcast(F32), ALU.subtract)\
                            .then_inc(h_uplo_ready, 1)
            pipelined(pool, step, 3)

        DOWN_LAG = 3
        RING = 4
        assert (2 * UNITS) % RING == 0
        m_x = [tok(0), tok(1)]
        m_hi, m_lo = [bufr(0), bufr(1)], [bufr(2), bufr(3)]
        m_logit = sb("m_logit", [P, TILES, E])
        m_top = sb("m_top", [P, TILES, 8])
        m_top_i = sb("m_top_i", [P, TILES, 8], U32)
        m_top_f = sb("m_top_f", [P, TILES, 2])
        m_diff = sb("m_diff", [P, TILES])
        m_th = sb("m_th", [P, TILES])
        m_w = sb("m_w", [P, 2, TILES])
        m_one = [sb(f"m_one{i}", [P, TILES, E]) for i in range(2)]
        m_part = [sb(f"m_part{i}", [P, TILES, E]) for i in range(2)]
        m_cw = sb("m_cw", [P, TILES, E])
        m_cwhi, m_cwlo = [[workr[0:E, i, :] for i in pair] for pair in ((4, 5), (6, 7))]
        m_silu, m_prod = [buf(2), buf(3)], [buf(4), buf(5)]
        m_sc, m_y = buf(6), buf(7)
        m_phi = [bufr(8 + i) for i in range(RING)]
        m_plo = [bufr(12 + i) for i in range(RING)]
        m_acc = tok(8)

        m_loaded = [sem(f"m_loaded{i}") for i in range(2)]
        m_turned = sem("m_turned", "pe")
        m_hi_ready = sem("m_hi_ready", "act")
        m_lo_ready = sem("m_lo_ready", "dve")
        m_logit_done = sem("m_logit_done", "pe")
        m_logit_ready = sem("m_logit_ready", "dve")
        m_chain = sem("m_chain", "dve")
        m_th_ready = sem("m_th_ready", "act")
        m_cw_turned = sem("m_cw_turned", "pe")
        m_cwhi_ready = sem("m_cwhi_ready", "dve")
        m_cwlo_ready = sem("m_cwlo_ready", "dve")
        m_up_done = sem("m_up_done", "pe")
        m_cw_done = sem("m_cw_done", "pe")
        m_silu_ready = sem("m_silu_ready", "act")
        m_sc_ready = sem("m_sc_ready", "dve")
        m_prod_ready = sem("m_prod_ready", "dve")
        m_phi_ready = sem("m_phi_ready", "act")
        m_plo_ready = sem("m_plo_ready", "pool")
        m_down_done = sem("m_down_done", "pe")
        m_y_ready = sem("m_y_ready", "act")
        m_y_turned = sem("m_y_turned", "pe")
        m_acc_ready = sem("m_acc_ready", "dve")
        m_out = Norm("m_out")
        ROUTED = E * HALVES
        CHAIN = 8

        def moe_sync(sp):
            for r in range(2):
                sp.wait_ge(h_out.ready, at(r + 1))
                sp.wait_ge(h_xx_ready, at(B - 1 + r))
                sp.dma_start(m_x[r][:, :, :], R[:, r, :, :]).then_inc(m_loaded[r], 16)
            with sp.Fori(1, B // 2) as i:
                b = 2 * i
                for r in range(2):
                    wait_apart(sp, m_acc_ready, at(b + r - 1))
                    wait_apart(sp, h_out.ready, at(b + r + 1))
                    sp.dma_start(m_x[r][:, :, :], R[:, b + r, :, :]).then_inc(m_loaded[r], 16)

        def units(s, r):
            return [((1 - r) * UNITS + u) % RING for u in range(UNITS)]

        def moe_pe(pe):
            pe.wait_ge(h_out.ready, at(B))
            def up(b, u, q):
                e, c = divmod(u, HALVES)
                pe.wait_ge(m_prod_ready, at(UNITS * b + u - 1))
                project(pe, bank[2 + u % 2][:, :], e * HID + c * P, m_hi[q], m_lo[q])
                project(pe, bank[4 + u % 2][:, :], EXPERTS + e * HID + c * P, m_hi[q], m_lo[q])\
                    .then_inc(m_up_done, 1)

            def weight(b, e, q):
                pe.wait_ge(m_sc_ready, at(ROUTED * b + HALVES * e))
                pe.matmul(bank[1][:, :], pick_e[:, e, :], m_cwhi[q][:, :], start=True, stop=False)
                pe.matmul(bank[1][:, :], pick_e[:, e, :], m_cwlo[q][:, :], start=False, stop=True).then_inc(m_cw_done, 1)

            def down(b, u, slot):
                e, c = divmod(u, HALVES)
                pe.wait_ge(m_phi_ready, at(UNITS * b + u + 1))
                pe.wait_ge(m_plo_ready, at(UNITS * b + u + 1))
                if u == 0:
                    pe.wait_ge(m_y_ready, at(b))
                project(pe, bank[6][:, :], 2 * EXPERTS + e * HID + c * P, m_phi[slot], m_plo[slot],
                        start=u == 0, stop=u == UNITS - 1).then_inc(m_down_done, 1)

            def step(s, r):
                b, q = s - 1, 1 - r
                slots, before = units(s, r), units(s - 1, 1 - r)
                for u in range(UNITS):
                    if there(b):
                        if u == 0:
                            pe.wait_ge(m_lo_ready, at(b + 1))
                        up(b, u, q)
                        if u >= HALVES and u % HALVES == 0:
                            if u == HALVES:
                                pe.wait_ge(m_cwlo_ready, at(b + 1))
                            weight(b, u // HALVES - 1, q)
                    v = u - DOWN_LAG
                    if v < 0:
                        if there(s - 2):
                            down(s - 2, UNITS + v, before[v])
                    elif there(b):
                        down(b, v, slots[v])
                    if u == 5 and there(s - 2):
                        pe.wait_ge(m_y_ready, at(s - 1))
                        pe.wait_ge(m_logit_ready, at(s - 1))
                        turn_tiles(pe, bank[7], lambda j: m_y[:, j * P:(j + 1) * P]).then_inc(m_y_turned, 1)
                    if u == 7 and there(s):
                        pe.wait_ge(m_loaded[r], 8 * (s - r) + 16)
                        pe.wait_ge(m_cwlo_ready, at(s))
                        turn_tiles(pe, bank[0], lambda j: m_x[r][:, j, :]).then_inc(m_turned, 1)
                    if u == 10 and there(s):
                        pe.wait_ge(m_lo_ready, at(s + 1))
                        pe.wait_ge(m_acc_ready, at(s - 1))
                        for j in range(TILES):
                            m = mm3(pe, bank[7][:, j * E:(j + 1) * E], m_hi[r][:, j * P:(j + 1) * P],
                                    m_lo[r][:, j * P:(j + 1) * P], r_hi[:, :], r_lo[:, :])
                        m.then_inc(m_logit_done, 1)
                    if u == 15 and there(s):
                        pe.wait_ge(m_chain, at(CHAIN * s + CHAIN))
                        for j in range(TILES):
                            m = pe.transpose(bank[0][0:E, j * P:(j + 1) * P], m_cw[:, j, :], ident[:, :])
                        m.then_inc(m_cw_turned, 1)
            pipelined(pe, step, 2)

        def moe_act(act):
            def phi(b, u, slot):
                act.wait_ge(m_prod_ready, at(UNITS * b + u + 1))
                act.wait_ge(m_down_done, at(UNITS * b + u + 1 - RING))
                act.activation(m_phi[slot][:, :], m_prod[u % 2][:, :], ACT.Copy).then_inc(m_phi_ready, 1)

            def step(s, r):
                b = s - 1
                slots = units(s, r)
                for u in range(UNITS):
                    if there(b):
                        act.wait_ge(m_up_done, at(UNITS * b + u + 1))
                        act.wait_ge(m_prod_ready, at(UNITS * b + u - 1))
                        act.activation(m_silu[u % 2][:, :], bank[2 + u % 2][:, :], ACT.Silu).then_inc(m_silu_ready, 1)
                        if u >= 1:
                            phi(b, u - 1, slots[u - 1])
                    if u == 3 and there(s - 2):
                        act.wait_ge(m_down_done, at(UNITS * (s - 1)))
                        act.wait_ge(m_y_turned, at(s - 2))
                        act.activation(m_y[:, :], bank[6][:, :], ACT.Copy).then_inc(m_y_ready, 1)
                    if u == 8 and there(s):
                        act.wait_ge(m_turned, at(s + 1))
                        act.wait_ge(m_up_done, at(UNITS * (s - 1)))
                        act.activation(m_hi[r][:, :], bank[0][:, :], ACT.Copy).then_inc(m_hi_ready, 1)
                    if u == 12 and there(s):
                        act.wait_ge(m_chain, at(CHAIN * s + 2))
                        act.activation(m_th[:, :], m_diff[:, :], ACT.Tanh, scale=0.5).then_inc(m_th_ready, 1)
                if there(b):
                    phi(b, UNITS - 1, slots[UNITS - 1])
            pipelined(act, step, 2)

        def moe_dve(dve):
            def wide(x):
                return x.unsqueeze(2).broadcast_to([P, TILES, E])

            def step(s, r):
                b = s - 1

                def link(i, n):
                    i.then_inc(m_chain, 1)
                    wait_apart(dve, m_chain, at(CHAIN * s + n))
                for u in range(UNITS):
                    if there(b):
                        x = m_silu[u % 2][:, :]
                        dve.wait_ge(m_silu_ready, at(UNITS * b + u + 1))
                        if u >= HALVES:
                            dve.wait_ge(m_cw_done, at(E * b + (u - HALVES) // HALVES + 1))
                            dve.wait_ge(m_prod_ready, at(UNITS * b + u))
                            dve.tensor_tensor(m_sc[:, :], bank[1][:, :], x, ALU.mult).then_inc(m_sc_ready, 1)
                            dve.wait_ge(m_sc_ready, at(ROUTED * b + u - HALVES + 1))
                            x = m_sc[:, :]
                        dve.wait_ge(m_plo_ready, at(UNITS * b + u - 1))
                        dve.wait_ge(m_phi_ready, at(UNITS * b + u - 1))
                        dve.tensor_tensor(m_prod[u % 2][:, :], bank[4 + u % 2][:, :], x, ALU.mult).then_inc(m_prod_ready, 1)
                    if u == 6 and there(s - 2):
                        dve.wait_ge(m_y_turned, at(s - 1))
                        dve.wait_ge(m_out.ready, at(s - 2))
                        dve.tensor_tensor(flat(m_acc), bank[7][:, :], flat(m_x[r]), ALU.add).then_inc(m_acc_ready, 1)
                        dve.wait_ge(m_acc_ready, at(s - 1))
                        norm_moments(dve, m_out, s - 2, m_acc)
                    if u == 8 and there(s - 2):
                        norm_apply(dve, m_out, s - 2, R[:, s - 2, :, :], m_acc)
                    if u == 9 and there(s):
                        dve.wait_ge(m_hi_ready, at(s + 1))
                        dve.tensor_tensor(m_lo[r][:, :], bank[0][:, :], m_hi[r][:, :].bitcast(F32), ALU.subtract)\
                           .then_inc(m_lo_ready, 1)
                    if u == 11 and there(s):
                        dve.wait_ge(m_logit_done, at(s + 1))
                        dve.tensor_tensor(m_logit[:, :, :], bank[7][:, 0:TILES * E].rearrange("p (j e) -> p j e", e=E),
                                          ebias[:, :].unsqueeze(1).broadcast_to([P, TILES, E]), ALU.add)\
                           .then_inc(m_logit_ready, 1)
                        wait_apart(dve, m_logit_ready, at(s + 1))
                        for j in range(TILES):
                            i = dve.max(m_top[:, j, :], m_logit[:, j, :])
                        link(i, 1)
                        link(dve.tensor_tensor(m_diff[:, :], m_top[:, :, 0], m_top[:, :, 1], ALU.subtract), 2)
                        for j in range(TILES):
                            i = dve.max_index(m_top_i[:, j, :], m_top[:, j, :], m_logit[:, j, :])
                        link(i, 3)
                        link(dve.tensor_copy(m_top_f[:, :, :], m_top_i[:, :, 0:2]), 4)
                        for n in range(2):
                            i = dve.tensor_tensor(m_one[n][:, :, :], iota_e[:, :].unsqueeze(1).broadcast_to([P, TILES, E]),
                                                  wide(m_top_f[:, :, n]), ALU.is_equal)
                        link(i, 5)
                    if u == 13 and there(s):
                        dve.wait_ge(m_th_ready, at(s + 1))
                        dve.tensor_scalar(m_w[:, 0, :], m_th[:, :], 0.5, 0.5, ALU.mult, ALU.add)
                        link(dve.tensor_scalar(m_w[:, 1, :], m_th[:, :], -0.5, 0.5, ALU.mult, ALU.add), 6)
                        for n in range(2):
                            i = dve.tensor_tensor(m_part[n][:, :, :], m_one[n][:, :, :], wide(m_w[:, n, :]), ALU.mult)
                        link(i, 7)
                        link(dve.tensor_tensor(m_cw[:, :, :], m_part[0][:, :, :], m_part[1][:, :, :], ALU.add), 8)
                    if u == 16 and there(s):
                        dve.wait_ge(m_cw_turned, at(s + 1))
                        dve.wait_ge(m_cw_done, at(E * (s - 1)))
                        dve.tensor_copy(m_cwhi[r][:, :], bank[0][0:E, :]).then_inc(m_cwhi_ready, 1)
                        dve.wait_ge(m_cwhi_ready, at(s + 1))
                        dve.tensor_tensor(m_cwlo[r][:, :], bank[0][0:E, :], m_cwhi[r][:, :].bitcast(F32), ALU.subtract)\
                           .then_inc(m_cwlo_ready, 1)
            pipelined(dve, step, 2)

        def moe_pool(pool):
            def step(s, r):
                b = s - 1
                slots = units(s, r)
                for u in range(UNITS):
                    if there(b):
                        pool.wait_ge(m_phi_ready, at(UNITS * b + u + 1))
                        pool.wait_ge(m_down_done, at(UNITS * b + u + 1 - RING))
                        pool.tensor_tensor(m_plo[slots[u]][:, :], m_prod[u % 2][:, :], m_phi[slots[u]][:, :].bitcast(F32),
                                           ALU.subtract).then_inc(m_plo_ready, 1)
                    if u == 6 and there(s - 2):
                        norm_rstd(pool, m_out, s - 2)
            pipelined(pool, step, 2)

        c_x = [tok(0), tok(1)]
        c_hi, c_lo = [bufr(0), bufr(1)], [bufr(2), bufr(3)]
        c_qhi, c_qlo = [bufr(4), bufr(5)], [bufr(6), bufr(7)]
        c_xsum = buf(13)[:, 0:P]
        c_z = [buf(14 + i)[:, 0:P] for i in range(2)]
        c_xb = tok(2)
        c_max, c_bias, c_den, c_rden, c_att = [sb(f"c_{n}", [P, TILES]) for n in ("max", "bias", "den", "rden", "att")]
        c_exp = [buf(3 + j) for j in range(TILES)]
        c_h, c_hhat, c_hg, c_acc = tok(7), tok(8), tok(9), tok(10)
        c_xbeta = [tok(11), tok(12)]

        c_loaded = [sem(f"c_loaded{i}") for i in range(2)]
        c_turned = sem("c_turned", "pe")
        c_hi_ready = sem("c_hi_ready", "act")
        c_lo_ready = sem("c_lo_ready", "dve")
        c_q_done = sem("c_q_done", "pe")
        c_qhi_ready = sem("c_qhi_ready", "act")
        c_qlo_ready = sem("c_qlo_ready", "dve")
        c_xsum_done = sem("c_xsum_done", "pe")
        c_xsum_ready = sem("c_xsum_ready", "act")
        c_z_done = sem("c_z_done", "pe")
        c_z_ready = sem("c_z_ready", "act")
        c_xb_ready = sem("c_xb_ready", "pool")
        c_xbeta_ready = sem("c_xbeta_ready", "pool")
        c_score_done = sem("c_score_done", "pe")
        c_max_ready = sem("c_max_ready", "dve")
        c_bias_ready = sem("c_bias_ready", "dve")
        c_exp_ready = sem("c_exp_ready", "act")
        c_rden_ready = sem("c_rden_ready", "dve")
        c_att_ready = sem("c_att_ready", "dve")
        c_h_ready = sem("c_h_ready", "dve")
        c_hg_ready = sem("c_hg_ready", "pool")
        c_acc_ready = sem("c_acc_ready", "dve")
        c_inner = Norm("c_inner")
        c_out = Norm("c_out")

        def att_sync(sp):
            for r in range(2):
                sp.wait_ge(m_out.ready, at(B - 1 + r))
                sp.dma_start(c_x[r][:, :, :], R[:, r, :, :]).then_inc(c_loaded[r], 16)
            with sp.Fori(1, B // 2) as i:
                b = 2 * i
                for r in range(2):
                    sp.wait_ge(c_xbeta_ready, at(b + r - 1))
                    sp.wait_ge(c_xsum_done, at(b + r - 1))
                    sp.dma_start(c_x[r][:, :, :], R[:, b + r, :, :]).then_inc(c_loaded[r], 16)

        def att_pe(pe):
            pe.wait_ge(m_out.ready, at(B))
            def step(s, r):
                if there(s):
                    pe.wait_ge(c_loaded[r], 8 * (s - r) + 16)
                    pe.wait_ge(c_lo_ready, at(s))
                    turn_tiles(pe, bank[0], lambda j: c_x[r][:, j, :]).then_inc(c_turned, 1)
                    pe.wait_ge(c_xsum_ready, at(s))
                    for j in range(TILES):
                        m = pe.matmul(bank[2][:, 0:P], c_x[r][:, j, :], ones[:, :], start=j == 0, stop=j == TILES - 1)
                    m.then_inc(c_xsum_done, 1)
                b, q = s - 1, 1 - r
                for j in range(TILES):
                    if there(b):
                        if j == 0:
                            pe.wait_ge(c_qlo_ready, at(b + 1))
                        pe.wait_ge(c_exp_ready, at(TILES * (b - 1) + j + 1))
                        tile = slice(j * P, (j + 1) * P)
                        mm3(pe, bank[4 + j][:, :], c_qhi[q][:, tile], c_qlo[q][:, tile], c_hi[q][:, :], c_lo[q][:, :])\
                            .then_inc(c_score_done, 1)
                    if j == 1 and there(s):
                        pe.wait_ge(c_lo_ready, at(s + 1))
                        pe.wait_ge(c_qlo_ready, at(s))
                        mm3(pe, bank[1][:, :], qk_hi[:, :], qk_lo[:, :], c_hi[r][:, :], c_lo[r][:, :]).then_inc(c_q_done, 1)
                        pe.wait_ge(c_xsum_ready, at(s + 1))
                        pe.wait_ge(c_z_ready, at(s))
                        pe.matmul(bank[3][:, 0:P], c_xsum[:, :], vfc[:, :], start=True, stop=True).then_inc(c_z_done, 1)
            pipelined(pe, step, 2)

        def att_act(act):
            def step(s, r):
                if there(s):
                    act.wait_ge(c_turned, at(s + 1))
                    act.wait_ge(c_score_done, at(TILES * (s - 1)))
                    act.activation(c_hi[r][:, :], bank[0][:, :], ACT.Copy).then_inc(c_hi_ready, 1)
                    act.wait_ge(c_xsum_done, at(s + 1))
                    act.wait_ge(c_z_done, at(s))
                    act.activation(c_xsum[:, :], bank[2][:, 0:P], ACT.Copy).then_inc(c_xsum_ready, 1)
                b = s - 1
                for j in range(TILES):
                    if there(b):
                        act.wait_ge(c_bias_ready, at(TILES * b + j + 1))
                        act.wait_ge(c_att_ready, at(b))
                        act.activation(c_exp[j][:, :], bank[4 + j][:, :], ACT.Exp, bias=c_bias[:, j:j + 1], scale=SCALE,
                                       accum_out=c_den[:, j:j + 1]).then_inc(c_exp_ready, 1)
                    if j == 1 and there(s):
                        act.wait_ge(c_q_done, at(s + 1))
                        act.activation(c_qhi[r][:, :], bank[1][:, :], ACT.Copy).then_inc(c_qhi_ready, 1)
                        act.wait_ge(c_z_done, at(s + 1))
                        act.wait_ge(c_h_ready, at(s - 1))
                        act.activation(c_z[r][:, :], bank[3][:, 0:P], ACT.Copy).then_inc(c_z_ready, 1)
            pipelined(act, step, 2)

        def att_dve(dve):
            def step(s, r):
                b, q = s - 1, 1 - r
                if there(s):
                    dve.wait_ge(c_hi_ready, at(s + 1))
                    dve.tensor_tensor(c_lo[r][:, :], bank[0][:, :], c_hi[r][:, :].bitcast(F32), ALU.subtract)\
                       .then_inc(c_lo_ready, 1)
                for j in range(TILES):
                    if there(b):
                        dve.wait_ge(c_score_done, at(TILES * b + j + 1))
                        dve.wait_ge(c_bias_ready, at(TILES * b + j))
                        dve.tensor_reduce(c_max[:, j:j + 1], bank[4 + j][:, :], AX.X, ALU.max).then_inc(c_max_ready, 1)
                        dve.wait_ge(c_max_ready, at(TILES * b + j + 1))
                        dve.wait_ge(c_exp_ready, at(TILES * (b - 1) + j + 1))
                        dve.tensor_scalar(c_bias[:, j:j + 1], c_max[:, j:j + 1], -SCALE, None, ALU.mult)\
                           .then_inc(c_bias_ready, 1)
                    if j == 1 and there(s - 2):
                        norm_apply(dve, c_inner, s - 2, c_hhat, c_h)
                    if j == 2 and there(s):
                        dve.wait_ge(c_qhi_ready, at(s + 1))
                        dve.tensor_tensor(c_qlo[r][:, :], bank[1][:, :], c_qhi[r][:, :].bitcast(F32), ALU.subtract)\
                           .then_inc(c_qlo_ready, 1)
                if there(s - 2):
                    dve.wait_ge(c_hg_ready, at(s - 1))
                    dve.wait_ge(c_xbeta_ready, at(s - 1))
                    dve.wait_ge(c_out.ready, at(s - 2))
                    dve.tensor_tensor(flat(c_acc), flat(c_hg), flat(c_xbeta[r]), ALU.add).then_inc(c_acc_ready, 1)
                    dve.wait_ge(c_acc_ready, at(s - 1))
                    norm_moments(dve, c_out, s - 2, c_acc)
                if there(b):
                    dve.wait_ge(c_exp_ready, at(TILES * b + TILES))
                    dve.reciprocal(c_rden[:, :], c_den[:, :]).then_inc(c_rden_ready, 1)
                    dve.wait_ge(c_rden_ready, at(b + 1))
                    dve.tensor_tensor(c_att[:, :], c_den[:, :], c_rden[:, :], ALU.mult).then_inc(c_att_ready, 1)
                    dve.wait_ge(c_att_ready, at(b + 1))
                    dve.wait_ge(c_z_ready, at(b + 1))
                    dve.wait_ge(c_xb_ready, at(b + 1))
                    dve.wait_ge(c_inner.ready, at(b))
                    for j in range(TILES):
                        i = dve.scalar_tensor_tensor(out=c_h[:, j, :], in0=c_z[q][:, :], scalar=c_att[:, j:j + 1],
                                                     in1=c_xb[:, j, :], op0=ALU.mult, op1=ALU.add)
                    i.then_inc(c_h_ready, 1)
                    dve.wait_ge(c_h_ready, at(b + 1))
                    norm_moments(dve, c_inner, b, c_h)
                if there(s - 2):
                    norm_apply(dve, c_out, s - 2, R[:, s - 2, :, :], c_acc)
            pipelined(dve, step, 2)

        def att_pool(pool):
            def row(x):
                return x[:, :].unsqueeze(1).broadcast_to([P, TILES, P])

            def step(s, r):
                b = s - 1
                if there(s - 2):
                    pool.wait_ge(c_inner.ready, at(s - 1))
                    pool.wait_ge(c_acc_ready, at(s - 2))
                    pool.tensor_tensor(c_hg[:, :, :], c_hhat[:, :, :], row(gamma), ALU.mult).then_inc(c_hg_ready, 1)
                if there(s):
                    pool.wait_ge(c_loaded[r], 8 * (s - r) + 16)
                    pool.wait_ge(c_h_ready, at(s))
                    pool.tensor_tensor(c_xb[:, :, :], c_x[r][:, :, :], row(bfc), ALU.add).then_inc(c_xb_ready, 1)
                    pool.wait_ge(c_acc_ready, at(s - 1))
                    pool.tensor_tensor(c_xbeta[r][:, :, :], c_x[r][:, :, :], row(beta), ALU.add).then_inc(c_xbeta_ready, 1)
                if there(s - 2):
                    norm_rstd(pool, c_out, s - 2)
                if there(b):
                    norm_rstd(pool, c_inner, b)
            pipelined(pool, step, 2)

        f_x = [tok(0), tok(1)]
        f_hi, f_lo = flat(w_hi)[:, 0:T], flat(w_lo)[:, 0:T]
        f_up = [buf(2), buf(3)]
        f_uphi = [[bufr(2 * c + i) for i in range(2)] for c in range(MLP1)]
        f_uplo = [[bufr(8 + 2 * c + i) for i in range(2)] for c in range(MLP1)]
        f_y, f_acc = buf(4), tok(5)
        f_res = [tok(6), tok(7)]

        f_loaded = [sem(f"f_loaded{i}") for i in range(2)]
        f_stored = [sem(f"f_stored{i}") for i in range(2)]
        f_turned = sem("f_turned", "pe")
        f_hi_ready = sem("f_hi_ready", "act")
        f_lo_ready = sem("f_lo_ready", "dve")
        f_up_done = sem("f_up_done", "pe")
        f_gelu_ready = sem("f_gelu_ready", "act")
        f_uphi_ready = sem("f_uphi_ready", "dve")
        f_uplo_ready = sem("f_uplo_ready", "pool")
        f_down_done = sem("f_down_done", "pe")
        f_y_ready = sem("f_y_ready", "act")
        f_y_turned = sem("f_y_turned", "pe")
        f_acc_ready = sem("f_acc_ready", "dve")
        f_out = Norm("f_out")

        def mlp_sync(sp):
            def load(b, r):
                wait_apart(sp, c_out.ready, at(b + 1))
                sp.dma_start(f_x[r][:, :, :], R[:, b, :, :]).then_inc(f_loaded[r], 16)

            def store(b, r):
                wait_apart(sp, f_out.ready, at(b + 1))
                sp.dma_start(out[b].rearrange("(j p) d -> p j d", p=P), f_res[r][:, :, :]).then_inc(f_stored[r], 16)
            for r in range(2):
                sp.wait_ge(c_xbeta_ready, at(B - 1 + r))
                sp.wait_ge(c_xsum_done, at(B - 1 + r))
                load(r, r)
            with sp.Fori(1, B // 2) as i:
                b = 2 * i
                for r in range(2):
                    wait_apart(sp, f_acc_ready, at(b + r - 1))
                    load(b + r, r)
                    store(b + r - 2, r)
            for r in range(2):
                store(B - 2 + r, r)
            for r in range(2):
                sp.wait_ge(f_stored[r], 16 * (B // 2))

        def mlp_pe(pe):
            pe.wait_ge(c_out.ready, at(B))
            def step(s, r):
                if there(s):
                    pe.wait_ge(f_loaded[r], 8 * (s - r) + 16)
                    pe.wait_ge(f_lo_ready, at(s))
                    turn_tiles(pe, bank[0], lambda j: f_x[r][:, j, :]).then_inc(f_turned, 1)
                b = s - 1
                if there(b):
                    for c in range(MLP1):
                        pe.wait_ge(f_uplo_ready, at(MLP1 * b + c + 1))
                        if c == 0:
                            pe.wait_ge(f_y_ready, at(b))
                        m = project(pe, bank[1][:, :], DN1 + c * P, f_uphi[c][1 - r], f_uplo[c][1 - r],
                                    start=c == 0, stop=c == MLP1 - 1)
                    m.then_inc(f_down_done, 1)
                if there(s):
                    pe.wait_ge(f_lo_ready, at(s + 1))
                    for c in range(MLP1):
                        pe.wait_ge(f_gelu_ready, at(MLP1 * (s - 1) + c + 1))
                        project(pe, bank[4 + c][:, :], UP1 + c * P, f_hi[:, :], f_lo[:, :])\
                            .then_inc(f_up_done, 1)
                if there(b):
                    pe.wait_ge(f_y_ready, at(b + 1))
                    pe.wait_ge(f_acc_ready, at(b))
                    turn_tiles(pe, bank[2], lambda j: f_y[:, j * P:(j + 1) * P]).then_inc(f_y_turned, 1)
            pipelined(pe, step, 2)

        def mlp_act(act):
            def step(s, r):
                if there(s):
                    act.wait_ge(f_turned, at(s + 1))
                    act.wait_ge(f_up_done, at(MLP1 * s))
                    act.activation(f_hi[:, :], bank[0][:, :], ACT.Copy).then_inc(f_hi_ready, 1)
                b = s - 1
                if there(b):
                    act.wait_ge(f_down_done, at(b + 1))
                    act.wait_ge(f_y_turned, at(b))
                    act.activation(f_y[:, :], bank[1][:, :], ACT.Identity, bias=f_b2[:, :]).then_inc(f_y_ready, 1)
                if there(s):
                    for c in range(MLP1):
                        act.wait_ge(f_up_done, at(MLP1 * s + c + 1))
                        act.wait_ge(f_uplo_ready, at(MLP1 * s + c - 1))
                        act.activation(f_up[c % 2][:, :], bank[4 + c][:, :], ACT.Gelu, bias=f_b1[:, c:c + 1])\
                           .then_inc(f_gelu_ready, 1)
            pipelined(act, step, 2)

        def mlp_dve(dve):
            def step(s, r):
                if there(s):
                    dve.wait_ge(f_hi_ready, at(s + 1))
                    dve.wait_ge(f_up_done, at(MLP1 * s))
                    dve.tensor_tensor(f_lo[:, :], bank[0][:, :], f_hi[:, :].bitcast(F32), ALU.subtract).then_inc(f_lo_ready, 1)
                    for c in range(MLP1):
                        dve.wait_ge(f_gelu_ready, at(MLP1 * s + c + 1))
                        dve.wait_ge(f_down_done, at(s - 1))
                        dve.tensor_copy(f_uphi[c][r][:, :], f_up[c % 2][:, :]).then_inc(f_uphi_ready, 1)
                b, q = s - 1, 1 - r
                if there(b):
                    dve.wait_ge(f_y_turned, at(b + 1))
                    dve.wait_ge(f_out.ready, at(b))
                    dve.tensor_tensor(flat(f_acc), bank[2][:, :], flat(f_x[q]), ALU.add).then_inc(f_acc_ready, 1)
                    dve.wait_ge(f_acc_ready, at(b + 1))
                    norm_moments(dve, f_out, b, f_acc)
                    if not isinstance(b, int) or b >= 2:
                        dve.wait_ge(f_stored[q], 8 * (b - q))
                    norm_apply(dve, f_out, b, f_res[q], f_acc)
            pipelined(dve, step, 3)

        def mlp_pool(pool):
            def step(s, r):
                if there(s):
                    for c in range(MLP1):
                        pool.wait_ge(f_uphi_ready, at(MLP1 * s + c + 1))
                        pool.wait_ge(f_down_done, at(s - 1))
                        pool.tensor_tensor(f_uplo[c][r][:, :], f_up[c % 2][:, :], f_uphi[c][r][:, :].bitcast(F32), ALU.subtract)\
                            .then_inc(f_uplo_ready, 1)
                if there(s - 1):
                    norm_rstd(pool, f_out, s - 1)
            pipelined(pool, step, 2)

        block = ctx.enter_context(nc.Block())

        @block.sync
        def _(sp):
            with nc.allow_non_contiguous_dma(reason="a few hundred bias values, one to a partition"):
                for dst, src in EARLY:
                    sp.dma_start(dst, src).then_inc(early, 16)
            load = gla_sync(sp)
            for dst, src in LATE:
                sp.dma_start(dst, src).then_inc(late_raw_in, 16)
            with nc.allow_non_contiguous_dma(reason="a few hundred bias values, one to a partition"):
                for dst, src in SMALL:
                    sp.dma_start(dst, src).then_inc(small_in, 16)
            gla_loads(sp, load)
            mid_sync(sp)
            moe_sync(sp)
            att_sync(sp)
            mlp_sync(sp)

        @block.gpsimd
        def _(pool):
            open_semaphores(pool, "pool")
            pool.memset(ident[:, :], 0.0).then_inc(pool_chain, 1)
            pool.memset(ones[:, :], 1.0).then_inc(pool_chain, 1)
            pool.memset(head_mean[:, :], 1.0 / DV).then_inc(pool_chain, 1)
            pool.memset(eps_row[:, :], EPS).then_inc(pool_chain, 1)
            pool.memset(minus_half[:, :], -0.5).then_inc(pool_chain, 1)
            pool.iota(iota_i[:, :], pattern=[[1, E]], base=0, channel_multiplier=0).then_inc(pool_chain, 1)
            pool.wait_ge(pool_chain, at(6))
            pool.affine_select(out=ident[:, :], in_=ident[:, :], compare_op=ALU.not_equal, fill=1.0, base=0,
                               pattern=[[-1, P]], channel_multiplier=1).then_inc(pool_chain, 1)
            hm = head_mean[:, :].rearrange("p (h v) -> p h v", v=DV)
            pool.affine_select(out=hm, in_=hm, compare_op=ALU.is_ge, fill=0.0, base=0,
                               pattern=[[-DV, H], [0, DV]], channel_multiplier=1).then_inc(pool_chain, 1)
            pool.wait_ge(pool_chain, at(8))
            pool.affine_select(out=hm, in_=hm, compare_op=ALU.is_ge, fill=0.0, base=DV - 1,
                               pattern=[[DV, H], [0, DV]], channel_multiplier=-1).then_inc(pool_chain, 1)
            pool.tensor_copy(iota_e[:, :], iota_i[:, :]).then_inc(const_made, 1)
            gla_pool(pool)
            pool.wait_ge(small_in, 16 * len(SMALL))
            pool.wait_ge(g_rms_ready, at(B))
            mid_pool(pool)
            pool.wait_ge(h_out.ready, at(B))
            moe_pool(pool)
            pool.wait_ge(m_out.ready, at(B))
            att_pool(pool)
            pool.wait_ge(c_out.ready, at(B))
            mlp_pool(pool)

        @block.vector
        def _(dve):
            open_semaphores(dve, "dve")
            dve.wait_ge(early, 16 * len(EARLY))

            def by_key(w, k):
                return w.rearrange("d (h k) -> d k h", k=DK)[:, k, :].unsqueeze(2)
            for k in range(DK):
                dve.tensor_scalar(w_raw[:, Q0 + k, :].rearrange("d (h v) -> d h v", v=DV),
                                  by_key(wq_raw[:, :], k).broadcast_to([P, H, DV]), float(DK) ** -0.5, None, ALU.mult)
                dve.tensor_copy(w_raw[:, K0 + k, :].rearrange("d (h v) -> d h v", v=DV),
                                by_key(wk_raw[:, :], k).broadcast_to([P, H, DV]))
            dve.tensor_scalar(wo_scaled[:, :], wo_raw[:, :], rms_col[:, :], 0.5, ALU.mult, ALU.mult).then_inc(prep_dve, 1)
            dve.wait_ge(pool_chain, at(9))
            for k in range(DK):
                dve.tensor_copy(spread_k[:, k, :].rearrange("p (h v) -> p h v", v=DV),
                                by_key(ident[0:HK, 0:HK], k).broadcast_to([HK, H, DV]))
            dve.tensor_copy(pick_e[:, :, :], ident[0:E, 0:E].unsqueeze(2).broadcast_to([E, E, P])).then_inc(prep_dve, 1)
            dve.wait_ge(prep_pe, at(1))
            dve.tensor_copy(gkw1_t[:, :], bank[0][0:LOWR, 0:P]).then_inc(prep_dve, 1)
            dve.wait_ge(prep_pe, at(2))
            for i in range(P // HK):
                g = dve.tensor_copy(w_raw[:, GK, i * HK:(i + 1) * HK], bank[1][:, 0:HK])
            g.then_inc(prep_dve, 1)
            dve.wait_ge(prep_dve, at(4))
            dve.tensor_scalar(flat(w_fold), flat(w_raw), ln_w[:, :], None, ALU.mult).then_inc(prep_dve, 1)
            dve.wait_ge(prep_dve, at(5))
            dve.tensor_copy(wo_hi[:, :], wo_scaled[:, :])
            dve.tensor_copy(flat(w_hi), flat(w_fold)).then_inc(prep_dve, 1)
            dve.wait_ge(prep_dve, at(6))
            dve.tensor_tensor(wo_lo[:, :], wo_scaled[:, :], wo_hi[:, :].bitcast(F32), ALU.subtract)
            dve.tensor_tensor(flat(w_lo), flat(w_fold), flat(w_hi).bitcast(F32), ALU.subtract).then_inc(prep_dve, 1)
            dve.wait_ge(prep_pe, at(3))
            dve.tensor_copy(w_bias[:, V:UP0], bank[2][:, V:UP0])
            dve.tensor_tensor(w_bias[0:HK, GK:GK + 1], bank[2][0:HK, GK:GK + 1], gk_b[:, :], ALU.add)
            dve.tensor_tensor(w_bias[:, UP0:NB0], bank[2][:, UP0:NB0], b1_col[:, :], ALU.add).then_inc(prep_dve, 1)
            gla_dve(dve)
            dve.wait_ge(g_rms_ready, at(B))
            dve.wait_ge(small_in, 16 * len(SMALL))
            dve.wait_ge(prep_pe, at(4))
            dve.tensor_copy(r_hi[:, :], bank[3][:, 0:E]).then_inc(prep_dve, 1)
            dve.wait_ge(prep_dve, at(9))
            dve.tensor_tensor(r_lo[:, :], bank[3][:, 0:E], r_hi[:, :].bitcast(F32), ALU.subtract)
            dve.tensor_copy(qk_hi[:, :], bank[4][:, 0:P]).then_inc(prep_dve, 1)
            dve.wait_ge(prep_dve, at(10))
            dve.tensor_tensor(qk_lo[:, :], bank[4][:, 0:P], qk_hi[:, :].bitcast(F32), ALU.subtract)
            dve.tensor_copy(fc_t[:, :], bank[5][:, 0:P]).then_inc(prep_dve, 1)
            dve.wait_ge(prep_pe, at(5))
            dve.tensor_copy(vfc[:, :], bank[6][:, 0:P]).then_inc(prep_dve, 1)
            mid_dve(dve)
            moe_dve(dve)
            att_dve(dve)
            mlp_dve(dve)

        @block.scalar
        def _(act):
            open_semaphores(act, "act")
            act.preload_act_table_set("natural_log_exp_and_others")
            act.wait_ge(prep_dve, at(8))
            act.wait_ge(pool_chain, at(9))
            gla_act(act)
            act.preload_act_table_set("gelu_and_others")
            act.wait_ge(g_rms_ready, at(B))
            act.wait_ge(small_in, 16 * len(SMALL))
            mid_act(act)
            act.preload_act_table_set("silu_and_others")
            act.wait_ge(h_out.ready, at(B))
            moe_act(act)
            act.preload_act_table_set("exp_and_others")
            act.wait_ge(m_out.ready, at(B))
            att_act(act)
            act.preload_act_table_set("gelu_and_others")
            act.wait_ge(c_out.ready, at(B))
            mlp_act(act)

        @block.tensor
        def _(pe):
            open_semaphores(pe, "pe")
            pe.wait_ge(early, 16 * len(EARLY))
            pe.wait_ge(pool_chain, at(9))
            pe.transpose(bank[0][0:LOWR, 0:P], gkw1[:, :], ident[:, :]).then_inc(prep_pe, 1)
            pe.wait_ge(prep_dve, at(3))
            pe.matmul(bank[1][:, 0:HK], gkw1_t[:, :], gkw2[:, :], start=True, stop=True).then_inc(prep_pe, 1)
            pe.wait_ge(prep_dve, at(4))
            for n in range(NB0):
                m = pe.matmul(bank[2][:, n:n + 1], w_raw[:, n, :], ln_b[:, :], start=True, stop=True)
            m.then_inc(prep_pe, 1)
            pe.wait_ge(prep_dve, at(8))
            gla_pe(pe)
            pe.wait_ge(g_rms_ready, at(B))
            pe.wait_ge(small_in, 16 * len(SMALL))
            pe.transpose(bank[3][:, 0:E], r_raw[:, :], ident[0:E, 0:E])
            pe.matmul(bank[4][:, 0:P], qkv_raw[:, 0, :], qkv_raw[:, 1, :], start=True, stop=True)
            pe.transpose(bank[5][:, 0:P], fc_raw[:, :], ident[:, :]).then_inc(prep_pe, 1)
            pe.wait_ge(prep_dve, at(11))
            pe.matmul(bank[6][:, 0:P], qkv_raw[:, 2, :], fc_t[:, :], start=True, stop=True).then_inc(prep_pe, 1)
            pe.wait_ge(prep_dve, at(12))
            pe.wait_ge(late_lo, at(2 * B))
            mid_pe(pe)
            moe_pe(pe)
            att_pe(pe)
            mlp_pe(pe)


_INS = ['L0_attn_x', 'L0_attn_ln_w', 'L0_attn_ln_b', 'L0_attn_Wq', 'L0_attn_Wk', 'L0_attn_Wv', 'L0_attn_gk_w1',
        'L0_attn_gk_w2', 'L0_attn_gk_b2', 'L0_attn_Wg', 'L0_attn_rms_w', 'L0_attn_Wo', 'L0_attn_W1', 'L0_attn_b1',
        'L0_attn_W2', 'L0_attn_b2', 'L0_ffn_router_w', 'L0_ffn_experts_bias', 'L0_ffn_w1', 'L0_ffn_w3', 'L0_ffn_w2',
        'L0_ffn_sw1', 'L0_ffn_sw3', 'L0_ffn_sw2', 'L1_attn_w_qkv', 'L1_attn_w_fc', 'L1_attn_b_fc', 'L1_attn_gamma',
        'L1_attn_beta', 'L1_ffn_w1', 'L1_ffn_b1', 'L1_ffn_w2', 'L1_ffn_b2']


def kernel(**inputs):
    import numpy as _np
    import concourse.bacc as _bacc
    from concourse import mybir as _mybir
    from concourse.bass_utils import run_bass_kernel_spmd as _run

    nc = _bacc.Bacc("TRN2", target_bir_lowering=False, num_devices=1)
    arrays, args = {}, {}
    for name in _INS:
        x = _np.ascontiguousarray(inputs[name])
        arrays[f"in_{name}_dram"] = x
        args[name] = nc.dram_tensor(f"in_{name}_dram", x.shape, _mybir.dt.from_np(x.dtype), kind="ExternalInput").ap()
    out = nc.dram_tensor("out_0_dram", inputs["L0_attn_x"].shape, _mybir.dt.float32, kind="ExternalOutput").ap()
    build(nc, args, out)
    r = _run(nc, [arrays], core_ids=[0])
    return r.results[0]["out_0_dram"]
```

```python
from contextlib import ExitStack

import concourse.bass as bass
from concourse import mybir

F32 = mybir.dt.float32
F32R = mybir.dt.float32r
I32 = mybir.dt.int32
U32 = mybir.dt.uint32
ALU = mybir.AluOpType
ACT = mybir.ActivationFunctionType
AX = mybir.AxisListType

P = 128
HEAD = 4
EPS = 1e-5
GATE_NORM = 16.0


def at(n):
    return HEAD + (max(n, 0) if isinstance(n, int) else n)


def build(nc, a, out):
    B, T, D = a["L0_attn_x"].shape
    assert D == P and B % 2 == 0
    TILES = T // P
    HK = a["L0_attn_Wq"].shape[1]
    DV = a["L0_attn_rms_w"].shape[0]
    H = D // DV
    DK = HK // H
    E, _, HID = a["L0_ffn_w1"].shape
    HALVES = HID // P
    UNITS = (E + 1) * HALVES
    MLP0 = a["L0_attn_W1"].shape[1] // P
    MLP1 = a["L1_ffn_w1"].shape[1] // P
    LOWR = a["L0_attn_gk_w1"].shape[1]
    SCALE = float(D) ** -0.5

    with ExitStack() as ctx:
        def sb(name, shape, dt=F32):
            return ctx.enter_context(nc.sbuf_tensor(name, shape, dt))

        starts = {"pe": [], "act": [], "dve": [], "pool": []}

        def sem(name, engine=None):
            s = ctx.enter_context(nc.semaphore(name))
            if engine:
                starts[engine].append(s)
            return s

        apart = ctx.enter_context(nc.semaphore("apart"))

        def wait_apart(eng, s, value):
            eng.wait_ge(s, value)
            eng.sem_inc(apart, 1)

        def open_semaphores(eng, name):
            for s in starts[name]:
                eng.sem_inc(s, HEAD)

        def pipelined(eng, step, lags):
            for s in range(lags):
                step(s, s % 2)
            turns = (B - lags) // 2
            with eng.Fori(0, turns) as i:
                s = 2 * i + lags
                step(s, lags % 2)
                step(s + 1, (lags + 1) % 2)
            for s in range(lags + 2 * turns, B + lags):
                step(s, s % 2)

        def there(b):
            return not isinstance(b, int) or 0 <= b < B

        bank = [ctx.enter_context(nc.psum_tensor(f"bank{i}", [P, 512], F32)) for i in range(8)]

        ident = sb("ident", [P, P])
        ones = sb("ones", [P, P])
        head_mean = sb("head_mean", [P, P])
        eps_row = sb("eps_row", [P, TILES])
        minus_half = sb("minus_half", [P, TILES])
        iota_i = sb("iota_i", [P, E], I32)
        iota_e = sb("iota_e", [P, E])
        spread_k = sb("spread_k", [P, DK, P], F32R)
        LO_ROW = 32
        pick_raw = sb("pick_raw", [LO_ROW + E, E])
        pick_e = sb("pick_e", [LO_ROW + E, E, P], F32R)

        ln_w = sb("ln_w", [P, 1])
        ln_b = sb("ln_b", [P, 1])
        rms_col = sb("rms_col", [P, 1])
        gk_b = sb("gk_b", [P, 1])
        b1_col = sb("b1_col", [P, MLP0])
        b2_col = sb("b2_col", [P, 1])
        ebias = sb("ebias", [P, E])
        f_b1 = sb("f_b1", [P, MLP1])
        f_b2 = sb("f_b2", [P, 1])
        bfc = sb("bfc", [P, P])
        gamma = sb("gamma", [P, P])
        beta = sb("beta", [P, P])

        GK, V, G, K0 = 0, 1, 2, 3
        Q0 = K0 + DK
        UP0 = Q0 + DK
        NB0 = UP0 + MLP0
        w_hi = sb("w_hi", [P, NB0, P], F32R)
        w_lo = sb("w_lo", [P, NB0, P], F32R)
        w_bias = sb("w_bias", [P, NB0])
        wo_scaled = sb("wo_scaled", [P, P])
        wo_hi = sb("wo_hi", [P, P], F32R)
        wo_lo = sb("wo_lo", [P, P], F32R)
        r_raw = sb("r_raw", [E, P])
        r_hi = sb("r_hi", [P, E], F32R)
        r_lo = sb("r_lo", [P, E], F32R)

        qkv_raw = sb("qkv_raw", [P, 3, P])
        fc_raw = sb("fc_raw", [P, P])
        fc_t = sb("fc_t", [P, P])
        qk_hi = sb("qk_hi", [P, P], F32R)
        qk_lo = sb("qk_lo", [P, P], F32R)
        vfc = sb("vfc", [P, P])


        R = sb("R", [P, B, TILES, P])
        gate = sb("gate", [P, B, T])
        rms_o = R[:, :, :, :].rearrange("p b j d -> p b (j d)")
        work = sb("work", [P, 24, T])
        workr = sb("workr", [P, 16, T], F32R)

        def buf(i):
            return work[:, i, :]

        def tok(i):
            return work[:, i, :].rearrange("p (j d) -> p j d", d=P)

        def bufr(i):
            return workr[:, i, :]
        wq_raw, wk_raw, wo_raw = buf(8)[:, 0:HK], buf(8)[:, HK:2 * HK], buf(9)[:, 0:P]
        gkw1, gkw1_t, gkw2 = buf(10)[:, 0:LOWR], work[0:LOWR, 11, 0:P], work[0:LOWR, 11, P:P + HK]
        w_raw = work[:, 12:16, :].rearrange("p n t -> p (n t)")[:, 0:NB0 * P].rearrange("p (n c) -> p n c", c=P)
        w_fold = work[:, 16:20, :].rearrange("p n t -> p (n t)")[:, 0:NB0 * P].rearrange("p (n c) -> p n c", c=P)

        EXPERTS = (E + 1) * HID
        UP1, DN1 = 3 * EXPERTS, 3 * EXPERTS + MLP1 * P
        DN0 = DN1 + MLP1 * P
        assert DN0 + MLP0 * P == 2 * B * T
        w_late_hi = sb("w_late_hi", [P, 2 * B, T], F32R)
        w_late_lo = sb("w_late_lo", [P, 2 * B, T], F32R)
        late_hi_row = w_late_hi[:, :, :].rearrange("p n t -> p (n t)")
        late_lo_row = w_late_lo[:, :, :].rearrange("p n t -> p (n t)")

        def late_raw(start, n):
            assert start // (B * T) == (start + n - 1) // (B * T)
            half = gate[:, :, :].rearrange("p b t -> p (b t)") if start < B * T else rms_o.rearrange("p b t -> p (b t)")
            return half[:, start % (B * T):start % (B * T) + n]

        def late(start, n=P):
            return late_hi_row[:, start:start + n], late_lo_row[:, start:start + n]

        early = sem("early_weights")
        late_raw_in = sem("late_raw_in")
        small_in = sem("small_in")
        const_made = sem("const_made", "pool")
        pool_chain = sem("pool_chain", "pool")
        prep_pe = sem("prep_pe", "pe")
        prep_dve = sem("prep_dve", "dve")
        prep_act = sem("prep_act", "act")
        late_hi = sem("late_hi", "act")
        late_lo = sem("late_lo", "pool")

        EARLY = [
            (ln_w[:, :], a["L0_attn_ln_w"].unsqueeze(1)),
            (ln_b[:, :], a["L0_attn_ln_b"].unsqueeze(1)),
            (gkw1[:, :], a["L0_attn_gk_w1"]),
            (gkw2[:, :], a["L0_attn_gk_w2"]),
            (wq_raw[:, :], a["L0_attn_Wq"]),
            (wk_raw[:, :], a["L0_attn_Wk"]),
            (w_raw[:, V, :], a["L0_attn_Wv"]),
            (w_raw[:, G, :], a["L0_attn_Wg"]),
            (w_raw[:, UP0:NB0, :], a["L0_attn_W1"].rearrange("d (c h) -> d c h", c=MLP0)),
            (gk_b[0:HK, :], a["L0_attn_gk_b2"].unsqueeze(1)),
            (gk_b[HK:2 * HK, :], a["L0_attn_gk_b2"].unsqueeze(1)),
            (b1_col[:, :], a["L0_attn_b1"].rearrange("(c p) -> p c", p=P)),
            (b2_col[:, :], a["L0_attn_b2"].unsqueeze(1)),
            (rms_col[:, :], a["L0_attn_rms_w"].unsqueeze(1).partition_broadcast(H)),
            (wo_raw[:, :], a["L0_attn_Wo"]),
        ]
        def experts(m, e, n):
            return late_raw(m * EXPERTS + e * HID, n * HID)
        split = B * T // HID - EXPERTS // HID
        LATE = [
            (experts(0, 0, 1), a["L0_ffn_sw1"][0]),
            (experts(0, 1, E).rearrange("d (e h) -> d e h", e=E), a["L0_ffn_w1"].rearrange("e d h -> d e h")),
            (experts(1, 0, 1), a["L0_ffn_sw3"][0]),
            (experts(1, 1, split - 1).rearrange("d (e h) -> d e h", h=HID),
             a["L0_ffn_w3"][0:split - 1].rearrange("e d h -> d e h")),
            (experts(1, split, E + 1 - split).rearrange("d (e h) -> d e h", h=HID),
             a["L0_ffn_w3"][split - 1:E].rearrange("e d h -> d e h")),
            (experts(2, 0, 1).rearrange("h (c d) -> h c d", c=HALVES),
             a["L0_ffn_sw2"][0].rearrange("(c h) d -> h c d", c=HALVES)),
            (experts(2, 1, E).rearrange("h (n d) -> h n d", d=P),
             a["L0_ffn_w2"].rearrange("e (c h) d -> h (e c) d", c=HALVES)),
            (late_raw(UP1, MLP1 * P), a["L1_ffn_w1"]),
            (late_raw(DN1, MLP1 * P).rearrange("h (c d) -> h c d", c=MLP1),
             a["L1_ffn_w2"].rearrange("(c h) d -> h c d", c=MLP1)),
            (late_raw(DN0, MLP0 * P).rearrange("h (c d) -> h c d", c=MLP0),
             a["L0_attn_W2"].rearrange("(c h) d -> h c d", c=MLP0)),
        ]
        SMALL = [
            (r_raw[:, :], a["L0_ffn_router_w"]),
            (ebias[:, :], a["L0_ffn_experts_bias"].partition_broadcast(P)),
            (qkv_raw[:, :, :], a["L1_attn_w_qkv"].rearrange("(c e) d -> e c d", c=3)),
            (fc_raw[:, :], a["L1_attn_w_fc"]),
            (bfc[:, :], a["L1_attn_b_fc"].partition_broadcast(P)),
            (gamma[:, :], a["L1_attn_gamma"].partition_broadcast(P)),
            (beta[:, :], a["L1_attn_beta"].partition_broadcast(P)),
            (f_b1[:, :], a["L1_ffn_b1"].rearrange("(c p) -> p c", p=P)),
            (f_b2[:, :], a["L1_ffn_b2"].unsqueeze(1)),
        ]

        def flat(t):
            return t[:, :, :].rearrange("p a b -> p (a b)")

        def project(pe, o, start_col, x_hi, x_lo, start=True, stop=True):
            hi, lo = late(start_col)
            return mm3(pe, o, hi, lo, x_hi, x_lo, start=start, stop=stop)

        def mm3(pe, o, weight_hi, weight_lo, x_hi, x_lo, start=True, stop=True):
            pe.matmul(o, weight_hi, x_hi, start=start, stop=False)
            pe.matmul(o, weight_hi, x_lo, start=False, stop=False)
            return pe.matmul(o, weight_lo, x_hi, start=False, stop=stop)

        def turn_tiles(pe, o, x):
            for j in range(TILES):
                m = pe.transpose(o[:, j * P:(j + 1) * P], x(j), ident[:, :])
            return m

        class Norm:
            def __init__(self, name):
                self.stats = sb(f"{name}_stats", [P, TILES, 6])
                self.moments = sb(f"{name}_moments", [P, TILES, 2])
                self.var_eps = sb(f"{name}_var_eps", [P, TILES])
                self.rstd = sb(f"{name}_rstd", [P, TILES])
                self.moments_ready = sem(f"{name}_moments_ready", "dve")
                self.rstd_ready = sem(f"{name}_rstd_ready", "pool")
                self.ready = sem(f"{name}_ready", "dve")

        def norm_moments(dve, n, b, x):
            for j in range(TILES):
                dve.bn_stats(n.stats[:, j, :], x[:, j, :]).then_inc(n.moments_ready, 1)
            wait_apart(dve, n.moments_ready, at((TILES + 1) * b + TILES))
            for j in range(TILES):
                i = dve.bn_aggr(n.moments[:, j, :], n.stats[:, j, :])
            i.then_inc(n.moments_ready, 1)

        def norm_rstd(pool, n, b):
            pool.wait_ge(n.moments_ready, at((TILES + 1) * (b + 1)))
            pool.tensor_tensor(n.var_eps[:, :], n.moments[:, :, 1], eps_row[:, :], ALU.add).then_inc(n.rstd_ready, 1)
            pool.wait_ge(n.rstd_ready, at(2 * b + 1))
            pool.tensor_tensor(n.rstd[:, :], n.var_eps[:, :], minus_half[:, :], ALU.pow).then_inc(n.rstd_ready, 1)

        def norm_apply(dve, n, b, o, x):
            dve.wait_ge(n.rstd_ready, at(2 * b + 2))
            for j in range(TILES):
                i = dve.tensor_scalar(o[:, j, :], x[:, j, :], n.moments[:, j, 0:1], n.rstd[:, j:j + 1],
                                      ALU.subtract, ALU.mult)
            i.then_inc(n.ready, 1)

        g_x = [tok(0), tok(1)]
        g_xhat = [tok(2), tok(3)]
        g_hhi, g_hlo = [bufr(0), bufr(1)], [bufr(2), bufr(3)]
        g_z, g_log, g_ls = buf(4), buf(5), buf(6)
        assert 2 * HK == P
        g_parts = bufr(4)
        g_v = buf(7)
        g_dec = [buf(8 + k) for k in range(DK)]
        g_kv = [buf(12 + k) for k in range(DK)]
        g_S = [buf(16 + k) for k in range(DK)]
        g_o = [buf(20), buf(21)]
        g_sq = buf(22)
        g_r = buf(23)

        g_loaded = [sem(f"g_loaded{i}") for i in range(2)]
        g_norm = Norm("g_norm")
        g_turned = sem("g_turned", "pe")
        g_hi_ready = sem("g_hi_ready", "act")
        g_lo_ready = sem("g_lo_ready", "dve")
        g_gk_done = sem("g_gk_done", "pe")
        g_v_done = sem("g_v_done", "pe")
        g_g_done = sem("g_g_done", "pe")
        g_k_done = sem("g_k_done", "pe")
        g_dec_done = sem("g_dec_done", "pe")
        g_q_done = sem("g_q_done", "pe")
        g_ms_done = sem("g_ms_done", "pe")
        g_z_ready = sem("g_z_ready", "act")
        g_abs_ready = sem("g_abs_ready", "act")
        g_exp_ready = sem("g_exp_ready", "act")
        g_log_ready = sem("g_log_ready", "act")
        g_v_ready = sem("g_v_ready", "act")
        g_gate_ready = sem("g_gate_ready", "act")
        g_dec_ready = sem("g_dec_ready", "act")
        g_sq_ready = sem("g_sq_ready", "act")
        g_ln_ready = sem("g_ln_ready", "act")
        g_r_ready = sem("g_r_ready", "act")
        g_ls_ready = sem("g_ls_ready", "dve")
        g_lshi_ready = sem("g_lshi_ready", "dve")
        g_lslo_ready = sem("g_lslo_ready", "pool")
        g_kv_ready = sem("g_kv_ready", "dve")
        g_S_ready = sem("g_S_ready", "dve")
        g_qS_ready = sem("g_qS_ready", "dve")
        g_sum_ready = sem("g_sum_ready", "pool")
        g_o_ready = sem("g_o_ready", "pool")
        g_rms_ready = sem("g_rms_ready", "pool")

        Q_BANK = [2, 3, 1, 0]

        def gla_sync(sp):
            def load(b, r):
                sp.dma_start(g_x[r][:, :, :], a["L0_attn_x"][b].rearrange("(j p) d -> p j d", p=P)).then_inc(g_loaded[r], 16)
            load(0, 0)
            load(1, 1)
            return load

        def gla_loads(sp, load):
            with sp.Fori(1, B // 2) as i:
                b = 2 * i
                for r in range(2):
                    sp.wait_ge(g_norm.ready, at(b + r - 1))
                    load(b + r, r)

        def gla_pe(pe):
            def step(s, r):
                t, b, e = s - 1, s - 2, s - 3
                if there(b):
                    hhi, hlo = g_hhi[r][:, :], g_hlo[r][:, :]

                    def apply(block, o):
                        return mm3(pe, o[:, :], w_hi[:, block, :], w_lo[:, block, :], hhi, hlo)
                    pe.wait_ge(g_lo_ready, at(b + 1))
                    pe.wait_ge(g_qS_ready, at(DK * (b - 1) + 1))
                    apply(GK, bank[2]).then_inc(g_gk_done, 1)
                    pe.wait_ge(g_qS_ready, at(DK * (b - 1) + 3))
                    apply(V, bank[1]).then_inc(g_v_done, 1)
                    apply(G, bank[3]).then_inc(g_g_done, 1)
                    for k in range(DK):
                        pe.wait_ge(g_dec_ready, at(DK * (b - 1) + k + 1))
                        apply(K0 + k, bank[4 + k]).then_inc(g_k_done, 1)
                if there(t):
                    pe.wait_ge(g_norm.ready, at(t + 1))
                    pe.wait_ge(g_qS_ready, at(DK * b) if there(b) else at(0))
                    turn_tiles(pe, bank[0], lambda j: g_xhat[1 - r][:, j, :]).then_inc(g_turned, 1)

                def mean_square():
                    pe.wait_ge(g_sq_ready, at(e + 1))
                    if there(b):
                        pe.wait_ge(g_v_ready, at(b + 1))
                    else:
                        pe.wait_ge(g_qS_ready, at(DK * B))
                    pe.matmul(bank[1][:, :], head_mean[:, :], g_sq[:, :], start=True, stop=True).then_inc(g_ms_done, 1)
                if there(b):
                    pe.wait_ge(g_lslo_ready, at(b + 1))
                    for k in range(DK):
                        pe.wait_ge(g_kv_ready, at(DK * b + k + 1))
                        pe.matmul(bank[4 + k][:, :], spread_k[:, k, :], g_parts[:, :], start=True, stop=True)\
                          .then_inc(g_dec_done, 1)
                        if k == 0:
                            pe.wait_ge(g_z_ready, at(b + 1))
                        elif k == 1:
                            pe.wait_ge(g_gate_ready, at(b + 1))
                        elif k == 2:
                            pe.wait_ge(g_v_ready, at(b + 1))
                            pe.wait_ge(g_ln_ready, at(e + 1))
                        elif there(t):
                            pe.wait_ge(g_lo_ready, at(t + 1))
                        apply(Q0 + k, bank[Q_BANK[k]]).then_inc(g_q_done, 1)
                        if k == 0 and there(e):
                            mean_square()
                elif there(e):
                    mean_square()
            pipelined(pe, step, 3)

        def gla_act(act):
            def step(s, r):
                t, b, e = s - 1, s - 2, s - 3
                if there(b):
                    act.wait_ge(g_gk_done, at(b + 1))
                    act.wait_ge(g_ls_ready, at(b))
                    act.activation(g_log[:, :], bank[2][:, :], ACT.Abs, bias=w_bias[:, GK:GK + 1]).then_inc(g_abs_ready, 1)
                    act.wait_ge(g_abs_ready, at(b + 1))
                    act.activation(g_log[:, :], g_log[:, :], ACT.Exp, scale=-1.0).then_inc(g_exp_ready, 1)
                    act.activation(g_z[:, :], bank[2][:, :], ACT.Identity, bias=w_bias[:, GK:GK + 1]).then_inc(g_z_ready, 1)
                    act.wait_ge(g_exp_ready, at(b + 1))
                    act.activation(g_log[:, :], g_log[:, :], ACT.Ln, bias=1.0).then_inc(g_log_ready, 1)
                    act.wait_ge(g_v_done, at(b + 1))
                    act.wait_ge(g_kv_ready, at(DK * b))
                    act.activation(g_v[:, :], bank[1][:, :], ACT.Identity, bias=w_bias[:, V:V + 1]).then_inc(g_v_ready, 1)
                    act.wait_ge(g_g_done, at(b + 1))
                    wait_apart(act, late_lo, at(2 * b + 2))
                    act.activation(gate[:, b, :], bank[3][:, :], ACT.Identity, bias=w_bias[:, G:G + 1]).then_inc(g_gate_ready, 1)
                if there(s):
                    act.wait_ge(late_raw_in, 16 * len(LATE))
                    for half, raw in enumerate((gate[:, s, :], rms_o[:, s, :])):
                        act.activation(w_late_hi[:, half * B + s, :], raw, ACT.Copy).then_inc(late_hi, 1)
                if there(t):
                    act.wait_ge(g_turned, at(t + 1))
                    act.wait_ge(g_q_done, at(DK * (t - 1)))
                    act.activation(g_hhi[1 - r][:, :], bank[0][:, :], ACT.Copy).then_inc(g_hi_ready, 1)

                def decay(k):
                    act.wait_ge(g_dec_done, at(DK * b + k + 1))
                    act.wait_ge(g_S_ready, at(DK * (b - 1) + k + 1))
                    act.activation(g_dec[k][:, :], bank[4 + k][:, :], ACT.Exp, scale=1.0 / GATE_NORM)\
                       .then_inc(g_dec_ready, 1)
                if there(e):
                    act.wait_ge(g_o_ready, at(e + 1))
                    act.wait_ge(g_ms_done, at(e))
                    act.activation(g_sq[:, :], g_o[1 - r][:, :], ACT.Square).then_inc(g_sq_ready, 1)
                if there(b):
                    decay(0)
                if there(e):
                    act.wait_ge(g_ms_done, at(e + 1))
                    act.wait_ge(g_rms_ready, at(e))
                    act.activation(g_r[:, :], bank[1][:, :], ACT.Ln, bias=eps_row[:, 0:1]).then_inc(g_ln_ready, 1)
                if there(b):
                    decay(1)
                if there(e):
                    act.wait_ge(g_ln_ready, at(e + 1))
                    act.activation(g_r[:, :], g_r[:, :], ACT.Exp, scale=-0.5).then_inc(g_r_ready, 1)
                if there(b):
                    decay(2)
                    decay(3)
            pipelined(act, step, 3)

        def gla_dve(dve):
            def step(s, r):
                t, b = s - 1, s - 2
                if there(t):
                    dve.wait_ge(g_turned, at(t - 1))
                    norm_apply(dve, g_norm, t, g_xhat[1 - r], g_x[1 - r])
                if there(b):
                    dve.wait_ge(g_z_ready, at(b + 1))
                    dve.wait_ge(g_log_ready, at(b + 1))
                    dve.wait_ge(g_lslo_ready, at(b))
                    dve.scalar_tensor_tensor(out=g_ls[:, :], in0=g_z[:, :], scalar=0.0, in1=g_log[:, :],
                                             op0=ALU.min, op1=ALU.subtract).then_inc(g_ls_ready, 1)
                    dve.wait_ge(g_ls_ready, at(b + 1))
                    dve.wait_ge(g_dec_done, at(DK * b))
                    dve.tensor_copy(g_parts[:, :], g_ls[:, :]).then_inc(g_lshi_ready, 1)
                    dve.wait_ge(g_v_ready, at(b + 1))
                    for k in range(DK):
                        dve.wait_ge(g_k_done, at(DK * b + k + 1))
                        dve.scalar_tensor_tensor(out=g_kv[k][:, :], in0=bank[4 + k][:, :], scalar=w_bias[:, K0 + k:K0 + k + 1],
                                                 in1=g_v[:, :], op0=ALU.add, op1=ALU.mult).then_inc(g_kv_ready, 1)
                if there(t):
                    dve.wait_ge(g_hi_ready, at(t + 1))
                    dve.wait_ge(g_q_done, at(DK * (t - 1)))
                    dve.tensor_tensor(g_hlo[1 - r][:, :], bank[0][:, :], g_hhi[1 - r][:, :].bitcast(F32), ALU.subtract)\
                       .then_inc(g_lo_ready, 1)
                for k in range(DK):
                    if there(b):
                        dve.wait_ge(g_dec_ready, at(DK * b + k + 1))
                        dve.wait_ge(g_kv_ready, at(DK * b + k + 1))
                        dve.wait_ge(g_o_ready, at(b))
                        dve.tensor_tensor_scan(g_S[k][:, :], g_dec[k][:, :], g_kv[k][:, :], 0.0, ALU.mult, ALU.add)\
                           .then_inc(g_S_ready, 1)
                        dve.wait_ge(g_S_ready, at(DK * b + k + 1))
                        dve.wait_ge(g_q_done, at(DK * b + k + 1))
                        dve.scalar_tensor_tensor(out=g_S[k][:, :], in0=bank[Q_BANK[k]][:, :],
                                                 scalar=w_bias[:, Q0 + k:Q0 + k + 1], in1=g_S[k][:, :],
                                                 op0=ALU.add, op1=ALU.mult).then_inc(g_qS_ready, 1)
                    if k == 1 and there(s):
                        dve.wait_ge(g_loaded[r], 8 * (s - r) + 16)
                        norm_moments(dve, g_norm, s, g_x[r])
            pipelined(dve, step, 3)

        def gla_pool(pool):
            def step(s, r):
                b, e = s - 2, s - 3
                if there(b):
                    pool.wait_ge(g_lshi_ready, at(b + 1))
                    pool.wait_ge(g_dec_done, at(DK * b))
                    pool.wait_ge(g_o_ready, at(b))
                    low = g_parts[HK:2 * HK, :]
                    pool.tensor_tensor(low, g_ls[HK:2 * HK, :], low.bitcast(F32), ALU.subtract).then_inc(g_lslo_ready, 1)
                    wait_apart(pool, g_lslo_ready, at(b + 1))
                if there(s):
                    for half, raw in enumerate((gate[:, s, :], rms_o[:, s, :])):
                        pool.wait_ge(late_hi, at(2 * s + half + 1))
                        pool.tensor_tensor(w_late_lo[:, half * B + s, :], raw, w_late_hi[:, half * B + s, :].bitcast(F32),
                                           ALU.subtract).then_inc(late_lo, 1)

                def pair(h):
                    pool.wait_ge(g_qS_ready, at(DK * b + 2 * h + 2))
                    pool.tensor_tensor(g_S[2 * h][:, :], g_S[2 * h][:, :], g_S[2 * h + 1][:, :], ALU.add)\
                        .then_inc(g_sum_ready, 1)
                if there(b):
                    pair(0)
                if there(e):
                    pool.wait_ge(g_r_ready, at(e + 1))
                    pool.tensor_tensor(rms_o[:, e, :], g_o[1 - r][:, :], g_r[:, :], ALU.mult).then_inc(g_rms_ready, 1)
                if there(s):
                    norm_rstd(pool, g_norm, s)
                if there(b):
                    pair(1)
                    pool.wait_ge(g_sum_ready, at(2 * b + 2))
                    pool.wait_ge(g_rms_ready, at(b - 1))
                    pool.tensor_tensor(g_o[r][:, :], g_S[0][:, :], g_S[2][:, :], ALU.add).then_inc(g_o_ready, 1)
            pipelined(pool, step, 3)

        h_x = [tok(0), tok(1)]
        h_tanh, h_gs, h_og = buf(2), buf(3), buf(4)
        h_oghi, h_oglo = [bufr(0), bufr(1)], [bufr(2), bufr(3)]
        h_y2 = buf(6)
        h_x1, h_xhat, h_acc = tok(7), tok(8), tok(9)
        h_hi, h_lo = bufr(4), bufr(5)
        h_up = [buf(10 + c) for c in range(MLP0)]
        h_uphi = [[bufr(6 + 2 * c + i) for i in range(2)] for c in range(MLP0)]
        h_uplo = [[bufr(10 + 2 * c + i) for i in range(2)] for c in range(MLP0)]

        h_loaded = [sem(f"h_loaded{i}") for i in range(2)]
        h_tanh_ready = sem("h_tanh_ready", "act")
        h_gs_ready = sem("h_gs_ready", "dve")
        h_og_ready = sem("h_og_ready", "dve")
        h_oghi_ready = sem("h_oghi_ready", "act")
        h_oglo_ready = sem("h_oglo_ready", "pool")
        h_wo_done = sem("h_wo_done", "pe")
        h_x1_ready = sem("h_x1_ready", "dve")
        h_xx_ready = sem("h_xx_ready", "pool")
        h_norm = Norm("h_norm")
        h_turned = sem("h_turned", "pe")
        h_hi_ready = sem("h_hi_ready", "act")
        h_lo_ready = sem("h_lo_ready", "dve")
        h_up_done = sem("h_up_done", "pe")
        h_gelu_ready = sem("h_gelu_ready", "act")
        h_uphi_ready = sem("h_uphi_ready", "dve")
        h_uplo_ready = sem("h_uplo_ready", "pool")
        h_down_done = sem("h_down_done", "pe")
        h_y2_ready = sem("h_y2_ready", "act")
        h_y2_turned = sem("h_y2_turned", "pe")
        h_acc_ready = sem("h_acc_ready", "dve")
        h_out = Norm("h_out")

        def mid_sync(sp):
            def load(b, r):
                sp.dma_start(h_x[r][:, :, :], a["L0_attn_x"][b].rearrange("(j p) d -> p j d", p=P)).then_inc(h_loaded[r], 16)
            for r in range(2):
                sp.wait_ge(g_norm.ready, at(B - 1 + r))
                load(r, r)
            with sp.Fori(1, B // 2) as i:
                b = 2 * i
                for r in range(2):
                    sp.wait_ge(h_xx_ready, at(b + r - 1))
                    load(b + r, r)

        def mid_pe(pe):
            def step(s, r):
                b = s - 1
                if there(b):
                    pe.wait_ge(h_oglo_ready, at(b + 1))
                    pe.wait_ge(h_oghi_ready, at(b + 1))
                    pe.wait_ge(h_x1_ready, at(b))
                    for j in range(TILES):
                        tile = slice(j * P, (j + 1) * P)
                        m = mm3(pe, bank[0][:, tile], h_oghi[1 - r][:, tile], h_oglo[1 - r][:, tile], wo_hi[:, :], wo_lo[:, :])
                    m.then_inc(h_wo_done, 1)
                b = s - 2
                if there(b):
                    pe.wait_ge(h_norm.ready, at(b + 1))
                    pe.wait_ge(h_lo_ready, at(b))
                    turn_tiles(pe, bank[2], lambda j: h_xhat[:, j, :]).then_inc(h_turned, 1)
                b = s - 3
                if there(b):
                    pe.wait_ge(h_uplo_ready, at(MLP0 * b + MLP0))
                    pe.wait_ge(h_y2_ready, at(b))
                    for c in range(MLP0):
                        m = project(pe, bank[5][:, :], DN0 + c * P, h_uphi[c][1 - r], h_uplo[c][1 - r],
                                    start=c == 0, stop=c == MLP0 - 1)
                    m.then_inc(h_down_done, 1)
                b = s - 2
                if there(b):
                    pe.wait_ge(h_lo_ready, at(b + 1))
                    for c in range(MLP0):
                        pe.wait_ge(h_gelu_ready, at(MLP0 * (b - 1) + c + 1))
                        mm3(pe, bank[3 + c][:, :], w_hi[:, UP0 + c, :], w_lo[:, UP0 + c, :], h_hi[:, :], h_lo[:, :])\
                            .then_inc(h_up_done, 1)
                b = s - 3
                if there(b):
                    pe.wait_ge(h_y2_ready, at(b + 1))
                    pe.wait_ge(h_acc_ready, at(b))
                    turn_tiles(pe, bank[6], lambda j: h_y2[:, j * P:(j + 1) * P]).then_inc(h_y2_turned, 1)
            pipelined(pe, step, 3)

        def mid_act(act):
            def step(s, r):
                if there(s):
                    act.wait_ge(h_gs_ready, at(s))
                    act.activation(h_tanh[:, :], gate[:, s, :], ACT.Tanh, scale=0.5).then_inc(h_tanh_ready, 1)
                b = s - 2
                if there(b):
                    act.wait_ge(h_turned, at(b + 1))
                    act.wait_ge(h_up_done, at(MLP0 * b))
                    act.activation(h_hi[:, :], bank[2][:, :], ACT.Copy).then_inc(h_hi_ready, 1)
                if there(s):
                    act.wait_ge(h_og_ready, at(s + 1))
                    act.wait_ge(h_wo_done, at(s - 1))
                    act.activation(h_oghi[r][:, :], h_og[:, :], ACT.Copy).then_inc(h_oghi_ready, 1)
                b = s - 3
                if there(b):
                    act.wait_ge(h_down_done, at(b + 1))
                    act.wait_ge(h_y2_turned, at(b))
                    act.activation(h_y2[:, :], bank[5][:, :], ACT.Identity, bias=b2_col[:, :]).then_inc(h_y2_ready, 1)
                b = s - 2
                if there(b):
                    for c in range(MLP0):
                        act.wait_ge(h_up_done, at(MLP0 * b + c + 1))
                        act.wait_ge(h_uplo_ready, at(MLP0 * (b - 1) + c + 1))
                        act.activation(h_up[c][:, :], bank[3 + c][:, :], ACT.Gelu, bias=w_bias[:, UP0 + c:UP0 + c + 1])\
                           .then_inc(h_gelu_ready, 1)
            pipelined(act, step, 3)

        def mid_dve(dve):
            def step(s, r):
                b = s - 2
                if there(b):
                    dve.wait_ge(h_turned, at(b))
                    norm_apply(dve, h_norm, b, h_xhat, h_x1)
                if there(s):
                    dve.wait_ge(h_tanh_ready, at(s + 1))
                    dve.scalar_tensor_tensor(out=h_gs[:, :], in0=h_tanh[:, :], scalar=1.0, in1=gate[:, s, :],
                                             op0=ALU.add, op1=ALU.mult).then_inc(h_gs_ready, 1)
                    dve.wait_ge(h_gs_ready, at(s + 1))
                    dve.wait_ge(h_oglo_ready, at(s))
                    dve.wait_ge(g_rms_ready, at(s + 1))
                    dve.tensor_tensor(h_og[:, :], h_gs[:, :], rms_o[:, s, :], ALU.mult).then_inc(h_og_ready, 1)
                if there(b):
                    dve.wait_ge(h_hi_ready, at(b + 1))
                    dve.wait_ge(h_up_done, at(MLP0 * b))
                    dve.tensor_tensor(h_lo[:, :], bank[2][:, :], h_hi[:, :].bitcast(F32), ALU.subtract).then_inc(h_lo_ready, 1)
                b = s - 1
                if there(b):
                    dve.wait_ge(h_wo_done, at(b + 1))
                    dve.wait_ge(h_loaded[1 - r], 8 * (b - (1 - r)) + 16)
                    dve.wait_ge(h_xx_ready, at(b))
                    dve.wait_ge(h_norm.ready, at(b))
                    dve.tensor_tensor(flat(h_x1), bank[0][:, :], flat(h_x[1 - r]), ALU.add).then_inc(h_x1_ready, 1)
                    dve.wait_ge(h_x1_ready, at(b + 1))
                    norm_moments(dve, h_norm, b, h_x1)
                b = s - 3
                if there(b):
                    dve.wait_ge(h_y2_turned, at(b + 1))
                    dve.wait_ge(h_xx_ready, at(b + 1))
                    dve.wait_ge(h_out.ready, at(b))
                    dve.tensor_tensor(flat(h_acc), bank[6][:, :], R[:, b, :, :].rearrange("p a b -> p (a b)"),
                                      ALU.add).then_inc(h_acc_ready, 1)
                    dve.wait_ge(h_acc_ready, at(b + 1))
                    norm_moments(dve, h_out, b, h_acc)
                b = s - 2
                if there(b):
                    for c in range(MLP0):
                        dve.wait_ge(h_gelu_ready, at(MLP0 * b + c + 1))
                        dve.wait_ge(h_down_done, at(b - 1))
                        dve.tensor_copy(h_uphi[c][r][:, :], h_up[c][:, :]).then_inc(h_uphi_ready, 1)
                b = s - 3
                if there(b):
                    norm_apply(dve, h_out, b, R[:, b, :, :], h_acc)
            pipelined(dve, step, 3)

        def mid_pool(pool):
            def step(s, r):
                if there(s):
                    pool.wait_ge(h_oghi_ready, at(s + 1))
                    pool.wait_ge(h_wo_done, at(s - 1))
                    pool.tensor_tensor(h_oglo[r][:, :], h_og[:, :], h_oghi[r][:, :].bitcast(F32), ALU.subtract)\
                        .then_inc(h_oglo_ready, 1)
                if there(s - 1):
                    norm_rstd(pool, h_norm, s - 1)
                if there(s - 3):
                    norm_rstd(pool, h_out, s - 3)
                b = s - 2
                if there(b):
                    for c in range(MLP0):
                        pool.wait_ge(h_uphi_ready, at(MLP0 * b + c + 1))
                        pool.wait_ge(h_down_done, at(b - 1))
                        pool.tensor_tensor(h_uplo[c][r][:, :], h_up[c][:, :], h_uphi[c][r][:, :].bitcast(F32), ALU.subtract)\
                            .then_inc(h_uplo_ready, 1)
                b = s - 1
                if there(b):
                    pool.wait_ge(h_x1_ready, at(b + 1))
                    pool.tensor_tensor(R[:, b, :, :].rearrange("p a b -> p (a b)"), flat(h_x[1 - r]), flat(h_x1), ALU.add)\
                        .then_inc(h_xx_ready, 1)
            pipelined(pool, step, 3)

        DOWN_LAG = 3
        RING = 4
        assert (2 * UNITS) % RING == 0
        m_x = [tok(0), tok(1)]
        m_hi, m_lo = [bufr(0), bufr(1)], [bufr(2), bufr(3)]
        m_logit = sb("m_logit", [P, TILES, E])
        m_top = sb("m_top", [P, TILES, 8])
        m_top_i = sb("m_top_i", [P, TILES, 8], U32)
        m_top_f = sb("m_top_f", [P, TILES, 2])
        m_diff = sb("m_diff", [P, TILES])
        m_th = sb("m_th", [P, TILES])
        m_w = sb("m_w", [P, 2, TILES])
        m_one = [sb(f"m_one{i}", [P, TILES, E]) for i in range(2)]
        m_part = [sb(f"m_part{i}", [P, TILES, E]) for i in range(2)]
        m_cw = sb("m_cw", [P, TILES, LO_ROW + E])
        m_parts = [workr[0:LO_ROW + E, i, :] for i in (4, 5)]
        m_silu, m_sc, m_prod = [buf(2), buf(3)], [buf(9), buf(10)], [buf(4), buf(5), buf(11), buf(12)]
        m_y = buf(7)
        m_phi = [bufr(8 + i) for i in range(RING)]
        m_plo = [bufr(12 + i) for i in range(RING)]
        m_acc = tok(8)

        m_loaded = [sem(f"m_loaded{i}") for i in range(2)]
        m_turned = sem("m_turned", "pe")
        m_hi_ready = sem("m_hi_ready", "act")
        m_lo_ready = sem("m_lo_ready", "dve")
        m_logit_done = sem("m_logit_done", "pe")
        m_logit_ready = sem("m_logit_ready", "dve")
        m_chain = sem("m_chain", "dve")
        m_th_ready = sem("m_th_ready", "act")
        m_cw_turned = sem("m_cw_turned", "pe")
        m_cwhi_ready = sem("m_cwhi_ready", "dve")
        m_gate_done = sem("m_gate_done", "pe")
        m_cwlo_ready = sem("m_cwlo_ready", "dve")
        m_up_done = sem("m_up_done", "pe")
        m_cw_done = sem("m_cw_done", "pe")
        m_silu_ready = sem("m_silu_ready", "act")
        m_sc_ready = sem("m_sc_ready", "dve")
        m_prod_ready = sem("m_prod_ready", "dve")
        m_phi_ready = sem("m_phi_ready", "act")
        m_plo_ready = sem("m_plo_ready", "pool")
        m_down_done = sem("m_down_done", "pe")
        m_y_ready = sem("m_y_ready", "act")
        m_y_turned = sem("m_y_turned", "pe")
        m_acc_ready = sem("m_acc_ready", "dve")
        m_out = Norm("m_out")
        ROUTED = E * HALVES
        CHAIN = 8

        def moe_sync(sp):
            for r in range(2):
                sp.wait_ge(h_out.ready, at(r + 1))
                sp.wait_ge(h_xx_ready, at(B - 1 + r))
                sp.dma_start(m_x[r][:, :, :], R[:, r, :, :]).then_inc(m_loaded[r], 16)
            with sp.Fori(1, B // 2) as i:
                b = 2 * i
                for r in range(2):
                    wait_apart(sp, m_turned, at(b + r - 1))
                    sp.dma_start(m_x[r][:, :, :], R[:, b + r, :, :]).then_inc(m_loaded[r], 16)

        def units(s, r):
            return [((1 - r) * UNITS + u) % RING for u in range(UNITS)]

        def moe_pe(pe):
            pe.wait_ge(h_out.ready, at(B))
            def up(b, u, q):
                e, c = divmod(u, HALVES)
                pe.wait_ge(m_prod_ready, at(UNITS * b + u - 1))
                project(pe, bank[2 + u % 2][:, :], e * HID + c * P, m_hi[q], m_lo[q]).then_inc(m_gate_done, 1)
                project(pe, bank[4 + u % 2][:, :], EXPERTS + e * HID + c * P, m_hi[q], m_lo[q])\
                    .then_inc(m_up_done, 1)

            def weight(b, e, q):
                pe.wait_ge(m_sc_ready, at(ROUTED * b + HALVES * e))
                pe.matmul(bank[1][:, :], pick_e[:, e, :], m_parts[q][:, :], start=True, stop=True).then_inc(m_cw_done, 1)

            def down(b, u, slot, q):
                e, c = divmod(u, HALVES)
                pe.wait_ge(m_phi_ready, at(UNITS * b + u + 1))
                pe.wait_ge(m_plo_ready, at(UNITS * b + u + 1))
                if u == 0:
                    pe.wait_ge(m_y_ready, at(b - 1))
                project(pe, bank[6 + q][:, :], 2 * EXPERTS + e * HID + c * P, m_phi[slot], m_plo[slot],
                        start=u == 0, stop=u == UNITS - 1).then_inc(m_down_done, 1)

            def step(s, r):
                b, q = s - 1, 1 - r
                slots, before = units(s, r), units(s - 1, 1 - r)
                for u in range(UNITS):
                    if there(b):
                        if u == 0:
                            pe.wait_ge(m_lo_ready, at(b + 1))
                        up(b, u, q)
                        if u >= HALVES and u % HALVES == 0:
                            if u == HALVES:
                                pe.wait_ge(m_cwlo_ready, at(b + 1))
                            weight(b, u // HALVES - 1, q)
                    v = u - DOWN_LAG
                    if v < 0:
                        if there(s - 2):
                            down(s - 2, UNITS + v, before[v], r)
                    elif there(b):
                        down(b, v, slots[v], q)
                    if u == 1 and there(s):
                        pe.wait_ge(m_loaded[r], 8 * (s - r) + 16)
                        pe.wait_ge(m_cwlo_ready, at(s))
                        turn_tiles(pe, bank[0], lambda j: m_x[r][:, j, :]).then_inc(m_turned, 1)
                    if u == 4 and there(s - 2):
                        pe.wait_ge(m_y_ready, at(s - 1))
                        pe.wait_ge(m_lo_ready, at(s + 1) if there(s) else at(B))
                        turn_tiles(pe, bank[0], lambda j: m_y[:, j * P:(j + 1) * P]).then_inc(m_y_turned, 1)
                    if u == 7 and there(s):
                        pe.wait_ge(m_lo_ready, at(s + 1))
                        pe.wait_ge(m_acc_ready, at(s - 1))
                        for j in range(TILES):
                            m = mm3(pe, bank[0][:, j * E:(j + 1) * E], m_hi[r][:, j * P:(j + 1) * P],
                                    m_lo[r][:, j * P:(j + 1) * P], r_hi[:, :], r_lo[:, :])
                        m.then_inc(m_logit_done, 1)
                    if u == 15 and there(s):
                        wait_apart(pe, m_chain, at(CHAIN * s + CHAIN))
                        for j in range(TILES):
                            m = pe.transpose(bank[0][0:LO_ROW + E, j * P:(j + 1) * P], m_cw[:, j, :], ident[:, :])
                        m.then_inc(m_cw_turned, 1)
            pipelined(pe, step, 2)

        def moe_act(act):
            def phi(b, u, slot):
                act.wait_ge(m_prod_ready, at(UNITS * b + u + 1))
                act.wait_ge(m_down_done, at(UNITS * b + u + 1 - RING))
                act.activation(m_phi[slot][:, :], m_prod[slot][:, :], ACT.Copy).then_inc(m_phi_ready, 1)

            def step(s, r):
                b = s - 1
                slots = units(s, r)
                for u in range(UNITS):
                    if there(b):
                        act.wait_ge(m_gate_done, at(UNITS * b + u + 1))
                        act.wait_ge(m_prod_ready, at(UNITS * b + u - 1))
                        act.activation(m_silu[u % 2][:, :], bank[2 + u % 2][:, :], ACT.Silu).then_inc(m_silu_ready, 1)
                        if u >= 1:
                            phi(b, u - 1, slots[u - 1])
                    if u == 2 and there(s):
                        act.wait_ge(m_turned, at(s + 1))
                        act.wait_ge(m_up_done, at(UNITS * (s - 1)))
                        act.activation(m_hi[r][:, :], bank[0][:, :], ACT.Copy).then_inc(m_hi_ready, 1)
                    if u == 3 and there(s - 2):
                        act.wait_ge(m_down_done, at(UNITS * (s - 1)))
                        act.wait_ge(m_y_turned, at(s - 2))
                        act.activation(m_y[:, :], bank[6 + r][:, :], ACT.Copy).then_inc(m_y_ready, 1)
                    if u == 12 and there(s):
                        act.wait_ge(m_chain, at(CHAIN * s + 2))
                        act.activation(m_th[:, :], m_diff[:, :], ACT.Tanh, scale=0.5).then_inc(m_th_ready, 1)
                if there(b):
                    phi(b, UNITS - 1, slots[UNITS - 1])
            pipelined(act, step, 2)

        def moe_dve(dve):
            def wide(x):
                return x.unsqueeze(2).broadcast_to([P, TILES, E])

            def routing(s, r, u):
                def so_far(n):
                    wait_apart(dve, m_chain, at(CHAIN * s + n))
                if u == 8:
                    dve.wait_ge(m_logit_done, at(s + 1))
                    dve.tensor_tensor(m_logit[:, :, :], bank[0][:, 0:TILES * E].rearrange("p (j e) -> p j e", e=E),
                                      ebias[:, :].unsqueeze(1).broadcast_to([P, TILES, E]), ALU.add)\
                       .then_inc(m_logit_ready, 1)
                if u == 9:
                    wait_apart(dve, m_logit_ready, at(s + 1))
                    for j in range(TILES):
                        i = dve.max(m_top[:, j, :], m_logit[:, j, :])
                    i.then_inc(m_chain, 1)
                if u == 10:
                    so_far(1)
                    dve.tensor_tensor(m_diff[:, :], m_top[:, :, 0], m_top[:, :, 1], ALU.subtract).then_inc(m_chain, 1)
                    for j in range(TILES):
                        i = dve.max_index(m_top_i[:, j, :], m_top[:, j, :], m_logit[:, j, :])
                    i.then_inc(m_chain, 1)
                if u == 11:
                    so_far(3)
                    dve.tensor_copy(m_top_f[:, :, :], m_top_i[:, :, 0:2]).then_inc(m_chain, 1)
                if u == 12:
                    so_far(4)
                    for n in range(2):
                        i = dve.tensor_tensor(m_one[n][:, :, :], iota_e[:, :].unsqueeze(1).broadcast_to([P, TILES, E]),
                                              wide(m_top_f[:, :, n]), ALU.is_equal)
                    i.then_inc(m_chain, 1)
                if u == 13:
                    dve.wait_ge(m_th_ready, at(s + 1))
                    dve.tensor_scalar(m_w[:, 0, :], m_th[:, :], 0.5, 0.5, ALU.mult, ALU.add)
                    dve.tensor_scalar(m_w[:, 1, :], m_th[:, :], -0.5, 0.5, ALU.mult, ALU.add).then_inc(m_chain, 1)
                    so_far(6)
                    for n in range(2):
                        i = dve.tensor_tensor(m_part[n][:, :, :], m_one[n][:, :, :], wide(m_w[:, n, :]), ALU.mult)
                    i.then_inc(m_chain, 1)
                if u == 14:
                    so_far(7)
                    for start in (0, LO_ROW):
                        i = dve.tensor_tensor(m_cw[:, :, start:start + E], m_part[0][:, :, :], m_part[1][:, :, :], ALU.add)
                    i.then_inc(m_chain, 1)
                if u == 16:
                    dve.wait_ge(m_cw_turned, at(s + 1))
                    dve.wait_ge(m_cw_done, at(E * (s - 1)))
                    dve.tensor_copy(m_parts[r][:, :], bank[0][0:LO_ROW + E, :]).then_inc(m_cwhi_ready, 1)
                if u == 17:
                    dve.wait_ge(m_cwhi_ready, at(s + 1))
                    low = m_parts[r][LO_ROW:LO_ROW + E, :]
                    dve.tensor_tensor(low, bank[0][LO_ROW:LO_ROW + E, :], low.bitcast(F32), ALU.subtract)\
                       .then_inc(m_cwlo_ready, 1)

            def step(s, r):
                b = s - 1
                slots = units(s, r)
                for u in range(UNITS):
                    if there(b):
                        x = m_silu[u % 2][:, :]
                        dve.wait_ge(m_silu_ready, at(UNITS * b + u + 1))
                        if u >= HALVES:
                            dve.wait_ge(m_cw_done, at(E * b + (u - HALVES) // HALVES + 1))
                            dve.wait_ge(m_prod_ready, at(UNITS * b + u - 1))
                            dve.tensor_tensor(m_sc[u % 2][:, :], bank[1][:, :], x, ALU.mult).then_inc(m_sc_ready, 1)
                            dve.wait_ge(m_sc_ready, at(ROUTED * b + u - HALVES + 1))
                            x = m_sc[u % 2][:, :]
                        dve.wait_ge(m_up_done, at(UNITS * b + u + 1))
                        dve.wait_ge(m_plo_ready, at(UNITS * b + u + 1 - RING))
                        dve.wait_ge(m_phi_ready, at(UNITS * b + u + 1 - RING))
                        dve.tensor_tensor(m_prod[slots[u]][:, :], bank[4 + u % 2][:, :], x, ALU.mult).then_inc(m_prod_ready, 1)
                    if u == 2 and there(s):
                        dve.wait_ge(m_hi_ready, at(s + 1))
                        dve.tensor_tensor(m_lo[r][:, :], bank[0][:, :], m_hi[r][:, :].bitcast(F32), ALU.subtract)\
                           .then_inc(m_lo_ready, 1)
                    if u == 5 and there(s - 2):
                        dve.wait_ge(m_y_turned, at(s - 1))
                        dve.wait_ge(m_out.ready, at(s - 2))
                        dve.tensor_tensor(flat(m_acc), bank[0][:, :], R[:, s - 2, :, :].rearrange("p a b -> p (a b)"),
                                          ALU.add).then_inc(m_acc_ready, 1)
                    if u == 6 and there(s - 2):
                        dve.wait_ge(m_acc_ready, at(s - 1))
                        norm_moments(dve, m_out, s - 2, m_acc)
                    if u == 7 and there(s - 2):
                        norm_apply(dve, m_out, s - 2, R[:, s - 2, :, :], m_acc)
                    if there(s):
                        routing(s, r, u)
            pipelined(dve, step, 2)

        def moe_pool(pool):
            def step(s, r):
                b = s - 1
                slots = units(s, r)
                for u in range(UNITS):
                    if there(b):
                        slot = slots[u]
                        pool.wait_ge(m_phi_ready, at(UNITS * b + u + 1))
                        pool.wait_ge(m_down_done, at(UNITS * b + u + 1 - RING))
                        pool.tensor_tensor(m_plo[slot][:, :], m_prod[slot][:, :], m_phi[slot][:, :].bitcast(F32),
                                           ALU.subtract).then_inc(m_plo_ready, 1)
                    if u == 6 and there(s - 2):
                        norm_rstd(pool, m_out, s - 2)
            pipelined(pool, step, 2)

        c_x = [tok(0), tok(1)]
        c_hi, c_lo = [bufr(0), bufr(1)], [bufr(2), bufr(3)]
        c_qhi, c_qlo = [bufr(4), bufr(5)], [bufr(6), bufr(7)]
        c_xsum = buf(13)[:, 0:P]
        c_z = [buf(14 + i)[:, 0:P] for i in range(2)]
        c_xb = tok(2)
        c_max, c_bias, c_den, c_rden, c_att = [sb(f"c_{n}", [P, TILES]) for n in ("max", "bias", "den", "rden", "att")]
        c_exp = [buf(3 + j) for j in range(TILES)]
        c_h, c_hhat, c_hg, c_acc = tok(7), tok(8), tok(9), tok(10)
        c_xbeta = [tok(11), tok(12)]

        c_loaded = [sem(f"c_loaded{i}") for i in range(2)]
        c_turned = sem("c_turned", "pe")
        c_hi_ready = sem("c_hi_ready", "act")
        c_lo_ready = sem("c_lo_ready", "dve")
        c_q_done = sem("c_q_done", "pe")
        c_qhi_ready = sem("c_qhi_ready", "act")
        c_qlo_ready = sem("c_qlo_ready", "dve")
        c_xsum_done = sem("c_xsum_done", "pe")
        c_xsum_ready = sem("c_xsum_ready", "act")
        c_z_done = sem("c_z_done", "pe")
        c_z_ready = sem("c_z_ready", "act")
        c_xb_ready = sem("c_xb_ready", "pool")
        c_xbeta_ready = sem("c_xbeta_ready", "pool")
        c_score_done = sem("c_score_done", "pe")
        c_max_ready = sem("c_max_ready", "dve")
        c_bias_ready = sem("c_bias_ready", "dve")
        c_exp_ready = sem("c_exp_ready", "act")
        c_rden_ready = sem("c_rden_ready", "dve")
        c_att_ready = sem("c_att_ready", "dve")
        c_h_ready = sem("c_h_ready", "dve")
        c_hg_ready = sem("c_hg_ready", "pool")
        c_acc_ready = sem("c_acc_ready", "dve")
        c_inner = Norm("c_inner")
        c_out = Norm("c_out")

        def att_sync(sp):
            for r in range(2):
                sp.wait_ge(m_out.ready, at(B - 1 + r))
                sp.dma_start(c_x[r][:, :, :], R[:, r, :, :]).then_inc(c_loaded[r], 16)
            with sp.Fori(1, B // 2) as i:
                b = 2 * i
                for r in range(2):
                    sp.wait_ge(c_xbeta_ready, at(b + r - 1))
                    sp.wait_ge(c_xsum_done, at(b + r - 1))
                    sp.dma_start(c_x[r][:, :, :], R[:, b + r, :, :]).then_inc(c_loaded[r], 16)

        def att_pe(pe):
            pe.wait_ge(m_out.ready, at(B))
            def step(s, r):
                if there(s):
                    pe.wait_ge(c_loaded[r], 8 * (s - r) + 16)
                    pe.wait_ge(c_lo_ready, at(s))
                    turn_tiles(pe, bank[0], lambda j: c_x[r][:, j, :]).then_inc(c_turned, 1)
                    pe.wait_ge(c_xsum_ready, at(s))
                    for j in range(TILES):
                        m = pe.matmul(bank[2][:, 0:P], c_x[r][:, j, :], ones[:, :], start=j == 0, stop=j == TILES - 1)
                    m.then_inc(c_xsum_done, 1)
                b, q = s - 1, 1 - r
                for j in range(TILES):
                    if there(b):
                        if j == 0:
                            pe.wait_ge(c_qlo_ready, at(b + 1))
                        pe.wait_ge(c_exp_ready, at(TILES * (b - 1) + j + 1))
                        tile = slice(j * P, (j + 1) * P)
                        mm3(pe, bank[4 + j][:, :], c_qhi[q][:, tile], c_qlo[q][:, tile], c_hi[q][:, :], c_lo[q][:, :])\
                            .then_inc(c_score_done, 1)
                    if j == 1 and there(s):
                        pe.wait_ge(c_lo_ready, at(s + 1))
                        pe.wait_ge(c_qlo_ready, at(s))
                        mm3(pe, bank[1][:, :], qk_hi[:, :], qk_lo[:, :], c_hi[r][:, :], c_lo[r][:, :]).then_inc(c_q_done, 1)
                        pe.wait_ge(c_xsum_ready, at(s + 1))
                        pe.wait_ge(c_z_ready, at(s))
                        pe.matmul(bank[3][:, 0:P], c_xsum[:, :], vfc[:, :], start=True, stop=True).then_inc(c_z_done, 1)
            pipelined(pe, step, 2)

        def att_act(act):
            def step(s, r):
                if there(s):
                    act.wait_ge(c_turned, at(s + 1))
                    act.wait_ge(c_score_done, at(TILES * (s - 1)))
                    act.activation(c_hi[r][:, :], bank[0][:, :], ACT.Copy).then_inc(c_hi_ready, 1)
                    act.wait_ge(c_xsum_done, at(s + 1))
                    act.wait_ge(c_z_done, at(s))
                    act.activation(c_xsum[:, :], bank[2][:, 0:P], ACT.Copy).then_inc(c_xsum_ready, 1)
                b = s - 1
                for j in range(TILES):
                    if there(b):
                        act.wait_ge(c_bias_ready, at(TILES * b + j + 1))
                        act.wait_ge(c_att_ready, at(b))
                        act.activation(c_exp[j][:, :], bank[4 + j][:, :], ACT.Exp, bias=c_bias[:, j:j + 1], scale=SCALE,
                                       accum_out=c_den[:, j:j + 1]).then_inc(c_exp_ready, 1)
                    if j == 1 and there(s):
                        act.wait_ge(c_q_done, at(s + 1))
                        act.activation(c_qhi[r][:, :], bank[1][:, :], ACT.Copy).then_inc(c_qhi_ready, 1)
                        act.wait_ge(c_z_done, at(s + 1))
                        act.wait_ge(c_h_ready, at(s - 1))
                        act.activation(c_z[r][:, :], bank[3][:, 0:P], ACT.Copy).then_inc(c_z_ready, 1)
            pipelined(act, step, 2)

        def att_dve(dve):
            def step(s, r):
                b, q = s - 1, 1 - r
                if there(s):
                    dve.wait_ge(c_hi_ready, at(s + 1))
                    dve.tensor_tensor(c_lo[r][:, :], bank[0][:, :], c_hi[r][:, :].bitcast(F32), ALU.subtract)\
                       .then_inc(c_lo_ready, 1)
                for j in range(TILES):
                    if there(b):
                        dve.wait_ge(c_score_done, at(TILES * b + j + 1))
                        dve.wait_ge(c_bias_ready, at(TILES * b + j))
                        dve.tensor_reduce(c_max[:, j:j + 1], bank[4 + j][:, :], AX.X, ALU.max).then_inc(c_max_ready, 1)
                        dve.wait_ge(c_max_ready, at(TILES * b + j + 1))
                        dve.wait_ge(c_exp_ready, at(TILES * (b - 1) + j + 1))
                        dve.tensor_scalar(c_bias[:, j:j + 1], c_max[:, j:j + 1], -SCALE, None, ALU.mult)\
                           .then_inc(c_bias_ready, 1)
                    if j == 1 and there(s - 2):
                        norm_apply(dve, c_inner, s - 2, c_hhat, c_h)
                    if j == 2 and there(s):
                        dve.wait_ge(c_qhi_ready, at(s + 1))
                        dve.tensor_tensor(c_qlo[r][:, :], bank[1][:, :], c_qhi[r][:, :].bitcast(F32), ALU.subtract)\
                           .then_inc(c_qlo_ready, 1)
                if there(s - 2):
                    dve.wait_ge(c_hg_ready, at(s - 1))
                    dve.wait_ge(c_xbeta_ready, at(s - 1))
                    dve.wait_ge(c_out.ready, at(s - 2))
                    dve.tensor_tensor(flat(c_acc), flat(c_hg), flat(c_xbeta[r]), ALU.add).then_inc(c_acc_ready, 1)
                    dve.wait_ge(c_acc_ready, at(s - 1))
                    norm_moments(dve, c_out, s - 2, c_acc)
                if there(b):
                    dve.wait_ge(c_exp_ready, at(TILES * b + TILES))
                    dve.reciprocal(c_rden[:, :], c_den[:, :]).then_inc(c_rden_ready, 1)
                    dve.wait_ge(c_rden_ready, at(b + 1))
                    dve.tensor_tensor(c_att[:, :], c_den[:, :], c_rden[:, :], ALU.mult).then_inc(c_att_ready, 1)
                    dve.wait_ge(c_att_ready, at(b + 1))
                    dve.wait_ge(c_z_ready, at(b + 1))
                    dve.wait_ge(c_xb_ready, at(b + 1))
                    dve.wait_ge(c_inner.ready, at(b))
                    for j in range(TILES):
                        i = dve.scalar_tensor_tensor(out=c_h[:, j, :], in0=c_z[q][:, :], scalar=c_att[:, j:j + 1],
                                                     in1=c_xb[:, j, :], op0=ALU.mult, op1=ALU.add)
                    i.then_inc(c_h_ready, 1)
                    dve.wait_ge(c_h_ready, at(b + 1))
                    norm_moments(dve, c_inner, b, c_h)
                if there(s - 2):
                    norm_apply(dve, c_out, s - 2, R[:, s - 2, :, :], c_acc)
            pipelined(dve, step, 2)

        def att_pool(pool):
            def row(x):
                return x[:, :].unsqueeze(1).broadcast_to([P, TILES, P])

            def step(s, r):
                b = s - 1
                if there(s - 2):
                    pool.wait_ge(c_inner.ready, at(s - 1))
                    pool.wait_ge(c_acc_ready, at(s - 2))
                    pool.tensor_tensor(c_hg[:, :, :], c_hhat[:, :, :], row(gamma), ALU.mult).then_inc(c_hg_ready, 1)
                if there(s):
                    pool.wait_ge(c_loaded[r], 8 * (s - r) + 16)
                    pool.wait_ge(c_h_ready, at(s))
                    pool.tensor_tensor(c_xb[:, :, :], c_x[r][:, :, :], row(bfc), ALU.add).then_inc(c_xb_ready, 1)
                    pool.wait_ge(c_acc_ready, at(s - 1))
                    pool.tensor_tensor(c_xbeta[r][:, :, :], c_x[r][:, :, :], row(beta), ALU.add).then_inc(c_xbeta_ready, 1)
                if there(s - 2):
                    norm_rstd(pool, c_out, s - 2)
                if there(b):
                    norm_rstd(pool, c_inner, b)
            pipelined(pool, step, 2)

        f_x = [tok(0), tok(1)]
        f_hi, f_lo = flat(w_hi)[:, 0:T], flat(w_lo)[:, 0:T]
        f_up = [buf(2), buf(3)]
        f_uphi = [[bufr(2 * c + i) for i in range(2)] for c in range(MLP1)]
        f_uplo = [[bufr(8 + 2 * c + i) for i in range(2)] for c in range(MLP1)]
        f_y, f_acc = buf(4), tok(5)
        f_res = [tok(6), tok(7)]

        f_loaded = [sem(f"f_loaded{i}") for i in range(2)]
        f_stored = [sem(f"f_stored{i}") for i in range(2)]
        f_turned = sem("f_turned", "pe")
        f_hi_ready = sem("f_hi_ready", "act")
        f_lo_ready = sem("f_lo_ready", "dve")
        f_up_done = sem("f_up_done", "pe")
        f_gelu_ready = sem("f_gelu_ready", "act")
        f_uphi_ready = sem("f_uphi_ready", "dve")
        f_uplo_ready = sem("f_uplo_ready", "pool")
        f_down_done = sem("f_down_done", "pe")
        f_y_ready = sem("f_y_ready", "act")
        f_y_turned = sem("f_y_turned", "pe")
        f_acc_ready = sem("f_acc_ready", "dve")
        f_out = Norm("f_out")

        def mlp_sync(sp):
            def load(b, r):
                wait_apart(sp, c_out.ready, at(b + 1))
                sp.dma_start(f_x[r][:, :, :], R[:, b, :, :]).then_inc(f_loaded[r], 16)

            def store(b, r):
                wait_apart(sp, f_out.ready, at(b + 1))
                sp.dma_start(out[b].rearrange("(j p) d -> p j d", p=P), f_res[r][:, :, :]).then_inc(f_stored[r], 16)
            for r in range(2):
                sp.wait_ge(c_xbeta_ready, at(B - 1 + r))
                sp.wait_ge(c_xsum_done, at(B - 1 + r))
                load(r, r)
            with sp.Fori(1, B // 2) as i:
                b = 2 * i
                for r in range(2):
                    wait_apart(sp, f_acc_ready, at(b + r - 1))
                    load(b + r, r)
                    store(b + r - 2, r)
            for r in range(2):
                store(B - 2 + r, r)
            for r in range(2):
                sp.wait_ge(f_stored[r], 16 * (B // 2))

        def mlp_pe(pe):
            pe.wait_ge(c_out.ready, at(B))
            def step(s, r):
                if there(s):
                    pe.wait_ge(f_loaded[r], 8 * (s - r) + 16)
                    pe.wait_ge(f_lo_ready, at(s))
                    turn_tiles(pe, bank[0], lambda j: f_x[r][:, j, :]).then_inc(f_turned, 1)
                b = s - 1
                if there(b):
                    for c in range(MLP1):
                        pe.wait_ge(f_uplo_ready, at(MLP1 * b + c + 1))
                        if c == 0:
                            pe.wait_ge(f_y_ready, at(b))
                        m = project(pe, bank[1][:, :], DN1 + c * P, f_uphi[c][1 - r], f_uplo[c][1 - r],
                                    start=c == 0, stop=c == MLP1 - 1)
                    m.then_inc(f_down_done, 1)
                if there(s):
                    pe.wait_ge(f_lo_ready, at(s + 1))
                    for c in range(MLP1):
                        pe.wait_ge(f_gelu_ready, at(MLP1 * (s - 1) + c + 1))
                        project(pe, bank[4 + c][:, :], UP1 + c * P, f_hi[:, :], f_lo[:, :])\
                            .then_inc(f_up_done, 1)
                if there(b):
                    pe.wait_ge(f_y_ready, at(b + 1))
                    pe.wait_ge(f_acc_ready, at(b))
                    turn_tiles(pe, bank[2], lambda j: f_y[:, j * P:(j + 1) * P]).then_inc(f_y_turned, 1)
            pipelined(pe, step, 2)

        def mlp_act(act):
            def step(s, r):
                if there(s):
                    act.wait_ge(f_turned, at(s + 1))
                    act.wait_ge(f_up_done, at(MLP1 * s))
                    act.activation(f_hi[:, :], bank[0][:, :], ACT.Copy).then_inc(f_hi_ready, 1)
                b = s - 1
                if there(b):
                    act.wait_ge(f_down_done, at(b + 1))
                    act.wait_ge(f_y_turned, at(b))
                    act.activation(f_y[:, :], bank[1][:, :], ACT.Identity, bias=f_b2[:, :]).then_inc(f_y_ready, 1)
                if there(s):
                    for c in range(MLP1):
                        act.wait_ge(f_up_done, at(MLP1 * s + c + 1))
                        act.wait_ge(f_uplo_ready, at(MLP1 * s + c - 1))
                        act.activation(f_up[c % 2][:, :], bank[4 + c][:, :], ACT.Gelu, bias=f_b1[:, c:c + 1])\
                           .then_inc(f_gelu_ready, 1)
            pipelined(act, step, 2)

        def mlp_dve(dve):
            def step(s, r):
                if there(s):
                    dve.wait_ge(f_hi_ready, at(s + 1))
                    dve.wait_ge(f_up_done, at(MLP1 * s))
                    dve.tensor_tensor(f_lo[:, :], bank[0][:, :], f_hi[:, :].bitcast(F32), ALU.subtract).then_inc(f_lo_ready, 1)
                    for c in range(MLP1):
                        dve.wait_ge(f_gelu_ready, at(MLP1 * s + c + 1))
                        dve.wait_ge(f_down_done, at(s - 1))
                        dve.tensor_copy(f_uphi[c][r][:, :], f_up[c % 2][:, :]).then_inc(f_uphi_ready, 1)
                b, q = s - 1, 1 - r
                if there(b):
                    dve.wait_ge(f_y_turned, at(b + 1))
                    dve.wait_ge(f_out.ready, at(b))
                    dve.tensor_tensor(flat(f_acc), bank[2][:, :], flat(f_x[q]), ALU.add).then_inc(f_acc_ready, 1)
                    dve.wait_ge(f_acc_ready, at(b + 1))
                    norm_moments(dve, f_out, b, f_acc)
                    if not isinstance(b, int) or b >= 2:
                        dve.wait_ge(f_stored[q], 8 * (b - q))
                    norm_apply(dve, f_out, b, f_res[q], f_acc)
            pipelined(dve, step, 3)

        def mlp_pool(pool):
            def step(s, r):
                if there(s):
                    for c in range(MLP1):
                        pool.wait_ge(f_uphi_ready, at(MLP1 * s + c + 1))
                        pool.wait_ge(f_down_done, at(s - 1))
                        pool.tensor_tensor(f_uplo[c][r][:, :], f_up[c % 2][:, :], f_uphi[c][r][:, :].bitcast(F32), ALU.subtract)\
                            .then_inc(f_uplo_ready, 1)
                if there(s - 1):
                    norm_rstd(pool, f_out, s - 1)
            pipelined(pool, step, 2)

        block = ctx.enter_context(nc.Block())

        @block.sync
        def _(sp):
            with nc.allow_non_contiguous_dma(reason="a few hundred bias values, one to a partition"):
                for dst, src in EARLY:
                    sp.dma_start(dst, src).then_inc(early, 16)
            load = gla_sync(sp)
            for dst, src in LATE:
                sp.dma_start(dst, src).then_inc(late_raw_in, 16)
            with nc.allow_non_contiguous_dma(reason="a few hundred bias values, one to a partition"):
                for dst, src in SMALL:
                    sp.dma_start(dst, src).then_inc(small_in, 16)
            gla_loads(sp, load)
            mid_sync(sp)
            moe_sync(sp)
            att_sync(sp)
            mlp_sync(sp)

        @block.gpsimd
        def _(pool):
            open_semaphores(pool, "pool")
            pool.memset(ident[:, :], 0.0).then_inc(pool_chain, 1)
            pool.memset(ones[:, :], 1.0).then_inc(pool_chain, 1)
            pool.memset(head_mean[:, :], 1.0 / DV).then_inc(pool_chain, 1)
            pool.memset(eps_row[:, :], EPS).then_inc(pool_chain, 1)
            pool.memset(m_cw[:, :, :], 0.0)
            pool.memset(minus_half[:, :], -0.5).then_inc(pool_chain, 1)
            pool.iota(iota_i[:, :], pattern=[[1, E]], base=0, channel_multiplier=0).then_inc(pool_chain, 1)
            pool.wait_ge(pool_chain, at(6))
            pool.affine_select(out=ident[:, :], in_=ident[:, :], compare_op=ALU.not_equal, fill=1.0, base=0,
                               pattern=[[-1, P]], channel_multiplier=1).then_inc(pool_chain, 1)
            hm = head_mean[:, :].rearrange("p (h v) -> p h v", v=DV)
            pool.affine_select(out=hm, in_=hm, compare_op=ALU.is_ge, fill=0.0, base=0,
                               pattern=[[-DV, H], [0, DV]], channel_multiplier=1).then_inc(pool_chain, 1)
            pool.wait_ge(pool_chain, at(8))
            pool.affine_select(out=hm, in_=hm, compare_op=ALU.is_ge, fill=0.0, base=DV - 1,
                               pattern=[[DV, H], [0, DV]], channel_multiplier=-1).then_inc(pool_chain, 1)
            pool.tensor_copy(iota_e[:, :], iota_i[:, :]).then_inc(const_made, 1)
            gla_pool(pool)
            pool.wait_ge(small_in, 16 * len(SMALL))
            pool.wait_ge(g_rms_ready, at(B))
            mid_pool(pool)
            pool.wait_ge(h_out.ready, at(B))
            moe_pool(pool)
            pool.wait_ge(m_out.ready, at(B))
            att_pool(pool)
            pool.wait_ge(c_out.ready, at(B))
            mlp_pool(pool)

        @block.vector
        def _(dve):
            open_semaphores(dve, "dve")
            dve.wait_ge(early, 16 * len(EARLY))

            def by_key(w, k):
                return w.rearrange("d (h k) -> d k h", k=DK)[:, k, :].unsqueeze(2)
            for k in range(DK):
                dve.tensor_scalar(w_raw[:, Q0 + k, :].rearrange("d (h v) -> d h v", v=DV),
                                  by_key(wq_raw[:, :], k).broadcast_to([P, H, DV]), float(DK) ** -0.5, None, ALU.mult)
                dve.tensor_copy(w_raw[:, K0 + k, :].rearrange("d (h v) -> d h v", v=DV),
                                by_key(wk_raw[:, :], k).broadcast_to([P, H, DV]))
            dve.tensor_scalar(wo_scaled[:, :], wo_raw[:, :], rms_col[:, :], 0.5, ALU.mult, ALU.mult).then_inc(prep_dve, 1)
            dve.wait_ge(pool_chain, at(9))
            for k in range(DK):
                dve.tensor_tensor(spread_k[:, k, :].rearrange("p (h v) -> p h v", v=DV),
                                  by_key(ident[:, 0:HK], k).broadcast_to([P, H, DV]),
                                  by_key(ident[:, HK:2 * HK], k).broadcast_to([P, H, DV]), ALU.add)
            dve.tensor_tensor(pick_raw[:, :], ident[0:LO_ROW + E, 0:E], ident[0:LO_ROW + E, LO_ROW:LO_ROW + E], ALU.add)\
               .then_inc(prep_dve, 1)
            dve.wait_ge(prep_pe, at(1))
            dve.tensor_copy(gkw1_t[:, :], bank[0][0:LOWR, 0:P]).then_inc(prep_dve, 1)
            dve.wait_ge(prep_pe, at(2))
            for i in range(P // HK):
                g = dve.tensor_copy(w_raw[:, GK, i * HK:(i + 1) * HK], bank[1][:, 0:HK])
            g.then_inc(prep_dve, 1)
            dve.wait_ge(prep_dve, at(4))
            dve.tensor_copy(pick_e[:, :, :], pick_raw[:, :].unsqueeze(2).broadcast_to([LO_ROW + E, E, P]))
            dve.tensor_scalar(flat(w_fold), flat(w_raw), ln_w[:, :], None, ALU.mult).then_inc(prep_dve, 1)
            dve.wait_ge(prep_dve, at(5))
            dve.tensor_copy(wo_hi[:, :], wo_scaled[:, :])
            dve.tensor_copy(flat(w_hi), flat(w_fold)).then_inc(prep_dve, 1)
            dve.wait_ge(prep_dve, at(6))
            dve.tensor_tensor(wo_lo[:, :], wo_scaled[:, :], wo_hi[:, :].bitcast(F32), ALU.subtract)
            dve.tensor_tensor(flat(w_lo), flat(w_fold), flat(w_hi).bitcast(F32), ALU.subtract).then_inc(prep_dve, 1)
            dve.wait_ge(prep_pe, at(3))
            dve.tensor_copy(w_bias[:, V:UP0], bank[2][:, V:UP0])
            dve.tensor_tensor(w_bias[:, GK:GK + 1], bank[2][:, GK:GK + 1], gk_b[:, :], ALU.add)
            dve.tensor_tensor(w_bias[:, UP0:NB0], bank[2][:, UP0:NB0], b1_col[:, :], ALU.add).then_inc(prep_dve, 1)
            gla_dve(dve)
            dve.wait_ge(g_rms_ready, at(B))
            dve.wait_ge(small_in, 16 * len(SMALL))
            dve.wait_ge(prep_pe, at(4))
            dve.tensor_copy(r_hi[:, :], bank[3][:, 0:E]).then_inc(prep_dve, 1)
            dve.wait_ge(prep_dve, at(9))
            dve.tensor_tensor(r_lo[:, :], bank[3][:, 0:E], r_hi[:, :].bitcast(F32), ALU.subtract)
            dve.tensor_copy(qk_hi[:, :], bank[4][:, 0:P]).then_inc(prep_dve, 1)
            dve.wait_ge(prep_dve, at(10))
            dve.tensor_tensor(qk_lo[:, :], bank[4][:, 0:P], qk_hi[:, :].bitcast(F32), ALU.subtract)
            dve.tensor_copy(fc_t[:, :], bank[5][:, 0:P]).then_inc(prep_dve, 1)
            dve.wait_ge(prep_pe, at(5))
            dve.tensor_copy(vfc[:, :], bank[6][:, 0:P]).then_inc(prep_dve, 1)
            mid_dve(dve)
            moe_dve(dve)
            att_dve(dve)
            mlp_dve(dve)

        @block.scalar
        def _(act):
            open_semaphores(act, "act")
            act.preload_act_table_set("natural_log_exp_and_others")
            act.wait_ge(prep_dve, at(8))
            act.wait_ge(pool_chain, at(9))
            gla_act(act)
            act.preload_act_table_set("gelu_and_others")
            act.wait_ge(g_rms_ready, at(B))
            act.wait_ge(small_in, 16 * len(SMALL))
            mid_act(act)
            act.preload_act_table_set("silu_and_others")
            act.wait_ge(h_out.ready, at(B))
            moe_act(act)
            act.preload_act_table_set("exp_and_others")
            act.wait_ge(m_out.ready, at(B))
            att_act(act)
            act.preload_act_table_set("gelu_and_others")
            act.wait_ge(c_out.ready, at(B))
            mlp_act(act)

        @block.tensor
        def _(pe):
            open_semaphores(pe, "pe")
            pe.wait_ge(early, 16 * len(EARLY))
            pe.wait_ge(pool_chain, at(9))
            pe.transpose(bank[0][0:LOWR, 0:P], gkw1[:, :], ident[:, :]).then_inc(prep_pe, 1)
            pe.wait_ge(prep_dve, at(3))
            pe.matmul(bank[1][:, 0:HK], gkw1_t[:, :], gkw2[:, :], start=True, stop=True).then_inc(prep_pe, 1)
            pe.wait_ge(prep_dve, at(4))
            for n in range(NB0):
                m = pe.matmul(bank[2][:, n:n + 1], w_raw[:, n, :], ln_b[:, :], start=True, stop=True)
            m.then_inc(prep_pe, 1)
            pe.wait_ge(prep_dve, at(8))
            gla_pe(pe)
            pe.wait_ge(g_rms_ready, at(B))
            pe.wait_ge(small_in, 16 * len(SMALL))
            pe.transpose(bank[3][:, 0:E], r_raw[:, :], ident[0:E, 0:E])
            pe.matmul(bank[4][:, 0:P], qkv_raw[:, 0, :], qkv_raw[:, 1, :], start=True, stop=True)
            pe.transpose(bank[5][:, 0:P], fc_raw[:, :], ident[:, :]).then_inc(prep_pe, 1)
            pe.wait_ge(prep_dve, at(11))
            pe.matmul(bank[6][:, 0:P], qkv_raw[:, 2, :], fc_t[:, :], start=True, stop=True).then_inc(prep_pe, 1)
            pe.wait_ge(prep_dve, at(12))
            pe.wait_ge(late_lo, at(2 * B))
            mid_pe(pe)
            moe_pe(pe)
            att_pe(pe)
            mlp_pe(pe)


_INS = ['L0_attn_x', 'L0_attn_ln_w', 'L0_attn_ln_b', 'L0_attn_Wq', 'L0_attn_Wk', 'L0_attn_Wv', 'L0_attn_gk_w1',
        'L0_attn_gk_w2', 'L0_attn_gk_b2', 'L0_attn_Wg', 'L0_attn_rms_w', 'L0_attn_Wo', 'L0_attn_W1', 'L0_attn_b1',
        'L0_attn_W2', 'L0_attn_b2', 'L0_ffn_router_w', 'L0_ffn_experts_bias', 'L0_ffn_w1', 'L0_ffn_w3', 'L0_ffn_w2',
        'L0_ffn_sw1', 'L0_ffn_sw3', 'L0_ffn_sw2', 'L1_attn_w_qkv', 'L1_attn_w_fc', 'L1_attn_b_fc', 'L1_attn_gamma',
        'L1_attn_beta', 'L1_ffn_w1', 'L1_ffn_b1', 'L1_ffn_w2', 'L1_ffn_b2']


def kernel(**inputs):
    import numpy as _np
    import concourse.bacc as _bacc
    from concourse import mybir as _mybir
    from concourse.bass_utils import run_bass_kernel_spmd as _run

    nc = _bacc.Bacc("TRN2", target_bir_lowering=False, num_devices=1)
    arrays, args = {}, {}
    for name in _INS:
        x = _np.ascontiguousarray(inputs[name])
        arrays[f"in_{name}_dram"] = x
        args[name] = nc.dram_tensor(f"in_{name}_dram", x.shape, _mybir.dt.from_np(x.dtype), kind="ExternalInput").ap()
    out = nc.dram_tensor("out_0_dram", inputs["L0_attn_x"].shape, _mybir.dt.float32, kind="ExternalOutput").ap()
    build(nc, args, out)
    r = _run(nc, [arrays], core_ids=[0])
    return r.results[0]["out_0_dram"]
```

```python
from contextlib import ExitStack

import concourse.bass as bass
from concourse import mybir

F32 = mybir.dt.float32
F32R = mybir.dt.float32r
I32 = mybir.dt.int32
U32 = mybir.dt.uint32
ALU = mybir.AluOpType
ACT = mybir.ActivationFunctionType
AX = mybir.AxisListType

P = 128
HEAD = 4
EPS = 1e-5
GATE_NORM = 16.0


def at(n):
    return HEAD + (max(n, 0) if isinstance(n, int) else n)


def build(nc, a, out):
    B, T, D = a["L0_attn_x"].shape
    assert D == P and B % 2 == 0
    TILES = T // P
    HK = a["L0_attn_Wq"].shape[1]
    DV = a["L0_attn_rms_w"].shape[0]
    H = D // DV
    DK = HK // H
    E, _, HID = a["L0_ffn_w1"].shape
    HALVES = HID // P
    UNITS = (E + 1) * HALVES
    MLP0 = a["L0_attn_W1"].shape[1] // P
    MLP1 = a["L1_ffn_w1"].shape[1] // P
    LOWR = a["L0_attn_gk_w1"].shape[1]
    SCALE = float(D) ** -0.5

    with ExitStack() as ctx:
        def sb(name, shape, dt=F32):
            return ctx.enter_context(nc.sbuf_tensor(name, shape, dt))

        starts = {"pe": [], "act": [], "dve": [], "pool": []}

        def sem(name, engine=None):
            s = ctx.enter_context(nc.semaphore(name))
            if engine:
                starts[engine].append(s)
            return s

        apart = ctx.enter_context(nc.semaphore("apart"))

        def wait_apart(eng, s, value):
            eng.wait_ge(s, value)
            eng.sem_inc(apart, 1)

        def open_semaphores(eng, name):
            for s in starts[name]:
                eng.sem_inc(s, HEAD)

        LAGS = {"gla": 3, "mid": 4, "moe": 2, "att": 4, "mlp": 4}
        TAIL = {name: lags + 2 * ((B - lags) // 2) for name, lags in LAGS.items()}

        def loop(eng, step, name):
            lags = LAGS[name]
            with eng.Fori(0, (B - lags) // 2) as i:
                s = 2 * i + lags
                step(s, lags % 2)
                step(s + 1, (lags + 1) % 2)

        def steps(step, first, end):
            for s in range(first, end):
                step(s, s % 2)

        def all_phases(eng, gla, mid, moe, att, mlp, before_mid, before_moe, before_att, weights=None):
            steps(gla, 0, 1)
            (weights or nothing)(eng)
            steps(gla, 1, LAGS["gla"])
            loop(eng, gla, "gla")
            steps(gla, TAIL["gla"], B + LAGS["gla"])
            before_mid(eng)
            steps(mid, 0, LAGS["mid"])
            loop(eng, mid, "mid")
            steps(mid, TAIL["mid"], B + 1)
            moe(0, 0, range(0, UNITS // 2))
            steps(mid, B + 1, B + 2)
            moe(0, 0, range(UNITS // 2, UNITS))
            steps(mid, B + 2, B + 4)
            before_moe(eng)
            steps(moe, 1, LAGS["moe"])
            loop(eng, moe, "moe")
            steps(moe, TAIL["moe"], B + 1)
            moe(B + 1, 1, range(0, DOWN_LAG + 1))
            steps(att, 0, 1)
            moe(B + 1, 1, range(DOWN_LAG + 1, UNITS))
            before_att(eng)
            steps(att, 1, LAGS["att"])
            loop(eng, att, "att")
            steps(att, TAIL["att"], B + 1)
            steps(mlp, 0, 2)
            steps(att, B + 1, B + 2)
            steps(mlp, 2, 3)
            steps(att, B + 2, B + 3)
            steps(mlp, 3, LAGS["mlp"])
            steps(att, B + 3, B + 4)
            loop(eng, mlp, "mlp")
            steps(mlp, TAIL["mlp"], B + LAGS["mlp"])

        def nothing(eng):
            pass

        def is_step(s, n):
            return isinstance(s, int) and s == n

        def there(b):
            return not isinstance(b, int) or 0 <= b < B

        bank = [ctx.enter_context(nc.psum_tensor(f"bank{i}", [P, 512], F32)) for i in range(8)]

        ident = sb("ident", [P, P])
        ones = sb("ones", [P, P])
        head_mean = sb("head_mean", [P, P])
        eps_row = sb("eps_row", [P, TILES])
        zero_row = sb("zero_row", [P, TILES])
        minus_half = sb("minus_half", [P, TILES])
        iota_i = sb("iota_i", [P, E], I32)
        iota_e = sb("iota_e", [P, E])
        spread_k = sb("spread_k", [P, DK, P], F32R)
        LO_ROW = 32
        pick_raw = sb("pick_raw", [LO_ROW + E, E])
        pick_e = sb("pick_e", [LO_ROW + E, E, P], F32R)

        ln_w = sb("ln_w", [P, 1])
        ln_b = sb("ln_b", [P, 1])
        rms_col = sb("rms_col", [P, 1])
        gk_b = sb("gk_b", [P, 1])
        b1_col = sb("b1_col", [P, MLP0])
        b2_col = sb("b2_col", [P, 1])
        ebias = sb("ebias", [P, E])
        f_b1 = sb("f_b1", [P, MLP1])
        f_b2 = sb("f_b2", [P, 1])
        bfc = sb("bfc", [P, P])
        gamma = sb("gamma", [P, P])
        beta = sb("beta", [P, P])

        GK, V, G, K0 = 0, 1, 2, 3
        Q0 = K0 + DK
        UP0 = Q0 + DK
        NB0 = UP0 + MLP0
        w_hi = sb("w_hi", [P, NB0, P], F32R)
        w_lo = sb("w_lo", [P, NB0, P], F32R)
        w_bias = sb("w_bias", [P, NB0])
        wo_scaled = sb("wo_scaled", [P, P])
        wo_hi = sb("wo_hi", [P, P], F32R)
        wo_lo = sb("wo_lo", [P, P], F32R)
        r_raw = sb("r_raw", [E, P])
        r_hi = sb("r_hi", [P, E], F32R)
        r_lo = sb("r_lo", [P, E], F32R)

        qkv_raw = sb("qkv_raw", [P, 3, P])
        fc_raw = sb("fc_raw", [P, P])
        fc_t = sb("fc_t", [P, P])
        qk_hi = sb("qk_hi", [P, P], F32R)
        qk_lo = sb("qk_lo", [P, P], F32R)
        vfc = sb("vfc", [P, P])


        R = sb("R", [P, B, TILES, P])
        gate = sb("gate", [P, B, T])
        rms_o = R[:, :, :, :].rearrange("p b j d -> p b (j d)")
        work = sb("work", [P, 24, T])
        workr = sb("workr", [P, 16, T], F32R)

        def buf(i):
            return work[:, i, :]

        def tok(i):
            return work[:, i, :].rearrange("p (j d) -> p j d", d=P)

        def bufr(i):
            return workr[:, i, :]
        wq_raw, wk_raw, wo_raw = buf(8)[:, 0:HK], buf(8)[:, HK:2 * HK], buf(9)[:, 0:P]
        gkw1, gkw1_t, gkw2 = buf(10)[:, 0:LOWR], work[0:LOWR, 11, 0:P], work[0:LOWR, 11, P:P + HK]
        w_raw = work[:, 12:16, :].rearrange("p n t -> p (n t)")[:, 0:NB0 * P].rearrange("p (n c) -> p n c", c=P)
        w_fold = work[:, 16:20, :].rearrange("p n t -> p (n t)")[:, 0:NB0 * P].rearrange("p (n c) -> p n c", c=P)

        EXPERTS = (E + 1) * HID
        UP1, DN1 = 3 * EXPERTS, 3 * EXPERTS + MLP1 * P
        DN0 = DN1 + MLP1 * P
        assert DN0 + MLP0 * P == 2 * B * T
        w_late_hi = sb("w_late_hi", [P, 2 * B, T], F32R)
        w_late_lo = sb("w_late_lo", [P, 2 * B, T], F32R)
        late_hi_row = w_late_hi[:, :, :].rearrange("p n t -> p (n t)")
        late_lo_row = w_late_lo[:, :, :].rearrange("p n t -> p (n t)")

        def late_raw(start, n):
            assert start // (B * T) == (start + n - 1) // (B * T)
            half = gate[:, :, :].rearrange("p b t -> p (b t)") if start < B * T else rms_o.rearrange("p b t -> p (b t)")
            return half[:, start % (B * T):start % (B * T) + n]

        def late(start, n=P):
            return late_hi_row[:, start:start + n], late_lo_row[:, start:start + n]

        early = sem("early_weights")
        late_raw_in = sem("late_raw_in")
        small_in = sem("small_in")
        const_made = sem("const_made", "pool")
        pool_chain = sem("pool_chain", "pool")
        prep_pe = sem("prep_pe", "pe")
        prep_dve = sem("prep_dve", "dve")
        prep_act = sem("prep_act", "act")
        late_hi = sem("late_hi", "act")
        late_lo = sem("late_lo", "pool")

        EARLY = [
            (ln_w[:, :], a["L0_attn_ln_w"].unsqueeze(1)),
            (ln_b[:, :], a["L0_attn_ln_b"].unsqueeze(1)),
            (gkw1[:, :], a["L0_attn_gk_w1"]),
            (gkw2[:, :], a["L0_attn_gk_w2"]),
            (wq_raw[:, :], a["L0_attn_Wq"]),
            (wk_raw[:, :], a["L0_attn_Wk"]),
            (w_raw[:, V, :], a["L0_attn_Wv"]),
            (w_raw[:, G, :], a["L0_attn_Wg"]),
            (w_raw[:, UP0:NB0, :], a["L0_attn_W1"].rearrange("d (c h) -> d c h", c=MLP0)),
            (gk_b[0:HK, :], a["L0_attn_gk_b2"].unsqueeze(1)),
            (gk_b[HK:2 * HK, :], a["L0_attn_gk_b2"].unsqueeze(1)),
            (b1_col[:, :], a["L0_attn_b1"].rearrange("(c p) -> p c", p=P)),
            (b2_col[:, :], a["L0_attn_b2"].unsqueeze(1)),
            (rms_col[:, :], a["L0_attn_rms_w"].unsqueeze(1).partition_broadcast(H)),
            (wo_raw[:, :], a["L0_attn_Wo"]),
        ]
        def experts(m, e, n):
            return late_raw(m * EXPERTS + e * HID, n * HID)
        split = B * T // HID - EXPERTS // HID
        LATE = [
            (experts(0, 0, 1), a["L0_ffn_sw1"][0]),
            (experts(0, 1, E).rearrange("d (e h) -> d e h", e=E), a["L0_ffn_w1"].rearrange("e d h -> d e h")),
            (experts(1, 0, 1), a["L0_ffn_sw3"][0]),
            (experts(1, 1, split - 1).rearrange("d (e h) -> d e h", h=HID),
             a["L0_ffn_w3"][0:split - 1].rearrange("e d h -> d e h")),
            (experts(1, split, E + 1 - split).rearrange("d (e h) -> d e h", h=HID),
             a["L0_ffn_w3"][split - 1:E].rearrange("e d h -> d e h")),
            (experts(2, 0, 1).rearrange("h (c d) -> h c d", c=HALVES),
             a["L0_ffn_sw2"][0].rearrange("(c h) d -> h c d", c=HALVES)),
            (experts(2, 1, E).rearrange("h (n d) -> h n d", d=P),
             a["L0_ffn_w2"].rearrange("e (c h) d -> h (e c) d", c=HALVES)),
            (late_raw(UP1, MLP1 * P), a["L1_ffn_w1"]),
            (late_raw(DN1, MLP1 * P).rearrange("h (c d) -> h c d", c=MLP1),
             a["L1_ffn_w2"].rearrange("(c h) d -> h c d", c=MLP1)),
            (late_raw(DN0, MLP0 * P).rearrange("h (c d) -> h c d", c=MLP0),
             a["L0_attn_W2"].rearrange("(c h) d -> h c d", c=MLP0)),
        ]
        SMALL = [
            (r_raw[:, :], a["L0_ffn_router_w"]),
            (ebias[:, :], a["L0_ffn_experts_bias"].partition_broadcast(P)),
            (qkv_raw[:, :, :], a["L1_attn_w_qkv"].rearrange("(c e) d -> e c d", c=3)),
            (fc_raw[:, :], a["L1_attn_w_fc"]),
            (bfc[:, :], a["L1_attn_b_fc"].partition_broadcast(P)),
            (gamma[:, :], a["L1_attn_gamma"].partition_broadcast(P)),
            (beta[:, :], a["L1_attn_beta"].partition_broadcast(P)),
            (f_b1[:, :], a["L1_ffn_b1"].rearrange("(c p) -> p c", p=P)),
            (f_b2[:, :], a["L1_ffn_b2"].unsqueeze(1)),
        ]

        def flat(t):
            return t[:, :, :].rearrange("p a b -> p (a b)")

        def project(pe, o, start_col, x_hi, x_lo, start=True, stop=True):
            hi, lo = late(start_col)
            return mm3(pe, o, hi, lo, x_hi, x_lo, start=start, stop=stop)

        def mm3(pe, o, weight_hi, weight_lo, x_hi, x_lo, start=True, stop=True):
            pe.matmul(o, weight_hi, x_hi, start=start, stop=False)
            pe.matmul(o, weight_hi, x_lo, start=False, stop=False)
            return pe.matmul(o, weight_lo, x_hi, start=False, stop=stop)

        def turn_tiles(pe, o, x):
            for j in range(TILES):
                m = pe.transpose(o[:, j * P:(j + 1) * P], x(j), ident[:, :])
            return m

        class Norm:
            def __init__(self, name, on_act=False):
                self.on_act = on_act
                self.stats = sb(f"{name}_stats", [P, TILES, 6])
                self.moments = sb(f"{name}_moments", [P, TILES, 2])
                self.var_eps = sb(f"{name}_var_eps", [P, TILES])
                self.rstd = sb(f"{name}_rstd", [P, TILES])
                self.moments_ready = sem(f"{name}_moments_ready", "dve")
                self.rstd_ready = sem(f"{name}_rstd_ready", "pool")
                self.ready = sem(f"{name}_ready", "act" if on_act else "dve")
                if on_act:
                    self.shift = sb(f"{name}_shift", [P, TILES])
                    self.shift_ready = sem(f"{name}_shift_ready", "pool")

        def norm_stats(dve, n, b, x):
            for j in range(TILES):
                dve.bn_stats(n.stats[:, j, :], x[:, j, :]).then_inc(n.moments_ready, 1)

        def norm_combine(dve, n, b):
            wait_apart(dve, n.moments_ready, at((TILES + 1) * b + TILES))
            if n.on_act:
                wait_apart(dve, n.shift_ready, at(2 * b))
            for j in range(TILES):
                i = dve.bn_aggr(n.moments[:, j, :], n.stats[:, j, :])
            i.then_inc(n.moments_ready, 1)

        def norm_moments(dve, n, b, x):
            norm_stats(dve, n, b, x)
            norm_combine(dve, n, b)

        def norm_rstd(pool, n, b):
            pool.wait_ge(n.moments_ready, at((TILES + 1) * (b + 1)))
            pool.tensor_tensor(n.var_eps[:, :], n.moments[:, :, 1], eps_row[:, :], ALU.add).then_inc(n.rstd_ready, 1)
            pool.wait_ge(n.rstd_ready, at(2 * b + 1))
            if n.on_act:
                pool.wait_ge(n.ready, at(b))
            pool.tensor_tensor(n.rstd[:, :], n.var_eps[:, :], minus_half[:, :], ALU.pow).then_inc(n.rstd_ready, 1)
            if n.on_act:
                pool.wait_ge(n.rstd_ready, at(2 * b + 2))
                product = n.var_eps
                pool.tensor_tensor(product[:, :], n.moments[:, :, 0], n.rstd[:, :], ALU.mult).then_inc(n.shift_ready, 1)
                pool.wait_ge(n.shift_ready, at(2 * b + 1))
                pool.tensor_tensor(n.shift[:, :], zero_row[:, :], product[:, :], ALU.subtract).then_inc(n.shift_ready, 1)

        def norm_apply_on_act(act, n, b, o, x):
            wait_apart(act, n.shift_ready, at(2 * b + 2))
            for j in range(TILES):
                i = act.activation(o[:, j, :], x[:, j, :], ACT.Identity, bias=n.shift[:, j:j + 1], scale=n.rstd[:, j:j + 1])
            i.then_inc(n.ready, 1)

        def norm_apply(dve, n, b, o, x):
            dve.wait_ge(n.rstd_ready, at(2 * b + 2))
            for j in range(TILES):
                i = dve.tensor_scalar(o[:, j, :], x[:, j, :], n.moments[:, j, 0:1], n.rstd[:, j:j + 1],
                                      ALU.subtract, ALU.mult)
            i.then_inc(n.ready, 1)

        g_x = [tok(0), tok(1)]
        g_xhat = [tok(2), tok(3)]
        g_hhi, g_hlo = [bufr(0), bufr(1)], [bufr(2), bufr(3)]
        g_z, g_log, g_ls = buf(4), buf(5), buf(6)
        assert 2 * HK == P
        g_parts = bufr(4)
        g_v = buf(7)
        g_dec = [buf(8 + k) for k in range(DK)]
        g_kv = [buf(12 + k) for k in range(DK)]
        g_S = [buf(16 + k) for k in range(DK)]
        g_o = [buf(20), buf(21)]
        g_sq = buf(22)
        g_r = buf(23)

        g_loaded = [sem(f"g_loaded{i}") for i in range(2)]
        g_norm = Norm("g_norm")
        g_turned = sem("g_turned", "pe")
        g_hi_ready = sem("g_hi_ready", "act")
        g_lo_ready = sem("g_lo_ready", "dve")
        g_gk_done = sem("g_gk_done", "pe")
        g_v_done = sem("g_v_done", "pe")
        g_g_done = sem("g_g_done", "pe")
        g_k_done = sem("g_k_done", "pe")
        g_dec_done = sem("g_dec_done", "pe")
        g_q_done = sem("g_q_done", "pe")
        g_ms_done = sem("g_ms_done", "pe")
        g_z_ready = sem("g_z_ready", "act")
        g_abs_ready = sem("g_abs_ready", "act")
        g_exp_ready = sem("g_exp_ready", "act")
        g_log_ready = sem("g_log_ready", "act")
        g_v_ready = sem("g_v_ready", "act")
        g_gate_ready = sem("g_gate_ready", "act")
        g_dec_ready = sem("g_dec_ready", "act")
        g_sq_ready = sem("g_sq_ready", "act")
        g_ln_ready = sem("g_ln_ready", "act")
        g_r_ready = sem("g_r_ready", "act")
        g_ls_ready = sem("g_ls_ready", "dve")
        g_lshi_ready = sem("g_lshi_ready", "dve")
        g_lslo_ready = sem("g_lslo_ready", "pool")
        g_kv_ready = sem("g_kv_ready", "dve")
        g_S_ready = sem("g_S_ready", "dve")
        g_qS_ready = sem("g_qS_ready", "dve")
        g_sum_ready = sem("g_sum_ready", "pool")
        g_o_ready = sem("g_o_ready", "pool")
        g_rms_ready = sem("g_rms_ready", "pool")

        Q_BANK = [2, 3, 1, 0]

        def gla_load(sp, b, r):
            sp.dma_start(g_x[r][:, :, :], a["L0_attn_x"][b].rearrange("(j p) d -> p j d", p=P)).then_inc(g_loaded[r], 16)

        def gla_sync(sp):
            with sp.Fori(1, B // 2) as i:
                b = 2 * i
                for r in range(2):
                    sp.wait_ge(g_norm.ready, at(b + r - 1))
                    gla_load(sp, b + r, r)

        def gla_pe(pe):
            def step(s, r):
                t, b, e = s - 1, s - 2, s - 3
                if there(b):
                    hhi, hlo = g_hhi[r][:, :], g_hlo[r][:, :]

                    def apply(block, o):
                        return mm3(pe, o[:, :], w_hi[:, block, :], w_lo[:, block, :], hhi, hlo)
                    pe.wait_ge(g_lo_ready, at(b + 1))
                    pe.wait_ge(g_qS_ready, at(DK * (b - 1) + 1))
                    apply(GK, bank[2]).then_inc(g_gk_done, 1)
                    pe.wait_ge(g_qS_ready, at(DK * (b - 1) + 3))
                    apply(V, bank[1]).then_inc(g_v_done, 1)
                    apply(G, bank[3]).then_inc(g_g_done, 1)
                    for k in range(DK):
                        pe.wait_ge(g_dec_ready, at(DK * (b - 1) + k + 1))
                        apply(K0 + k, bank[4 + k]).then_inc(g_k_done, 1)
                if there(t):
                    pe.wait_ge(g_norm.ready, at(t + 1))
                    pe.wait_ge(g_qS_ready, at(DK * b) if there(b) else at(0))
                    turn_tiles(pe, bank[0], lambda j: g_xhat[1 - r][:, j, :]).then_inc(g_turned, 1)

                def mean_square():
                    pe.wait_ge(g_sq_ready, at(e + 1))
                    if there(b):
                        pe.wait_ge(g_v_ready, at(b + 1))
                    else:
                        pe.wait_ge(g_qS_ready, at(DK * B))
                    pe.matmul(bank[1][:, :], head_mean[:, :], g_sq[:, :], start=True, stop=True).then_inc(g_ms_done, 1)
                if there(b):
                    pe.wait_ge(g_lslo_ready, at(b + 1))
                    for k in range(DK):
                        pe.wait_ge(g_kv_ready, at(DK * b + k + 1))
                        pe.matmul(bank[4 + k][:, :], spread_k[:, k, :], g_parts[:, :], start=True, stop=True)\
                          .then_inc(g_dec_done, 1)
                        if k == 0:
                            pe.wait_ge(g_z_ready, at(b + 1))
                        elif k == 1:
                            pe.wait_ge(g_gate_ready, at(b + 1))
                        elif k == 2:
                            pe.wait_ge(g_v_ready, at(b + 1))
                            pe.wait_ge(g_ln_ready, at(e + 1))
                        elif there(t):
                            pe.wait_ge(g_lo_ready, at(t + 1))
                        apply(Q0 + k, bank[Q_BANK[k]]).then_inc(g_q_done, 1)
                        if k == 0 and there(e):
                            mean_square()
                elif there(e):
                    mean_square()
            return step

        def gla_act(act):
            def step(s, r):
                t, b, e = s - 1, s - 2, s - 3
                if there(b):
                    act.wait_ge(g_gk_done, at(b + 1))
                    act.wait_ge(g_ls_ready, at(b))
                    act.activation(g_log[:, :], bank[2][:, :], ACT.Abs, bias=w_bias[:, GK:GK + 1]).then_inc(g_abs_ready, 1)
                    act.wait_ge(g_abs_ready, at(b + 1))
                    act.activation(g_log[:, :], g_log[:, :], ACT.Exp, scale=-1.0).then_inc(g_exp_ready, 1)
                    act.activation(g_z[:, :], bank[2][:, :], ACT.Identity, bias=w_bias[:, GK:GK + 1]).then_inc(g_z_ready, 1)
                    act.wait_ge(g_exp_ready, at(b + 1))
                    act.activation(g_log[:, :], g_log[:, :], ACT.Ln, bias=1.0).then_inc(g_log_ready, 1)
                    act.wait_ge(g_v_done, at(b + 1))
                    act.wait_ge(g_kv_ready, at(DK * b))
                    act.activation(g_v[:, :], bank[1][:, :], ACT.Identity, bias=w_bias[:, V:V + 1]).then_inc(g_v_ready, 1)
                    act.wait_ge(g_g_done, at(b + 1))
                    wait_apart(act, late_lo, at(2 * b + 2))
                    act.activation(gate[:, b, :], bank[3][:, :], ACT.Identity, bias=w_bias[:, G:G + 1]).then_inc(g_gate_ready, 1)

                def late_part():
                    act.wait_ge(late_raw_in, 16 * len(LATE))
                    for half, raw in enumerate((gate[:, t, :], rms_o[:, t, :])):
                        act.activation(w_late_hi[:, half * B + t, :], raw, ACT.Copy).then_inc(late_hi, 1)
                if there(t) and not is_step(s, 1):
                    late_part()
                if there(t):
                    act.wait_ge(g_turned, at(t + 1))
                    act.wait_ge(g_q_done, at(DK * (t - 1)))
                    act.activation(g_hhi[1 - r][:, :], bank[0][:, :], ACT.Copy).then_inc(g_hi_ready, 1)
                if is_step(s, 1):
                    late_part()

                def decay(k):
                    act.wait_ge(g_dec_done, at(DK * b + k + 1))
                    act.wait_ge(g_S_ready, at(DK * (b - 1) + k + 1))
                    act.activation(g_dec[k][:, :], bank[4 + k][:, :], ACT.Exp, scale=1.0 / GATE_NORM)\
                       .then_inc(g_dec_ready, 1)
                if there(e):
                    act.wait_ge(g_o_ready, at(e + 1))
                    act.wait_ge(g_ms_done, at(e))
                    act.activation(g_sq[:, :], g_o[1 - r][:, :], ACT.Square).then_inc(g_sq_ready, 1)
                if there(b):
                    decay(0)
                if there(e):
                    act.wait_ge(g_ms_done, at(e + 1))
                    act.wait_ge(g_rms_ready, at(e))
                    act.activation(g_r[:, :], bank[1][:, :], ACT.Ln, bias=eps_row[:, 0:1]).then_inc(g_ln_ready, 1)
                if there(b):
                    decay(1)
                if there(e):
                    act.wait_ge(g_ln_ready, at(e + 1))
                    act.activation(g_r[:, :], g_r[:, :], ACT.Exp, scale=-0.5).then_inc(g_r_ready, 1)
                if there(b):
                    decay(2)
                    decay(3)
            return step

        def gla_dve(dve):
            def step(s, r):
                t, b = s - 1, s - 2
                if there(t):
                    dve.wait_ge(g_turned, at(t - 1))
                    norm_apply(dve, g_norm, t, g_xhat[1 - r], g_x[1 - r])
                if there(b):
                    dve.wait_ge(g_z_ready, at(b + 1))
                    dve.wait_ge(g_log_ready, at(b + 1))
                    dve.wait_ge(g_lslo_ready, at(b))
                    dve.scalar_tensor_tensor(out=g_ls[:, :], in0=g_z[:, :], scalar=0.0, in1=g_log[:, :],
                                             op0=ALU.min, op1=ALU.subtract).then_inc(g_ls_ready, 1)
                    dve.wait_ge(g_ls_ready, at(b + 1))
                    dve.wait_ge(g_dec_done, at(DK * b))
                    dve.tensor_copy(g_parts[:, :], g_ls[:, :]).then_inc(g_lshi_ready, 1)
                    dve.wait_ge(g_v_ready, at(b + 1))
                    for k in range(DK):
                        dve.wait_ge(g_k_done, at(DK * b + k + 1))
                        dve.scalar_tensor_tensor(out=g_kv[k][:, :], in0=bank[4 + k][:, :], scalar=w_bias[:, K0 + k:K0 + k + 1],
                                                 in1=g_v[:, :], op0=ALU.add, op1=ALU.mult).then_inc(g_kv_ready, 1)
                if there(t):
                    dve.wait_ge(g_hi_ready, at(t + 1))
                    dve.wait_ge(g_q_done, at(DK * (t - 1)))
                    dve.tensor_tensor(g_hlo[1 - r][:, :], bank[0][:, :], g_hhi[1 - r][:, :].bitcast(F32), ALU.subtract)\
                       .then_inc(g_lo_ready, 1)
                for k in range(DK):
                    if there(b):
                        dve.wait_ge(g_dec_ready, at(DK * b + k + 1))
                        dve.wait_ge(g_kv_ready, at(DK * b + k + 1))
                        dve.wait_ge(g_o_ready, at(b))
                        dve.tensor_tensor_scan(g_S[k][:, :], g_dec[k][:, :], g_kv[k][:, :], 0.0, ALU.mult, ALU.add)\
                           .then_inc(g_S_ready, 1)
                        dve.wait_ge(g_S_ready, at(DK * b + k + 1))
                        dve.wait_ge(g_q_done, at(DK * b + k + 1))
                        dve.scalar_tensor_tensor(out=g_S[k][:, :], in0=bank[Q_BANK[k]][:, :],
                                                 scalar=w_bias[:, Q0 + k:Q0 + k + 1], in1=g_S[k][:, :],
                                                 op0=ALU.add, op1=ALU.mult).then_inc(g_qS_ready, 1)
                    if k == 1 and there(s):
                        dve.wait_ge(g_loaded[r], 8 * (s - r) + 16)
                        norm_moments(dve, g_norm, s, g_x[r])
            return step

        def gla_pool(pool):
            def step(s, r):
                t, b, e = s - 1, s - 2, s - 3
                if is_step(s, 0):
                    norm_rstd(pool, g_norm, 0)
                if there(b):
                    pool.wait_ge(g_lshi_ready, at(b + 1))
                    pool.wait_ge(g_dec_done, at(DK * b))
                    pool.wait_ge(g_o_ready, at(b))
                    if is_step(s, 2):
                        pool.wait_ge(late_lo, at(2))
                    low = g_parts[HK:2 * HK, :]
                    pool.tensor_tensor(low, g_ls[HK:2 * HK, :], low.bitcast(F32), ALU.subtract).then_inc(g_lslo_ready, 1)
                    wait_apart(pool, g_lslo_ready, at(b + 1))
                if is_step(s, 1):
                    norm_rstd(pool, g_norm, 1)
                if there(t):
                    for half, raw in enumerate((gate[:, t, :], rms_o[:, t, :])):
                        pool.wait_ge(late_hi, at(2 * t + half + 1))
                        pool.tensor_tensor(w_late_lo[:, half * B + t, :], raw, w_late_hi[:, half * B + t, :].bitcast(F32),
                                           ALU.subtract).then_inc(late_lo, 1)

                def pair(h):
                    pool.wait_ge(g_qS_ready, at(DK * b + 2 * h + 2))
                    pool.tensor_tensor(g_S[2 * h][:, :], g_S[2 * h][:, :], g_S[2 * h + 1][:, :], ALU.add)\
                        .then_inc(g_sum_ready, 1)
                if there(b):
                    pair(0)
                if there(e):
                    pool.wait_ge(g_r_ready, at(e + 1))
                    pool.tensor_tensor(rms_o[:, e, :], g_o[1 - r][:, :], g_r[:, :], ALU.mult).then_inc(g_rms_ready, 1)
                if there(s) and not is_step(s, 0) and not is_step(s, 1):
                    norm_rstd(pool, g_norm, s)
                if there(b):
                    pair(1)
                    pool.wait_ge(g_sum_ready, at(2 * b + 2))
                    pool.wait_ge(g_rms_ready, at(b - 1))
                    pool.tensor_tensor(g_o[r][:, :], g_S[0][:, :], g_S[2][:, :], ALU.add).then_inc(g_o_ready, 1)
            return step

        h_x = [tok(0), tok(1)]
        h_tanh, h_gs, h_og = buf(2), buf(3), buf(4)
        h_oghi, h_oglo = [bufr(0), bufr(1)], [bufr(2), bufr(3)]
        h_y2 = buf(6)
        h_x1 = [tok(7), tok(12)]
        h_xhat, h_acc = tok(8), tok(9)
        h_hi, h_lo = bufr(14), bufr(15)
        h_up = [buf(10 + c) for c in range(MLP0)]
        h_uphi = [[bufr(6 + 2 * c + i) for i in range(2)] for c in range(MLP0)]
        h_uplo = [[bufr(10 + 2 * c + i) for i in range(2)] for c in range(MLP0)]

        h_loaded = [sem(f"h_loaded{i}") for i in range(2)]
        h_tanh_ready = sem("h_tanh_ready", "act")
        h_gs_ready = sem("h_gs_ready", "dve")
        h_og_ready = sem("h_og_ready", "dve")
        h_oghi_ready = sem("h_oghi_ready", "act")
        h_oglo_ready = sem("h_oglo_ready", "pool")
        h_wo_done = sem("h_wo_done", "pe")
        h_x1_ready = sem("h_x1_ready", "dve")
        h_xx_ready = sem("h_xx_ready", "pool")
        h_norm = Norm("h_norm", on_act=True)
        h_turned = sem("h_turned", "pe")
        h_hi_ready = sem("h_hi_ready", "act")
        h_lo_ready = sem("h_lo_ready", "dve")
        h_up_done = sem("h_up_done", "pe")
        h_gelu_ready = sem("h_gelu_ready", "act")
        h_uphi_ready = sem("h_uphi_ready", "act")
        h_uplo_ready = sem("h_uplo_ready", "pool")
        h_down_done = sem("h_down_done", "pe")
        h_y2_ready = sem("h_y2_ready", "act")
        h_y2_turned = sem("h_y2_turned", "pe")
        h_acc_ready = sem("h_acc_ready", "dve")
        h_out = Norm("h_out")

        def mid_sync(sp):
            def load(b, r):
                sp.dma_start(h_x[r][:, :, :], a["L0_attn_x"][b].rearrange("(j p) d -> p j d", p=P)).then_inc(h_loaded[r], 16)
            for r in range(2):
                sp.wait_ge(g_norm.ready, at(B - 1 + r))
                load(r, r)
            with sp.Fori(1, B // 2) as i:
                b = 2 * i
                for r in range(2):
                    sp.wait_ge(h_xx_ready, at(b + r - 1))
                    load(b + r, r)

        def mid_pe(pe):
            def step(s, r):
                b = s - 1
                if there(b):
                    pe.wait_ge(h_oglo_ready, at(b + 1))
                    pe.wait_ge(h_oghi_ready, at(b + 1))
                    pe.wait_ge(h_x1_ready, at(b))
                    for j in range(TILES):
                        tile = slice(j * P, (j + 1) * P)
                        m = mm3(pe, bank[0][:, tile], h_oghi[1 - r][:, tile], h_oglo[1 - r][:, tile], wo_hi[:, :], wo_lo[:, :])
                    m.then_inc(h_wo_done, 1)
                b = s - 2
                if there(b):
                    pe.wait_ge(h_norm.ready, at(b + 1))
                    pe.wait_ge(h_lo_ready, at(b))
                    turn_tiles(pe, bank[2], lambda j: h_xhat[:, j, :]).then_inc(h_turned, 1)
                b = s - 3
                if there(b):
                    pe.wait_ge(h_uplo_ready, at(MLP0 * b + MLP0))
                    pe.wait_ge(h_y2_ready, at(b))
                    for c in range(MLP0):
                        m = project(pe, bank[5][:, :], DN0 + c * P, h_uphi[c][1 - r], h_uplo[c][1 - r],
                                    start=c == 0, stop=c == MLP0 - 1)
                    m.then_inc(h_down_done, 1)
                b = s - 2
                if there(b):
                    pe.wait_ge(h_lo_ready, at(b + 1))
                    for c in range(MLP0):
                        pe.wait_ge(h_gelu_ready, at(MLP0 * (b - 1) + c + 1))
                        mm3(pe, bank[3 + c][:, :], w_hi[:, UP0 + c, :], w_lo[:, UP0 + c, :], h_hi[:, :], h_lo[:, :])\
                            .then_inc(h_up_done, 1)
                b = s - 3
                if there(b):
                    pe.wait_ge(h_y2_ready, at(b + 1))
                    pe.wait_ge(h_acc_ready, at(b))
                    turn_tiles(pe, bank[6], lambda j: h_y2[:, j * P:(j + 1) * P]).then_inc(h_y2_turned, 1)
            return step

        def mid_act(act):
            def step(s, r):
                if is_step(s, 0):
                    act.wait_ge(g_turned, at(B))
                    act.wait_ge(g_q_done, at(DK * B))
                if there(s):
                    act.wait_ge(h_gs_ready, at(s))
                    act.activation(h_tanh[:, :], gate[:, s, :], ACT.Tanh, scale=0.5).then_inc(h_tanh_ready, 1)
                b = s - 2
                if there(b):
                    wait_apart(act, h_turned, at(b))
                    norm_apply_on_act(act, h_norm, b, h_xhat, h_x1[r])
                    act.wait_ge(h_turned, at(b + 1))
                    act.wait_ge(h_up_done, at(MLP0 * b))
                    act.activation(h_hi[:, :], bank[2][:, :], ACT.Copy).then_inc(h_hi_ready, 1)
                if there(s):
                    act.wait_ge(h_og_ready, at(s + 1))
                    act.wait_ge(h_wo_done, at(s - 1))
                    act.activation(h_oghi[r][:, :], h_og[:, :], ACT.Copy).then_inc(h_oghi_ready, 1)
                b = s - 3
                if there(b):
                    act.wait_ge(h_down_done, at(b + 1))
                    act.wait_ge(h_y2_turned, at(b))
                    act.activation(h_y2[:, :], bank[5][:, :], ACT.Identity, bias=b2_col[:, :]).then_inc(h_y2_ready, 1)
                b = s - 2
                if there(b):
                    for c in range(MLP0):
                        act.wait_ge(h_up_done, at(MLP0 * b + c + 1))
                        act.wait_ge(h_uplo_ready, at(MLP0 * (b - 1) + c + 1))
                        act.activation(h_up[c][:, :], bank[3 + c][:, :], ACT.Gelu, bias=w_bias[:, UP0 + c:UP0 + c + 1])\
                           .then_inc(h_gelu_ready, 1)
                    for c in range(MLP0):
                        act.wait_ge(h_gelu_ready, at(MLP0 * b + c + 1))
                        act.wait_ge(h_down_done, at(b - 1))
                        act.activation(h_uphi[c][r][:, :], h_up[c][:, :], ACT.Copy).then_inc(h_uphi_ready, 1)
            return step

        def mid_dve(dve):
            def step(s, r):
                if there(s):
                    dve.wait_ge(h_tanh_ready, at(s + 1))
                    dve.scalar_tensor_tensor(out=h_gs[:, :], in0=h_tanh[:, :], scalar=1.0, in1=gate[:, s, :],
                                             op0=ALU.add, op1=ALU.mult).then_inc(h_gs_ready, 1)
                b = s - 1
                if there(b):
                    dve.wait_ge(h_wo_done, at(b + 1))
                    dve.wait_ge(h_loaded[1 - r], 8 * (b - (1 - r)) + 16)
                    dve.wait_ge(h_xx_ready, at(b - 1))
                    dve.wait_ge(h_norm.ready, at(b - 1))
                    dve.tensor_tensor(flat(h_x1[1 - r]), bank[0][:, :], flat(h_x[1 - r]), ALU.add).then_inc(h_x1_ready, 1)
                if there(s):
                    dve.wait_ge(h_gs_ready, at(s + 1))
                    dve.wait_ge(h_oglo_ready, at(s))
                    dve.wait_ge(g_rms_ready, at(s + 1))
                    dve.tensor_tensor(h_og[:, :], h_gs[:, :], rms_o[:, s, :], ALU.mult).then_inc(h_og_ready, 1)
                if there(b):
                    dve.wait_ge(h_x1_ready, at(b + 1))
                    norm_stats(dve, h_norm, b, h_x1[1 - r])
                b = s - 2
                if there(b):
                    dve.wait_ge(h_hi_ready, at(b + 1))
                    dve.wait_ge(h_up_done, at(MLP0 * b))
                    dve.tensor_tensor(h_lo[:, :], bank[2][:, :], h_hi[:, :].bitcast(F32), ALU.subtract).then_inc(h_lo_ready, 1)
                if there(s - 1):
                    norm_combine(dve, h_norm, s - 1)
                if there(s - 4):
                    norm_apply(dve, h_out, s - 4, R[:, s - 4, :, :], h_acc)
                b = s - 3
                if there(b):
                    dve.wait_ge(h_y2_turned, at(b + 1))
                    dve.wait_ge(h_xx_ready, at(b + 1))
                    dve.wait_ge(h_out.ready, at(b))
                    dve.tensor_tensor(flat(h_acc), bank[6][:, :], R[:, b, :, :].rearrange("p a b -> p (a b)"),
                                      ALU.add).then_inc(h_acc_ready, 1)
                    dve.wait_ge(h_acc_ready, at(b + 1))
                    norm_moments(dve, h_out, b, h_acc)
            return step

        def mid_pool(pool):
            def step(s, r):
                if is_step(s, 0):
                    pool.wait_ge(g_q_done, at(DK * B))
                if there(s):
                    pool.wait_ge(h_oghi_ready, at(s + 1))
                    pool.wait_ge(h_wo_done, at(s - 1))
                    pool.tensor_tensor(h_oglo[r][:, :], h_og[:, :], h_oghi[r][:, :].bitcast(F32), ALU.subtract)\
                        .then_inc(h_oglo_ready, 1)
                if there(s - 1):
                    norm_rstd(pool, h_norm, s - 1)
                b = s - 2
                if there(b):
                    for c in range(MLP0):
                        pool.wait_ge(h_uphi_ready, at(MLP0 * b + c + 1))
                        pool.wait_ge(h_down_done, at(b - 1))
                        pool.tensor_tensor(h_uplo[c][r][:, :], h_up[c][:, :], h_uphi[c][r][:, :].bitcast(F32), ALU.subtract)\
                            .then_inc(h_uplo_ready, 1)
                if there(s - 3):
                    norm_rstd(pool, h_out, s - 3)
                b = s - 1
                if there(b):
                    pool.wait_ge(h_x1_ready, at(b + 1))
                    pool.tensor_tensor(R[:, b, :, :].rearrange("p a b -> p (a b)"), flat(h_x[1 - r]), flat(h_x1[1 - r]), ALU.add)\
                        .then_inc(h_xx_ready, 1)
            return step

        DOWN_LAG = 3
        RING = 4
        assert (2 * UNITS) % RING == 0
        m_x = [tok(0), tok(1)]
        m_hi, m_lo = [bufr(0), bufr(1)], [bufr(2), bufr(3)]
        m_logit = sb("m_logit", [P, TILES, E])
        m_top = sb("m_top", [P, TILES, 8])
        m_top_i = sb("m_top_i", [P, TILES, 8], U32)
        m_top_f = sb("m_top_f", [P, TILES, 2])
        m_diff = sb("m_diff", [P, TILES])
        m_th = sb("m_th", [P, TILES])
        m_w = sb("m_w", [P, 2, TILES])
        m_one = [sb(f"m_one{i}", [P, TILES, E]) for i in range(2)]
        m_part = [sb(f"m_part{i}", [P, TILES, E]) for i in range(2)]
        m_cw = sb("m_cw", [P, TILES, LO_ROW + E])
        m_parts = [workr[0:LO_ROW + E, i, :] for i in (4, 5)]
        m_silu, m_sc, m_prod = [buf(2), buf(3)], [buf(9), buf(10)], [buf(4), buf(5), buf(11), buf(12)]
        m_y = buf(7)
        m_phi = [bufr(8 + i) for i in range(RING)]
        m_plo = [bufr(12 + i) for i in range(RING)]
        m_acc = tok(8)

        m_loaded = [sem(f"m_loaded{i}") for i in range(2)]
        m_turned = sem("m_turned", "pe")
        m_hi_ready = sem("m_hi_ready", "act")
        m_lo_ready = sem("m_lo_ready", "dve")
        m_logit_done = sem("m_logit_done", "pe")
        m_logit_ready = sem("m_logit_ready", "dve")
        m_chain = sem("m_chain", "dve")
        m_th_ready = sem("m_th_ready", "act")
        m_cw_turned = sem("m_cw_turned", "pe")
        m_cwhi_ready = sem("m_cwhi_ready", "dve")
        m_gate_done = sem("m_gate_done", "pe")
        m_cwlo_ready = sem("m_cwlo_ready", "dve")
        m_up_done = sem("m_up_done", "pe")
        m_cw_done = sem("m_cw_done", "pe")
        m_silu_ready = sem("m_silu_ready", "act")
        m_sc_ready = sem("m_sc_ready", "dve")
        m_prod_ready = sem("m_prod_ready", "dve")
        m_phi_ready = sem("m_phi_ready", "act")
        m_plo_ready = sem("m_plo_ready", "pool")
        m_down_done = sem("m_down_done", "pe")
        m_y_ready = sem("m_y_ready", "act")
        m_y_turned = sem("m_y_turned", "pe")
        m_acc_ready = sem("m_acc_ready", "dve")
        m_out = Norm("m_out")
        ROUTED = E * HALVES
        CHAIN = 8

        def moe_sync(sp):
            for r in range(2):
                sp.wait_ge(h_out.ready, at(r + 1))
                sp.wait_ge(h_xx_ready, at(B - 1 + r))
                sp.dma_start(m_x[r][:, :, :], R[:, r, :, :]).then_inc(m_loaded[r], 16)
            with sp.Fori(1, B // 2) as i:
                b = 2 * i
                for r in range(2):
                    wait_apart(sp, m_turned, at(b + r - 1))
                    sp.dma_start(m_x[r][:, :, :], R[:, b + r, :, :]).then_inc(m_loaded[r], 16)

        def units(s, r):
            return [((1 - r) * UNITS + u) % RING for u in range(UNITS)]

        def moe_pe(pe):
            def up(b, u, q):
                e, c = divmod(u, HALVES)
                pe.wait_ge(m_prod_ready, at(UNITS * b + u - 1))
                project(pe, bank[2 + u % 2][:, :], e * HID + c * P, m_hi[q], m_lo[q]).then_inc(m_gate_done, 1)
                project(pe, bank[4 + u % 2][:, :], EXPERTS + e * HID + c * P, m_hi[q], m_lo[q])\
                    .then_inc(m_up_done, 1)

            def weight(b, e, q):
                pe.wait_ge(m_sc_ready, at(ROUTED * b + HALVES * e))
                pe.matmul(bank[1][:, :], pick_e[:, e, :], m_parts[q][:, :], start=True, stop=True).then_inc(m_cw_done, 1)

            def down(b, u, slot, q):
                e, c = divmod(u, HALVES)
                pe.wait_ge(m_phi_ready, at(UNITS * b + u + 1))
                pe.wait_ge(m_plo_ready, at(UNITS * b + u + 1))
                if u == 0:
                    pe.wait_ge(m_y_ready, at(b - 1))
                project(pe, bank[6 + q][:, :], 2 * EXPERTS + e * HID + c * P, m_phi[slot], m_plo[slot],
                        start=u == 0, stop=u == UNITS - 1).then_inc(m_down_done, 1)

            def step(s, r, part=range(UNITS)):
                b, q = s - 1, 1 - r
                slots, before = units(s, r), units(s - 1, 1 - r)
                if is_step(s, 1):
                    pe.wait_ge(h_out.ready, at(B))
                for u in part:
                    if there(b):
                        if u == 0:
                            pe.wait_ge(m_lo_ready, at(b + 1))
                        up(b, u, q)
                        if u >= HALVES and u % HALVES == 0:
                            if u == HALVES:
                                pe.wait_ge(m_cwlo_ready, at(b + 1))
                            weight(b, u // HALVES - 1, q)
                    v = u - DOWN_LAG
                    if v < 0:
                        if there(s - 2):
                            down(s - 2, UNITS + v, before[v], r)
                    elif there(b):
                        down(b, v, slots[v], q)
                    if u == 1 and there(s):
                        pe.wait_ge(m_loaded[r], 8 * (s - r) + 16)
                        if is_step(s, 0):
                            pe.wait_ge(h_x1_ready, at(B))
                        pe.wait_ge(m_cwlo_ready, at(s))
                        turn_tiles(pe, bank[0], lambda j: m_x[r][:, j, :]).then_inc(m_turned, 1)
                    if u == 4 and there(s - 2):
                        if is_step(s, B + 1):
                            pe.wait_ge(c_lo_ready, at(1))
                        pe.wait_ge(m_y_ready, at(s - 1))
                        pe.wait_ge(m_lo_ready, at(s + 1) if there(s) else at(B))
                        turn_tiles(pe, bank[0], lambda j: m_y[:, j * P:(j + 1) * P]).then_inc(m_y_turned, 1)
                    if u == 7 and there(s):
                        pe.wait_ge(m_lo_ready, at(s + 1))
                        pe.wait_ge(m_acc_ready, at(s - 1))
                        for j in range(TILES):
                            m = mm3(pe, bank[0][:, j * E:(j + 1) * E], m_hi[r][:, j * P:(j + 1) * P],
                                    m_lo[r][:, j * P:(j + 1) * P], r_hi[:, :], r_lo[:, :])
                        m.then_inc(m_logit_done, 1)
                    if u == 15 and there(s):
                        wait_apart(pe, m_chain, at(CHAIN * s + CHAIN))
                        for j in range(TILES):
                            m = pe.transpose(bank[0][0:LO_ROW + E, j * P:(j + 1) * P], m_cw[:, j, :], ident[:, :])
                        m.then_inc(m_cw_turned, 1)
            return step

        def moe_act(act):
            def phi(b, u, slot):
                act.wait_ge(m_prod_ready, at(UNITS * b + u + 1))
                act.wait_ge(m_down_done, at(UNITS * b + u + 1 - RING))
                act.activation(m_phi[slot][:, :], m_prod[slot][:, :], ACT.Copy).then_inc(m_phi_ready, 1)

            def step(s, r, part=range(UNITS)):
                b = s - 1
                slots = units(s, r)
                if is_step(s, 1):
                    act.wait_ge(h_out.ready, at(B))
                for u in part:
                    if there(b):
                        act.wait_ge(m_gate_done, at(UNITS * b + u + 1))
                        act.wait_ge(m_prod_ready, at(UNITS * b + u - 1))
                        act.activation(m_silu[u % 2][:, :], bank[2 + u % 2][:, :], ACT.Silu).then_inc(m_silu_ready, 1)
                        if u >= 1:
                            phi(b, u - 1, slots[u - 1])
                    if u == 2 and there(s):
                        act.wait_ge(m_turned, at(s + 1))
                        if is_step(s, 0):
                            act.wait_ge(h_wo_done, at(B))
                        act.wait_ge(m_up_done, at(UNITS * (s - 1)))
                        act.activation(m_hi[r][:, :], bank[0][:, :], ACT.Copy).then_inc(m_hi_ready, 1)
                    if u == 3 and there(s - 2):
                        act.wait_ge(m_down_done, at(UNITS * (s - 1)))
                        act.wait_ge(m_y_turned, at(s - 2))
                        act.activation(m_y[:, :], bank[6 + r][:, :], ACT.Copy).then_inc(m_y_ready, 1)
                    if u == 12 and there(s):
                        act.wait_ge(m_chain, at(CHAIN * s + 2))
                        act.activation(m_th[:, :], m_diff[:, :], ACT.Tanh, scale=0.5).then_inc(m_th_ready, 1)
                if there(b) and UNITS - 1 in part:
                    phi(b, UNITS - 1, slots[UNITS - 1])
            return step

        def moe_dve(dve):
            def wide(x):
                return x.unsqueeze(2).broadcast_to([P, TILES, E])

            def routing(s, r, u):
                def so_far(n):
                    wait_apart(dve, m_chain, at(CHAIN * s + n))
                if u == 8:
                    dve.wait_ge(m_logit_done, at(s + 1))
                    dve.tensor_tensor(m_logit[:, :, :], bank[0][:, 0:TILES * E].rearrange("p (j e) -> p j e", e=E),
                                      ebias[:, :].unsqueeze(1).broadcast_to([P, TILES, E]), ALU.add)\
                       .then_inc(m_logit_ready, 1)
                if u == 9:
                    wait_apart(dve, m_logit_ready, at(s + 1))
                    for j in range(TILES):
                        i = dve.max(m_top[:, j, :], m_logit[:, j, :])
                    i.then_inc(m_chain, 1)
                if u == 10:
                    so_far(1)
                    dve.tensor_tensor(m_diff[:, :], m_top[:, :, 0], m_top[:, :, 1], ALU.subtract).then_inc(m_chain, 1)
                    for j in range(TILES):
                        i = dve.max_index(m_top_i[:, j, :], m_top[:, j, :], m_logit[:, j, :])
                    i.then_inc(m_chain, 1)
                if u == 11:
                    so_far(3)
                    dve.tensor_copy(m_top_f[:, :, :], m_top_i[:, :, 0:2]).then_inc(m_chain, 1)
                if u == 12:
                    so_far(4)
                    for n in range(2):
                        i = dve.tensor_tensor(m_one[n][:, :, :], iota_e[:, :].unsqueeze(1).broadcast_to([P, TILES, E]),
                                              wide(m_top_f[:, :, n]), ALU.is_equal)
                    i.then_inc(m_chain, 1)
                if u == 13:
                    dve.wait_ge(m_th_ready, at(s + 1))
                    dve.tensor_scalar(m_w[:, 0, :], m_th[:, :], 0.5, 0.5, ALU.mult, ALU.add)
                    dve.tensor_scalar(m_w[:, 1, :], m_th[:, :], -0.5, 0.5, ALU.mult, ALU.add).then_inc(m_chain, 1)
                    so_far(6)
                    for n in range(2):
                        i = dve.tensor_tensor(m_part[n][:, :, :], m_one[n][:, :, :], wide(m_w[:, n, :]), ALU.mult)
                    i.then_inc(m_chain, 1)
                if u == 14:
                    so_far(7)
                    for start in (0, LO_ROW):
                        i = dve.tensor_tensor(m_cw[:, :, start:start + E], m_part[0][:, :, :], m_part[1][:, :, :], ALU.add)
                    i.then_inc(m_chain, 1)
                if u == 16:
                    dve.wait_ge(m_cw_turned, at(s + 1))
                    dve.wait_ge(m_cw_done, at(E * (s - 1)))
                    dve.tensor_copy(m_parts[r][:, :], bank[0][0:LO_ROW + E, :]).then_inc(m_cwhi_ready, 1)
                if u == 17:
                    dve.wait_ge(m_cwhi_ready, at(s + 1))
                    low = m_parts[r][LO_ROW:LO_ROW + E, :]
                    dve.tensor_tensor(low, bank[0][LO_ROW:LO_ROW + E, :], low.bitcast(F32), ALU.subtract)\
                       .then_inc(m_cwlo_ready, 1)

            def step(s, r, part=range(UNITS)):
                b = s - 1
                slots = units(s, r)
                if is_step(s, 1):
                    dve.wait_ge(h_out.ready, at(B))
                for u in part:
                    if there(b):
                        x = m_silu[u % 2][:, :]
                        dve.wait_ge(m_silu_ready, at(UNITS * b + u + 1))
                        if u >= HALVES:
                            dve.wait_ge(m_cw_done, at(E * b + (u - HALVES) // HALVES + 1))
                            dve.wait_ge(m_prod_ready, at(UNITS * b + u - 1))
                            dve.tensor_tensor(m_sc[u % 2][:, :], bank[1][:, :], x, ALU.mult).then_inc(m_sc_ready, 1)
                            dve.wait_ge(m_sc_ready, at(ROUTED * b + u - HALVES + 1))
                            x = m_sc[u % 2][:, :]
                        dve.wait_ge(m_up_done, at(UNITS * b + u + 1))
                        dve.wait_ge(m_plo_ready, at(UNITS * b + u + 1 - RING))
                        dve.wait_ge(m_phi_ready, at(UNITS * b + u + 1 - RING))
                        dve.tensor_tensor(m_prod[slots[u]][:, :], bank[4 + u % 2][:, :], x, ALU.mult).then_inc(m_prod_ready, 1)
                    if u == 2 and there(s):
                        dve.wait_ge(m_hi_ready, at(s + 1))
                        dve.tensor_tensor(m_lo[r][:, :], bank[0][:, :], m_hi[r][:, :].bitcast(F32), ALU.subtract)\
                           .then_inc(m_lo_ready, 1)
                    if u == 5 and there(s - 2):
                        dve.wait_ge(m_y_turned, at(s - 1))
                        dve.wait_ge(m_out.ready, at(s - 2))
                        dve.tensor_tensor(flat(m_acc), bank[0][:, :], R[:, s - 2, :, :].rearrange("p a b -> p (a b)"),
                                          ALU.add).then_inc(m_acc_ready, 1)
                    if u == 6 and there(s - 2):
                        dve.wait_ge(m_acc_ready, at(s - 1))
                        norm_moments(dve, m_out, s - 2, m_acc)
                    if u == 7 and there(s - 2):
                        if not is_step(s, B + 1):
                            norm_apply(dve, m_out, s - 2, R[:, s - 2, :, :], m_acc)
                    if there(s):
                        routing(s, r, u)
            return step

        def moe_pool(pool):
            def step(s, r, part=range(UNITS)):
                b = s - 1
                slots = units(s, r)
                if is_step(s, 1):
                    pool.wait_ge(h_out.ready, at(B))
                for u in part:
                    if there(b):
                        slot = slots[u]
                        pool.wait_ge(m_phi_ready, at(UNITS * b + u + 1))
                        pool.wait_ge(m_down_done, at(UNITS * b + u + 1 - RING))
                        pool.tensor_tensor(m_plo[slot][:, :], m_prod[slot][:, :], m_phi[slot][:, :].bitcast(F32),
                                           ALU.subtract).then_inc(m_plo_ready, 1)
                    if u == 6 and there(s - 2):
                        norm_rstd(pool, m_out, s - 2)
            return step

        c_x = [tok(0), tok(1)]
        c_hi, c_lo = [bufr(0), bufr(1)], [bufr(2), bufr(3)]
        c_qhi, c_qlo = [bufr(4), bufr(5)], [bufr(6), bufr(7)]
        c_xsum = buf(14)[:, 0:P]
        c_z = [buf(14)[:, (1 + i) * P:(2 + i) * P] for i in range(2)]
        c_xb = tok(13)
        c_bias, c_den, c_rden, c_att = [sb(f"c_{n}", [P, TILES]) for n in ("bias", "den", "rden", "att")]
        c_exp = [buf(16 + j) for j in range(TILES)]
        c_h = [tok(20), tok(15)]
        c_hhat, c_hg, c_acc = tok(21), tok(22), tok(23)
        c_xbeta = tok(6)

        c_loaded = [sem(f"c_loaded{i}") for i in range(2)]
        c_turned = sem("c_turned", "pe")
        c_hi_ready = sem("c_hi_ready", "act")
        c_lo_ready = sem("c_lo_ready", "dve")
        c_q_done = sem("c_q_done", "pe")
        c_qhi_ready = sem("c_qhi_ready", "act")
        c_qlo_ready = sem("c_qlo_ready", "dve")
        c_xsum_done = sem("c_xsum_done", "pe")
        c_xsum_ready = sem("c_xsum_ready", "act")
        c_z_done = sem("c_z_done", "pe")
        c_z_ready = sem("c_z_ready", "act")
        c_xb_ready = sem("c_xb_ready", "pool")
        c_xbeta_ready = sem("c_xbeta_ready", "pool")
        c_score_done = sem("c_score_done", "pe")
        c_bias_ready = sem("c_bias_ready", "dve")
        c_exp_ready = sem("c_exp_ready", "act")
        c_rden_ready = sem("c_rden_ready", "dve")
        c_att_ready = sem("c_att_ready", "dve")
        c_h_ready = sem("c_h_ready", "dve")
        c_hg_ready = sem("c_hg_ready", "pool")
        c_acc_ready = sem("c_acc_ready", "pool")
        c_inner = Norm("c_inner", on_act=True)
        c_out = Norm("c_out")

        def att_sync(sp):
            for r in range(2):
                sp.wait_ge(m_turned, at(B - 1 + r))
                sp.wait_ge(m_out.ready, at(r + 1))
                sp.dma_start(c_x[r][:, :, :], R[:, r, :, :]).then_inc(c_loaded[r], 16)
            with sp.Fori(1, B // 2) as i:
                b = 2 * i
                for r in range(2):
                    wait_apart(sp, m_out.ready, at(b + r + 1))
                    sp.wait_ge(c_xsum_done, at(b + r - 1))
                    sp.dma_start(c_x[r][:, :, :], R[:, b + r, :, :]).then_inc(c_loaded[r], 16)

        def att_pe(pe):
            def step(s, r):
                if is_step(s, 0):
                    pe.wait_ge(m_acc_ready, at(B - 1))
                    pe.wait_ge(m_prod_ready, at(UNITS * B))
                if is_step(s, 1):
                    pe.wait_ge(m_acc_ready, at(B))
                    pe.wait_ge(m_y_ready, at(B))
                if there(s):
                    pe.wait_ge(c_loaded[r], 8 * (s - r) + 16)
                    pe.wait_ge(c_lo_ready, at(s))
                    turn_tiles(pe, bank[0], lambda j: c_x[r][:, j, :]).then_inc(c_turned, 1)
                b, q = s - 1, 1 - r
                for j in range(TILES):
                    if there(b):
                        if j == 0:
                            pe.wait_ge(c_qlo_ready, at(b + 1))
                        pe.wait_ge(c_exp_ready, at(TILES * (b - 1) + j + 1))
                        tile = slice(j * P, (j + 1) * P)
                        mm3(pe, bank[4 + j][:, :], c_qhi[q][:, tile], c_qlo[q][:, tile], c_hi[q][:, :], c_lo[q][:, :])\
                            .then_inc(c_score_done, 1)
                if there(s):
                    pe.wait_ge(c_xsum_ready, at(s))
                    for j in range(TILES):
                        m = pe.matmul(bank[2][:, 0:1], c_x[r][:, j, :], ones[:, 0:1], start=j == 0, stop=j == TILES - 1)
                    m.then_inc(c_xsum_done, 1)
                    pe.wait_ge(c_lo_ready, at(s + 1))
                    pe.wait_ge(c_qlo_ready, at(s))
                    mm3(pe, bank[1][:, :], qk_hi[:, :], qk_lo[:, :], c_hi[r][:, :], c_lo[r][:, :]).then_inc(c_q_done, 1)
                    pe.wait_ge(c_xsum_ready, at(s + 1))
                    pe.wait_ge(c_z_ready, at(s))
                    pe.matmul(bank[3][:, 0:P], c_xsum[:, :], vfc[:, :], start=True, stop=True).then_inc(c_z_done, 1)
            return step

        def att_act(act):
            def step(s, r):
                if is_step(s, 0):
                    act.wait_ge(m_up_done, at(UNITS * B))
                    act.wait_ge(m_cw_done, at(E * B))
                if there(s):
                    act.wait_ge(c_turned, at(s + 1))
                    act.wait_ge(c_score_done, at(TILES * (s - 1)))
                    act.activation(c_hi[r][:, :], bank[0][:, :], ACT.Copy).then_inc(c_hi_ready, 1)
                b = s - 1
                for j in range(TILES):
                    if there(b):
                        act.wait_ge(c_bias_ready, at(TILES * b + j + 1))
                        act.wait_ge(c_att_ready, at(b))
                        act.activation(c_exp[j][:, :], bank[4 + j][:, :], ACT.Exp, bias=c_bias[:, j:j + 1], scale=-1.0,
                                       accum_out=c_den[:, j:j + 1]).then_inc(c_exp_ready, 1)
                    if j == 1 and there(s):
                        act.wait_ge(c_xsum_done, at(s + 1))
                        act.wait_ge(c_z_done, at(s))
                        act.activation(c_xsum[:, :], bank[2][:, 0:1].broadcast_to([P, P]), ACT.Copy).then_inc(c_xsum_ready, 1)
                        act.wait_ge(c_q_done, at(s + 1))
                        act.activation(c_qhi[r][:, :], bank[1][:, :], ACT.Copy).then_inc(c_qhi_ready, 1)
                if there(s):
                    act.wait_ge(c_z_done, at(s + 1))
                    act.wait_ge(c_h_ready, at(s - 1))
                    act.activation(c_z[r][:, :], bank[3][:, 0:P], ACT.Copy).then_inc(c_z_ready, 1)
                if there(s - 2):
                    wait_apart(act, c_hg_ready, at(s - 2))
                    norm_apply_on_act(act, c_inner, s - 2, c_hhat, c_h[r])
            return step

        def att_dve(dve):
            def step(s, r):
                b, q = s - 1, 1 - r

                def minima(pair):
                    for j in pair:
                        dve.wait_ge(c_score_done, at(TILES * b + j + 1))
                        dve.wait_ge(c_exp_ready, at(TILES * (b - 1) + j + 1))
                        dve.tensor_reduce(c_bias[:, j:j + 1], bank[4 + j][:, :], AX.X, ALU.min).then_inc(c_bias_ready, 1)
                if there(s):
                    dve.wait_ge(c_hi_ready, at(s + 1))
                    dve.tensor_tensor(c_lo[r][:, :], bank[0][:, :], c_hi[r][:, :].bitcast(F32), ALU.subtract)\
                       .then_inc(c_lo_ready, 1)
                if there(s - 2) and not is_step(s, B + 1):
                    norm_combine(dve, c_inner, s - 2)
                if there(s - 4) and not is_step(s, B + 1):
                    norm_apply(dve, c_out, s - 4, R[:, s - 4, :, :], c_acc)
                if there(b):
                    minima(range(TILES))
                if is_step(s, 1):
                    norm_apply(dve, m_out, B - 1, R[:, B - 1, :, :], m_acc)
                if there(s - 3):
                    dve.wait_ge(c_acc_ready, at(s - 2))
                    norm_stats(dve, c_out, s - 3, c_acc)
                if there(s):
                    dve.wait_ge(c_qhi_ready, at(s + 1))
                    dve.tensor_tensor(c_qlo[r][:, :], bank[1][:, :], c_qhi[r][:, :].bitcast(F32), ALU.subtract)\
                       .then_inc(c_qlo_ready, 1)
                if there(s - 3):
                    norm_combine(dve, c_out, s - 3)
                if there(b):
                    dve.wait_ge(c_exp_ready, at(TILES * b + TILES))
                    dve.reciprocal(c_rden[:, :], c_den[:, :]).then_inc(c_rden_ready, 1)
                    dve.wait_ge(c_rden_ready, at(b + 1))
                    dve.tensor_tensor(c_att[:, :], c_den[:, :], c_rden[:, :], ALU.mult).then_inc(c_att_ready, 1)
                    dve.wait_ge(c_att_ready, at(b + 1))
                    dve.wait_ge(c_z_ready, at(b + 1))
                    dve.wait_ge(c_xb_ready, at(b + 1))
                    dve.wait_ge(c_inner.ready, at(b - 1))
                    for j in range(TILES):
                        i = dve.scalar_tensor_tensor(out=c_h[q][:, j, :], in0=c_z[q][:, :], scalar=c_att[:, j:j + 1],
                                                     in1=c_xb[:, j, :], op0=ALU.mult, op1=ALU.add)
                    i.then_inc(c_h_ready, 1)
                    dve.wait_ge(c_h_ready, at(b + 1))
                    norm_stats(dve, c_inner, b, c_h[q])
                if is_step(s, B):
                    norm_combine(dve, c_inner, s - 1)
                    norm_apply(dve, c_out, s - 3, R[:, s - 3, :, :], c_acc)
            return step

        def att_pool(pool):
            def row(x):
                return x[:, :].unsqueeze(1).broadcast_to([P, TILES, P])

            def step(s, r):
                b = s - 1
                def outer_sum(n):
                    pool.wait_ge(c_xbeta_ready, at(n + 1))
                    pool.wait_ge(c_hg_ready, at(n + 1))
                    pool.wait_ge(c_out.ready, at(n))
                    pool.tensor_tensor(flat(c_acc), flat(c_hg), flat(c_xbeta), ALU.add).then_inc(c_acc_ready, 1)
                if there(s - 2) and not is_step(s, B + 1):
                    norm_rstd(pool, c_inner, s - 2)
                if there(s - 3) and not is_step(s, B + 1):
                    outer_sum(s - 3)
                if is_step(s, 1):
                    pool.wait_ge(m_out.ready, at(1))
                if is_step(s, 2):
                    pool.wait_ge(m_out.ready, at(B))
                if there(b):
                    wait_apart(pool, c_h_ready, at(b))
                    pool.tensor_tensor(c_xb[:, :, :], R[:, b, :, :], row(bfc), ALU.add).then_inc(c_xb_ready, 1)
                if there(s - 2):
                    wait_apart(pool, c_acc_ready, at(s - 2))
                    pool.tensor_tensor(c_xbeta[:, :, :], R[:, s - 2, :, :], row(beta), ALU.add).then_inc(c_xbeta_ready, 1)
                if there(s - 3):
                    norm_rstd(pool, c_out, s - 3)
                if there(s - 2):
                    pool.wait_ge(c_inner.ready, at(s - 1))
                    pool.tensor_tensor(c_hg[:, :, :], c_hhat[:, :, :], row(gamma), ALU.mult).then_inc(c_hg_ready, 1)
                if is_step(s, B):
                    norm_rstd(pool, c_inner, s - 1)
                    outer_sum(s - 2)
            return step

        f_x = [tok(0), tok(1)]
        f_hi, f_lo = flat(w_hi)[:, 0:T], flat(w_lo)[:, 0:T]
        f_up = [buf(2 + c) for c in range(MLP1)]
        BY_POOL = MLP1 - 1
        f_uphi = [[bufr(8 + c), bufr(c)] for c in range(MLP1)]
        f_uplo = [[bufr(12 + c), bufr(4 + c)] for c in range(MLP1)]
        f_y, f_acc = buf(7), [tok(8), tok(11)]
        f_res = [tok(9), tok(10)]

        f_loaded = [sem(f"f_loaded{i}") for i in range(2)]
        f_stored = [sem(f"f_stored{i}") for i in range(2)]
        f_turned = sem("f_turned", "pe")
        f_hi_ready = sem("f_hi_ready", "act")
        f_lo_ready = sem("f_lo_ready", "dve")
        f_up_done = sem("f_up_done", "pe")
        f_gelu_ready = sem("f_gelu_ready", "act")
        f_uphi_ready = sem("f_uphi_ready", "dve")
        f_uplo_ready = sem("f_uplo_ready", "pool")
        f_uplo_last = sem("f_uplo_last", "dve")
        f_down_done = sem("f_down_done", "pe")
        f_y_ready = sem("f_y_ready", "act")
        f_y_turned = sem("f_y_turned", "pe")
        f_acc_ready = sem("f_acc_ready", "dve")
        f_out = Norm("f_out")

        def mlp_sync(sp):
            def load(b, r):
                wait_apart(sp, c_out.ready, at(b + 1))
                sp.dma_start(f_x[r][:, :, :], R[:, b, :, :]).then_inc(f_loaded[r], 16)

            def store(b, r):
                wait_apart(sp, f_out.ready, at(b + 1))
                sp.dma_start(out[b].rearrange("(j p) d -> p j d", p=P), f_res[r][:, :, :]).then_inc(f_stored[r], 16)
            for r in range(2):
                sp.sem_inc(f_stored[r], 16)
                sp.wait_ge(c_xsum_done, at(B - 1 + r))
                load(r, r)

            def turn(b):
                for r in range(2):
                    wait_apart(sp, f_turned, at(b + r - 1))
                    load(b + r, r)
                    if there(b + r - 4):
                        store(b + r - 4, r)
            turn(2)
            with sp.Fori(2, B // 2) as i:
                turn(2 * i)
            for b in range(B - 4, B):
                store(b, b % 2)
            for r in range(2):
                sp.wait_ge(f_stored[r], 16 + 16 * (B // 2))

        def uplo_wait(eng, b, c):
            if c < BY_POOL:
                eng.wait_ge(f_uplo_ready, at(BY_POOL * b + c + 1))
            else:
                eng.wait_ge(f_uplo_last, at((MLP1 - BY_POOL) * b + c - BY_POOL + 1))

        def mlp_pe(pe):
            def step(s, r):
                if is_step(s, 0):
                    pe.wait_ge(c_lo_ready, at(B))
                b = s - 1
                if is_step(s, 1):
                    pe.wait_ge(c_qlo_ready, at(B))
                    pe.wait_ge(c_exp_ready, at(TILES * B))
                    pe.wait_ge(c_z_ready, at(B))
                if there(b):
                    pe.wait_ge(f_lo_ready, at(b + 1))
                    for c in range(MLP1):
                        pe.wait_ge(f_gelu_ready, at(MLP1 * (b - 1) + c + 1))
                        project(pe, bank[4 + c][:, :], UP1 + c * P, f_hi[:, :], f_lo[:, :])\
                            .then_inc(f_up_done, 1)
                if there(s):
                    pe.wait_ge(f_loaded[r], 8 * (s - r) + 16)
                    pe.wait_ge(f_lo_ready, at(s))
                    turn_tiles(pe, bank[0], lambda j: f_x[r][:, j, :]).then_inc(f_turned, 1)
                b = s - 3
                if there(b):
                    pe.wait_ge(f_y_ready, at(b + 1))
                    pe.wait_ge(f_acc_ready, at(b))
                    turn_tiles(pe, bank[2], lambda j: f_y[:, j * P:(j + 1) * P]).then_inc(f_y_turned, 1)
                b = s - 2
                if there(b):
                    for c in range(MLP1):
                        uplo_wait(pe, b, c)
                        if c == 0:
                            pe.wait_ge(f_y_ready, at(b))
                        m = project(pe, bank[1][:, :], DN1 + c * P, f_uphi[c][r], f_uplo[c][r],
                                    start=c == 0, stop=c == MLP1 - 1)
                    m.then_inc(f_down_done, 1)
            return step

        def mlp_act(act):
            def step(s, r):
                b = s - 1
                if there(b):
                    for c in range(MLP1):
                        act.wait_ge(f_up_done, at(MLP1 * b + c + 1))
                        uplo_wait(act, b - 1, c)
                        act.activation(f_up[c][:, :], bank[4 + c][:, :], ACT.Gelu, bias=f_b1[:, c:c + 1])\
                           .then_inc(f_gelu_ready, 1)
                if there(s):
                    act.wait_ge(f_turned, at(s + 1))
                    act.wait_ge(f_up_done, at(MLP1 * s))
                    act.activation(f_hi[:, :], bank[0][:, :], ACT.Copy).then_inc(f_hi_ready, 1)
                if is_step(s, 0):
                    act.preload_act_table_set("gelu_and_others")
                b = s - 2
                if there(b):
                    act.wait_ge(f_down_done, at(b + 1))
                    act.wait_ge(f_y_turned, at(b))
                    act.activation(f_y[:, :], bank[1][:, :], ACT.Identity, bias=f_b2[:, :]).then_inc(f_y_ready, 1)
            return step

        def mlp_dve(dve):
            def step(s, r):
                b = s - 1

                def apply():
                    dve.wait_ge(f_stored[r], 8 * (s - 4 - r) + 16)
                    norm_apply(dve, f_out, s - 4, f_res[r], f_acc[r])
                for c in range(MLP1):
                    if there(b):
                        dve.wait_ge(f_gelu_ready, at(MLP1 * b + c + 1))
                        dve.wait_ge(f_down_done, at(b - 1))
                        dve.tensor_copy(f_uphi[c][1 - r][:, :], f_up[c][:, :]).then_inc(f_uphi_ready, 1)
                        if c >= BY_POOL:
                            dve.wait_ge(f_uphi_ready, at(MLP1 * b + c + 1))
                            dve.tensor_tensor(f_uplo[c][1 - r][:, :], f_up[c][:, :], f_uphi[c][1 - r][:, :].bitcast(F32),
                                              ALU.subtract).then_inc(f_uplo_last, 1)
                    if c == 1 and there(b) and there(s - 4):
                        apply()
                if there(s):
                    dve.wait_ge(f_hi_ready, at(s + 1))
                    dve.wait_ge(f_up_done, at(MLP1 * s))
                    dve.tensor_tensor(f_lo[:, :], bank[0][:, :], f_hi[:, :].bitcast(F32), ALU.subtract).then_inc(f_lo_ready, 1)
                b = s - 3
                if there(b):
                    dve.wait_ge(f_y_turned, at(b + 1))
                    dve.wait_ge(f_out.ready, at(b - 1))
                    dve.tensor_tensor(flat(f_acc[1 - r]), bank[2][:, :], R[:, b, :, :].rearrange("p a b -> p (a b)"), ALU.add)\
                       .then_inc(f_acc_ready, 1)
                    dve.wait_ge(f_acc_ready, at(b + 1))
                    norm_stats(dve, f_out, b, f_acc[1 - r])
                if not there(s - 1) and there(s - 4):
                    apply()
                    wait_apart(dve, f_out.ready, at(s - 3))
                if there(b):
                    norm_combine(dve, f_out, b)
            return step

        def mlp_pool(pool):
            def step(s, r):
                b = s - 1
                if there(b):
                    for c in range(BY_POOL):
                        pool.wait_ge(f_uphi_ready, at(MLP1 * b + c + 1))
                        pool.wait_ge(f_down_done, at(b - 1))
                        pool.tensor_tensor(f_uplo[c][1 - r][:, :], f_up[c][:, :], f_uphi[c][1 - r][:, :].bitcast(F32),
                                           ALU.subtract).then_inc(f_uplo_ready, 1)
                if there(s - 3):
                    norm_rstd(pool, f_out, s - 3)
            return step

        block = ctx.enter_context(nc.Block())

        @block.sync
        def _(sp):
            gla_load(sp, 0, 0)
            with nc.allow_non_contiguous_dma(reason="a few hundred bias values, one to a partition"):
                for dst, src in EARLY:
                    sp.dma_start(dst, src).then_inc(early, 16)
            gla_load(sp, 1, 1)
            for dst, src in LATE:
                sp.dma_start(dst, src).then_inc(late_raw_in, 16)
            with nc.allow_non_contiguous_dma(reason="a few hundred bias values, one to a partition"):
                for dst, src in SMALL:
                    sp.dma_start(dst, src).then_inc(small_in, 16)
            gla_sync(sp)
            mid_sync(sp)
            moe_sync(sp)
            att_sync(sp)
            mlp_sync(sp)

        @block.gpsimd
        def _(pool):
            open_semaphores(pool, "pool")
            pool.memset(ident[:, :], 0.0).then_inc(pool_chain, 1)
            pool.memset(ones[:, :], 1.0).then_inc(pool_chain, 1)
            pool.memset(head_mean[:, :], 1.0 / DV).then_inc(pool_chain, 1)
            pool.memset(eps_row[:, :], EPS).then_inc(pool_chain, 1)
            pool.memset(m_cw[:, :, :], 0.0)
            pool.memset(zero_row[:, :], 0.0)
            pool.memset(minus_half[:, :], -0.5).then_inc(pool_chain, 1)
            pool.iota(iota_i[:, :], pattern=[[1, E]], base=0, channel_multiplier=0).then_inc(pool_chain, 1)
            pool.wait_ge(pool_chain, at(6))
            pool.affine_select(out=ident[:, :], in_=ident[:, :], compare_op=ALU.not_equal, fill=1.0, base=0,
                               pattern=[[-1, P]], channel_multiplier=1).then_inc(pool_chain, 1)
            hm = head_mean[:, :].rearrange("p (h v) -> p h v", v=DV)
            pool.affine_select(out=hm, in_=hm, compare_op=ALU.is_ge, fill=0.0, base=0,
                               pattern=[[-DV, H], [0, DV]], channel_multiplier=1).then_inc(pool_chain, 1)
            pool.wait_ge(pool_chain, at(8))
            pool.affine_select(out=hm, in_=hm, compare_op=ALU.is_ge, fill=0.0, base=DV - 1,
                               pattern=[[DV, H], [0, DV]], channel_multiplier=-1).then_inc(pool_chain, 1)
            pool.tensor_copy(iota_e[:, :], iota_i[:, :]).then_inc(const_made, 1)

            def loaded(pool):
                pool.wait_ge(small_in, 16 * len(SMALL))
            all_phases(pool, gla_pool(pool), mid_pool(pool), moe_pool(pool), att_pool(pool), mlp_pool(pool),
                       loaded, nothing, nothing, nothing)

        @block.vector
        def _(dve):
            open_semaphores(dve, "dve")

            def by_key(w, k):
                return w.rearrange("d (h k) -> d k h", k=DK)[:, k, :].unsqueeze(2)

            def weights(dve):
                dve.wait_ge(early, 16 * len(EARLY))
                for k in range(DK):
                    dve.tensor_scalar(w_raw[:, Q0 + k, :].rearrange("d (h v) -> d h v", v=DV),
                                      by_key(wq_raw[:, :], k).broadcast_to([P, H, DV]), float(DK) ** -0.5, None, ALU.mult)
                    dve.tensor_copy(w_raw[:, K0 + k, :].rearrange("d (h v) -> d h v", v=DV),
                                    by_key(wk_raw[:, :], k).broadcast_to([P, H, DV]))
                dve.tensor_scalar(wo_scaled[:, :], wo_raw[:, :], rms_col[:, :], 0.5, ALU.mult, ALU.mult).then_inc(prep_dve, 1)
                dve.wait_ge(pool_chain, at(9))
                for k in range(DK):
                    dve.tensor_tensor(spread_k[:, k, :].rearrange("p (h v) -> p h v", v=DV),
                                      by_key(ident[:, 0:HK], k).broadcast_to([P, H, DV]),
                                      by_key(ident[:, HK:2 * HK], k).broadcast_to([P, H, DV]), ALU.add)
                dve.tensor_tensor(pick_raw[:, :], ident[0:LO_ROW + E, 0:E], ident[0:LO_ROW + E, LO_ROW:LO_ROW + E], ALU.add)\
                   .then_inc(prep_dve, 1)
                dve.wait_ge(prep_pe, at(1))
                dve.tensor_copy(gkw1_t[:, :], bank[0][0:LOWR, 0:P]).then_inc(prep_dve, 1)
                dve.wait_ge(prep_pe, at(2))
                for i in range(P // HK):
                    g = dve.tensor_copy(w_raw[:, GK, i * HK:(i + 1) * HK], bank[1][:, 0:HK])
                g.then_inc(prep_dve, 1)
                dve.wait_ge(prep_dve, at(4))
                dve.tensor_copy(pick_e[:, :, :], pick_raw[:, :].unsqueeze(2).broadcast_to([LO_ROW + E, E, P]))
                dve.tensor_scalar(flat(w_fold), flat(w_raw), ln_w[:, :], None, ALU.mult).then_inc(prep_dve, 1)
                dve.wait_ge(prep_dve, at(5))
                dve.tensor_copy(wo_hi[:, :], wo_scaled[:, :])
                dve.tensor_copy(flat(w_hi), flat(w_fold)).then_inc(prep_dve, 1)
                dve.wait_ge(prep_dve, at(6))
                dve.tensor_tensor(wo_lo[:, :], wo_scaled[:, :], wo_hi[:, :].bitcast(F32), ALU.subtract)
                dve.tensor_tensor(flat(w_lo), flat(w_fold), flat(w_hi).bitcast(F32), ALU.subtract).then_inc(prep_dve, 1)
                dve.wait_ge(prep_pe, at(3))
                dve.tensor_copy(w_bias[:, V:UP0], bank[2][:, V:UP0])
                dve.tensor_tensor(w_bias[:, GK:GK + 1], bank[2][:, GK:GK + 1], gk_b[:, :], ALU.add)
                dve.tensor_tensor(w_bias[:, UP0:NB0], bank[2][:, UP0:NB0], b1_col[:, :], ALU.add).then_inc(prep_dve, 1)

            def late_weights(dve):
                dve.wait_ge(small_in, 16 * len(SMALL))
                dve.wait_ge(prep_pe, at(4))
                dve.tensor_copy(r_hi[:, :], bank[3][:, 0:E]).then_inc(prep_dve, 1)
                dve.wait_ge(prep_dve, at(9))
                dve.tensor_tensor(r_lo[:, :], bank[3][:, 0:E], r_hi[:, :].bitcast(F32), ALU.subtract)
                dve.tensor_scalar(qk_hi[:, :], bank[4][:, 0:P], -SCALE, None, ALU.mult).then_inc(prep_dve, 1)
                dve.wait_ge(prep_dve, at(10))
                dve.scalar_tensor_tensor(out=qk_lo[:, :], in0=bank[4][:, 0:P], scalar=-SCALE, in1=qk_hi[:, :].bitcast(F32),
                                         op0=ALU.mult, op1=ALU.subtract)
                dve.tensor_copy(fc_t[:, :], bank[5][:, 0:P]).then_inc(prep_dve, 1)
                dve.wait_ge(prep_pe, at(5))
                dve.tensor_copy(vfc[:, :], bank[6][:, 0:P]).then_inc(prep_dve, 1)
            all_phases(dve, gla_dve(dve), mid_dve(dve), moe_dve(dve), att_dve(dve), mlp_dve(dve),
                       late_weights, nothing, nothing, weights)

        @block.scalar
        def _(act):
            open_semaphores(act, "act")
            act.preload_act_table_set("natural_log_exp_and_others")
            act.wait_ge(prep_dve, at(8))
            act.wait_ge(pool_chain, at(9))

            def gelu_tables(act):
                act.preload_act_table_set("gelu_and_others")

            def silu_tables(act):
                act.preload_act_table_set("silu_and_others")

            def exp_tables(act):
                act.preload_act_table_set("exp_and_others")
            act.wait_ge(small_in, 16 * len(SMALL))
            all_phases(act, gla_act(act), mid_act(act), moe_act(act), att_act(act), mlp_act(act),
                       gelu_tables, silu_tables, exp_tables)

        @block.tensor
        def _(pe):
            open_semaphores(pe, "pe")
            pe.wait_ge(early, 16 * len(EARLY))
            pe.wait_ge(pool_chain, at(9))
            pe.transpose(bank[0][0:LOWR, 0:P], gkw1[:, :], ident[:, :]).then_inc(prep_pe, 1)
            pe.wait_ge(prep_dve, at(3))
            pe.matmul(bank[1][:, 0:HK], gkw1_t[:, :], gkw2[:, :], start=True, stop=True).then_inc(prep_pe, 1)
            pe.wait_ge(prep_dve, at(4))
            for n in range(NB0):
                m = pe.matmul(bank[2][:, n:n + 1], w_raw[:, n, :], ln_b[:, :], start=True, stop=True)
            m.then_inc(prep_pe, 1)
            pe.wait_ge(prep_dve, at(8))

            def late_weights(pe):
                pe.wait_ge(g_qS_ready, at(DK * B))
                pe.wait_ge(small_in, 16 * len(SMALL))
                pe.transpose(bank[3][:, 0:E], r_raw[:, :], ident[0:E, 0:E])
                pe.matmul(bank[4][:, 0:P], qkv_raw[:, 0, :], qkv_raw[:, 1, :], start=True, stop=True)
                pe.transpose(bank[5][:, 0:P], fc_raw[:, :], ident[:, :]).then_inc(prep_pe, 1)
                pe.wait_ge(prep_dve, at(11))
                pe.matmul(bank[6][:, 0:P], qkv_raw[:, 2, :], fc_t[:, :], start=True, stop=True).then_inc(prep_pe, 1)
                pe.wait_ge(prep_dve, at(12))
                pe.wait_ge(late_lo, at(2 * B))
            all_phases(pe, gla_pe(pe), mid_pe(pe), moe_pe(pe), att_pe(pe), mlp_pe(pe),
                       late_weights, nothing, nothing)


_INS = ['L0_attn_x', 'L0_attn_ln_w', 'L0_attn_ln_b', 'L0_attn_Wq', 'L0_attn_Wk', 'L0_attn_Wv', 'L0_attn_gk_w1',
        'L0_attn_gk_w2', 'L0_attn_gk_b2', 'L0_attn_Wg', 'L0_attn_rms_w', 'L0_attn_Wo', 'L0_attn_W1', 'L0_attn_b1',
        'L0_attn_W2', 'L0_attn_b2', 'L0_ffn_router_w', 'L0_ffn_experts_bias', 'L0_ffn_w1', 'L0_ffn_w3', 'L0_ffn_w2',
        'L0_ffn_sw1', 'L0_ffn_sw3', 'L0_ffn_sw2', 'L1_attn_w_qkv', 'L1_attn_w_fc', 'L1_attn_b_fc', 'L1_attn_gamma',
        'L1_attn_beta', 'L1_ffn_w1', 'L1_ffn_b1', 'L1_ffn_w2', 'L1_ffn_b2']


def kernel(**inputs):
    import numpy as _np
    import concourse.bacc as _bacc
    from concourse import mybir as _mybir
    from concourse.bass_utils import run_bass_kernel_spmd as _run

    nc = _bacc.Bacc("TRN2", target_bir_lowering=False, num_devices=1)
    arrays, args = {}, {}
    for name in _INS:
        x = _np.ascontiguousarray(inputs[name])
        arrays[f"in_{name}_dram"] = x
        args[name] = nc.dram_tensor(f"in_{name}_dram", x.shape, _mybir.dt.from_np(x.dtype), kind="ExternalInput").ap()
    out = nc.dram_tensor("out_0_dram", inputs["L0_attn_x"].shape, _mybir.dt.float32, kind="ExternalOutput").ap()
    build(nc, args, out)
    r = _run(nc, [arrays], core_ids=[0])
    return r.results[0]["out_0_dram"]
```
